# Optimizing a Trainium2 kernel written in Bass

```python
import numpy as np
import jax
import jax.numpy as jnp

def _softmax(x, axis=-1):
    return jax.nn.softmax(x, axis=axis)

def _gelu(x):
    return jax.nn.gelu(x, approximate=True)

def _silu(x):
    return jax.nn.silu(x)

def _sigmoid(x):
    return jax.nn.sigmoid(x)

def _layernorm(x, axis=-1, eps=1e-05):
    m = jnp.mean(x, axis=axis, keepdims=True)
    v = jnp.var(x, axis=axis, keepdims=True)
    return (x - m) / jnp.sqrt(v + eps)

def _scatter_add(tgt, idx, src, axis=0):
    return tgt.at[idx].add(src)

def _segment_sum(src, seg, n):
    return jax.ops.segment_sum(src, seg, n)
kernel_name = 'mk_xattn_ffn_d1_seqx_r4_9196b7'

def setup_inputs(seed: int=0):
    np.random.seed(seed)
    _w = jnp.asarray

    def _rec_inputs():
        import jax
        import jax.numpy as jnp
        _rk = jax.random.key(seed)
        x = 2.818e-05 + 1 * jax.random.normal(jax.random.fold_in(_rk, 1), (4, 512, 512), jnp.float32)
        _lenS = 512 - jax.random.randint(jax.random.fold_in(_rk, 7), (4,), 0, max(1, 512 // 4) + 1, jnp.int32)
        _lenS2 = 512 - jax.random.randint(jax.random.fold_in(_rk, 8), (4,), 0, max(1, 512 // 4) + 1, jnp.int32)
        _ctx_1024P = jax.random.normal(jax.random.fold_in(_rk, 11), (4, 16, 256), jnp.float32)
        _ctx_1024c = jax.random.dirichlet(jax.random.fold_in(_rk, 511), 0.3 * jnp.ones((16,), jnp.float32), (4, 512))
        _ctx_1024t = jnp.einsum('bsk,bkd->bsd', _ctx_1024c, _ctx_1024P)
        _ctx_1024t = _ctx_1024t * jax.lax.rsqrt(jnp.mean(jnp.square(_ctx_1024t)) + 1e-12) * 0.953939
        ctx_1024 = 7.22013e-05 + 1.00017 * (_ctx_1024t + 0.3 * jax.random.normal(jax.random.fold_in(_rk, 611), (4, 512, 256), jnp.float32))
        return (x, ctx_1024)
    x, ctx_1024 = _rec_inputs()

    def _L0_xattn_setup():
        import jax, jax.numpy as jnp
        import numpy as np
        B_, L_, D_MODEL = (4, 512, 256)
        D_STATE, D_CONV, EXPAND = (16, 4, 2)
        D_INNER = EXPAND * D_MODEL
        DT_RANK = (D_MODEL + 15) // 16

        def silu(x):
            return x * jax.nn.sigmoid(x)
        key = jax.random.key(seed)
        ks = jax.random.split(key, 10)
        f32 = jnp.float32
        hidden_states = jax.random.normal(ks[0], (B_, L_, D_MODEL), dtype=f32)
        z = jax.random.normal(ks[1], (B_, D_INNER, L_), dtype=f32)
        in_proj_w = jax.random.normal(ks[2], (D_INNER, D_MODEL), dtype=f32) * 0.02
        conv_w = jax.random.normal(ks[3], (D_INNER, 1, D_CONV), dtype=f32) * 0.1
        conv_b = jax.random.normal(ks[4], (D_INNER,), dtype=f32) * 0.02
        x_proj_w = jax.random.normal(ks[5], (DT_RANK + 2 * D_STATE, D_INNER), dtype=f32) * 0.02
        dt_proj_w = jax.random.uniform(ks[6], (D_INNER, DT_RANK), dtype=f32, minval=-DT_RANK ** (-0.5), maxval=DT_RANK ** (-0.5))
        dt = jnp.exp(jax.random.uniform(ks[7], (D_INNER,), dtype=f32, minval=np.log(0.001), maxval=np.log(0.1)))
        dt_proj_b = jnp.log(jnp.expm1(dt))
        A_log = jnp.log(jnp.broadcast_to(jnp.arange(1, D_STATE + 1, dtype=f32), (D_INNER, D_STATE)))
        D = jnp.ones((D_INNER,), f32)
        return {'hidden_states': hidden_states, 'z': z, 'in_proj_w': in_proj_w, 'conv_w': conv_w, 'conv_b': conv_b, 'x_proj_w': x_proj_w, 'dt_proj_w': dt_proj_w, 'dt_proj_b': dt_proj_b, 'A_log': A_log, 'D': D}
    _L0_xattn_all = _L0_xattn_setup()
    _L0_xattn_in = {k: v for k, v in _L0_xattn_all.items() if k in ('in_proj_w', 'conv_w', 'conv_b', 'x_proj_w', 'dt_proj_w', 'dt_proj_b', 'A_log', 'D')}
    del _L0_xattn_all

    def _L0_ffn_setup():
        import jax, jax.numpy as jnp
        import numpy as np
        H = 512
        I = 352
        E = 16
        K = 2
        SI = I * 2

        def _swiglu(gu, inter):
            g, u = (gu[..., :inter], gu[..., inter:])
            return jax.nn.silu(g) * u
        key = jax.random.key(seed)
        ks = jax.random.split(key, 6)
        s = 0.02
        hidden_states = jax.random.normal(ks[0], (1, 256, H), dtype=jnp.float32)
        gate_w = jax.random.normal(ks[1], (E, H), dtype=jnp.float32) * s
        w_gate_up = jax.random.normal(ks[2], (E, H, 2 * I), dtype=jnp.float32) * s
        w_down = jax.random.normal(ks[3], (E, I, H), dtype=jnp.float32) * s
        shared_gate_up = jax.random.normal(ks[4], (H, 2 * SI), dtype=jnp.float32) * s
        shared_down = jax.random.normal(ks[5], (SI, H), dtype=jnp.float32) * s
        return {'hidden_states': hidden_states, 'gate_w': gate_w, 'w_gate_up': w_gate_up, 'w_down': w_down, 'shared_gate_up': shared_gate_up, 'shared_down': shared_down}
    _L0_ffn_all = _L0_ffn_setup()
    _L0_ffn_in = {k: v for k, v in _L0_ffn_all.items() if k in ('gate_w', 'w_gate_up', 'w_down', 'shared_gate_up', 'shared_down')}
    del _L0_ffn_all
    return {'x': x, 'ctx_1024': ctx_1024, 'L0_xattn_in_proj_w': _L0_xattn_in['in_proj_w'], 'L0_xattn_conv_w': _L0_xattn_in['conv_w'], 'L0_xattn_conv_b': _L0_xattn_in['conv_b'], 'L0_xattn_x_proj_w': _L0_xattn_in['x_proj_w'], 'L0_xattn_dt_proj_w': _L0_xattn_in['dt_proj_w'], 'L0_xattn_dt_proj_b': _L0_xattn_in['dt_proj_b'], 'L0_xattn_A_log': _L0_xattn_in['A_log'], 'L0_xattn_D': _L0_xattn_in['D'], 'L0_ffn_gate_w': _L0_ffn_in['gate_w'], 'L0_ffn_w_gate_up': _L0_ffn_in['w_gate_up'], 'L0_ffn_w_down': _L0_ffn_in['w_down'], 'L0_ffn_shared_gate_up': _L0_ffn_in['shared_gate_up'], 'L0_ffn_shared_down': _L0_ffn_in['shared_down']}

def reference(x, ctx_1024, L0_xattn_in_proj_w, L0_xattn_conv_w, L0_xattn_conv_b, L0_xattn_x_proj_w, L0_xattn_dt_proj_w, L0_xattn_dt_proj_b, L0_xattn_A_log, L0_xattn_D, L0_ffn_gate_w, L0_ffn_w_gate_up, L0_ffn_w_down, L0_ffn_shared_gate_up, L0_ffn_shared_down):
    import jax
    import jax.numpy as jnp

    def _L0_xattn_ref(hidden_states, z, in_proj_w, conv_w, conv_b, x_proj_w, dt_proj_w, dt_proj_b, A_log, D):
        import jax, jax.numpy as jnp
        import numpy as np
        B_, L_, D_MODEL = (4, 512, 256)
        D_STATE, D_CONV, EXPAND = (16, 4, 2)
        D_INNER = EXPAND * D_MODEL
        DT_RANK = (D_MODEL + 15) // 16

        def silu(x):
            return x * jax.nn.sigmoid(x)
        Bsz, L, _ = hidden_states.shape
        d_inner, _, d_conv = conv_w.shape
        dt_rank = dt_proj_w.shape[1]
        d_state = A_log.shape[1]
        x = jnp.einsum('bld,ed->bel', hidden_states, in_proj_w)
        xc = jax.lax.conv_general_dilated(x, conv_w, window_strides=(1,), padding=[(d_conv - 1, 0)], feature_group_count=d_inner, dimension_numbers=('NCH', 'OIH', 'NCH'))
        x = silu(xc + conv_b[None, :, None])
        x_dbl = jnp.einsum('bdl,ed->bel', x, x_proj_w)
        dt_low, Bm, Cm = jnp.split(x_dbl, [dt_rank, dt_rank + d_state], axis=1)
        dt = jnp.einsum('brl,dr->bdl', dt_low, dt_proj_w)
        dt = jax.nn.softplus(dt + dt_proj_b[None, :, None])
        A = -jnp.exp(A_log)
        dt_t = jnp.moveaxis(dt, -1, 0)
        B_t = jnp.moveaxis(Bm, -1, 0)
        C_t = jnp.moveaxis(Cm, -1, 0)
        u_t = jnp.moveaxis(x, -1, 0)

        def step(state, inp):
            d, b, c, u = inp
            dA = jnp.exp(d[..., None] * A)
            state = state * dA + (d * u)[..., None] * b[:, None, :]
            y = jnp.einsum('bdn,bn->bd', state, c)
            return (state, y)
        state0 = jnp.zeros((Bsz, d_inner, d_state), x.dtype)
        _, ys = jax.lax.scan(step, state0, (dt_t, B_t, C_t, u_t))
        y = jnp.moveaxis(ys, 0, 2)
        y = y + D[None, :, None] * x
        y = y * silu(z)
        return jnp.swapaxes(y, 1, 2)

    def _L0_ffn_ref(hidden_states, gate_w, w_gate_up, w_down, shared_gate_up, shared_down):
        import jax, jax.numpy as jnp
        import numpy as np
        H = 512
        I = 352
        E = 16
        K = 2
        SI = I * 2

        def _swiglu(gu, inter):
            g, u = (gu[..., :inter], gu[..., inter:])
            return jax.nn.silu(g) * u
        orig_shape = hidden_states.shape
        x = hidden_states.reshape(-1, H)
        logits = jnp.einsum('th,eh->te', x, gate_w)
        scores = jax.nn.softmax(logits, axis=-1)
        topk_w, topk_idx = jax.lax.top_k(scores, K)
        combine = jnp.sum(jax.nn.one_hot(topk_idx, E, dtype=x.dtype) * topk_w[..., None], axis=1)
        gu = jnp.einsum('th,ehj->etj', x, w_gate_up)
        h = _swiglu(gu, I)
        y = jnp.einsum('eti,eih,te->th', h, w_down, combine)
        gu_s = x @ shared_gate_up
        y = y + _swiglu(gu_s, SI) @ shared_down
        return y.reshape(orig_shape)
    x = x + _L0_xattn_ref(ctx_1024, _layernorm(x, axis=-1), L0_xattn_in_proj_w, L0_xattn_conv_w, L0_xattn_conv_b, L0_xattn_x_proj_w, L0_xattn_dt_proj_w, L0_xattn_dt_proj_b, L0_xattn_A_log, L0_xattn_D)
    x = x + _L0_ffn_ref(_layernorm(x, axis=-1), L0_ffn_gate_w, L0_ffn_w_gate_up, L0_ffn_w_down, L0_ffn_shared_gate_up, L0_ffn_shared_down)
    return x

_drawn_inputs = setup_inputs


def setup_inputs(seed=0):
    import zlib

    import numpy as np

    out = dict(_drawn_inputs(seed))
    spreads = {'L0_xattn_D': (1.0, 0.6)}
    factors = {'ctx_1024': 2.891,
     'L0_xattn_in_proj_w': 2.896,
     'L0_xattn_conv_w': 2.955,
     'L0_xattn_conv_b': 8.0,
     'L0_xattn_x_proj_w': 8.0,
     'L0_xattn_dt_proj_w': 8.0,
     'L0_xattn_dt_proj_b': 8.0,
     'L0_xattn_A_log': 8.0,
     'L0_ffn_gate_w': 8.0,
     'L0_ffn_w_gate_up': 7.334,
     'L0_ffn_w_down': 7.309,
     'L0_ffn_shared_gate_up': 8.0,
     'L0_ffn_shared_down': 8.0}
    for name, (base, spread) in spreads.items():
        noise = np.random.default_rng([zlib.crc32(name.encode()), seed]).standard_normal(out[name].shape)
        drawn = base * np.exp(spread * noise) if base else spread * noise
        out[name] = jnp.asarray(drawn.astype(out[name].dtype))
    for name, factor in factors.items():
        out[name] = (out[name] * factor).astype(out[name].dtype)
    return out
```

```python
import concourse.bass as bass
from concourse import mybir
from contextlib import ExitStack

F32 = mybir.dt.float32
I32 = mybir.dt.int32
U32 = mybir.dt.uint32
ALU = mybir.AluOpType
ACT = mybir.ActivationFunctionType
AX = mybir.AxisListType

P = 128
B, L = 4, 512
DM, H = 256, 512
DT, NE = H // P, 16
NS, RK = 16, 16
NX = RK + 2 * NS
I = 352
IT = [(0, 128), (128, 128), (256, 96)]
KH = H // P
T = B * L
NT = T // P
TB = L // P
K = 2
UNITS = T * K // P + NE - 1
EPS = 1e-5
THETA = 2.0 ** -6
GRP = 4
NG = NS // GRP
STEPS = DT * NS
RING_H, RING_G = 3, 8


def program(nc, x, ctxT, inT, convw, convb, xpT, dtT, dtb, alog, dskip, gateT, wgu, wdn, sgu, sdn, out):
    bc_d = nc.dram_tensor("bc_scratch", [B, 2 * NS, L], F32, kind="Internal").ap()
    u_d = nc.dram_tensor("u_scratch", [B, P, DT, L], F32, kind="Internal").ap()
    dt_d = nc.dram_tensor("dt_scratch", [B, P, DT, L], F32, kind="Internal").ap()
    sz_d = nc.dram_tensor("silu_z_scratch", [T, H], F32, kind="Internal").ap()
    x1_d = nc.dram_tensor("x1_scratch", [T, H], F32, kind="Internal").ap()
    xn_d = nc.dram_tensor("xn_scratch", [T + P, H], F32, kind="Internal").ap()

    def batch_rows(t, b):
        return t[bass.ds(b * L, L), :].rearrange("(t p) h -> p t h", p=P)

    with ExitStack() as stack:
        def sb(name, shape, dt=F32):
            return stack.enter_context(nc.sbuf_tensor(name, shape, dt))

        def sem(name):
            return stack.enter_context(nc.semaphore(name))

        bank = [stack.enter_context(nc.psum_tensor(f"bank{i}", [P, 512], F32)) for i in range(8)]
        XIN, XDB, DTP = bank[0:2], bank[2], bank[4:6]
        HS, Y, G, U, YO, TP = bank[0:3], bank[3], bank[4], bank[5], bank[6], bank[7]
        RANK, TOT, TABLE = bank[0], bank[1], bank[2]
        TX, TH = bank[3], bank[7]

        ident = sb("ident", [P, P])
        ones = sb("ones", [P, P])
        upper = sb("upper", [P, P])
        iota_row = sb("iota_row", [P, P])
        part = sb("part", [P, 1])
        zrow = sb("zrow", [P, H])
        c_conv = sb("c_conv", [P, DT, 4])
        c_convb = sb("c_convb", [P, DT])
        c_dtb = sb("c_dtb", [P, DT])
        c_alog = sb("c_alog", [P, DT, NS])
        c_a = sb("c_a", [P, DT, NS])
        c_d = sb("c_d", [P, DT])
        c_gate = sb("c_gate", [P, KH, NE])
        ws_gu = sb("ws_gu", [P, KH, 4 * I])
        ws_dn = sb("ws_dn", [P, 2, 3, H])
        logits = sb("logits", [P, NT + 1, NE])

        halves = sb("halves", [P, TB])
        pre = ExitStack()

        def psb(name, shape, dt=F32):
            return pre.enter_context(nc.sbuf_tensor(name, shape, dt))

        p_ctx = psb("p_ctx", [P, 2, L])
        p_in = psb("p_in", [P, 2, H])
        p_xp = psb("p_xp", [P, DT, NX])
        p_dtw = psb("p_dtw", [RK, H])
        p_acc = psb("p_acc", [P, DT, L])
        p_u = psb("p_u", [P, DT, L])
        p_xd = psb("p_xd", [NX, L])
        p_abs = psb("p_abs", [P, 2, L])
        p_e = psb("p_e", [P, DT, L])
        p_relu = psb("p_relu", [P, DT, L])
        p_ln = psb("p_ln", [P, DT, L])
        p_ser = psb("p_ser", [P, DT, L])
        p_mask = psb("p_mask", [P, 2, L], I32)
        p_dt = psb("p_dt", [P, DT, L])
        p_x = psb("p_x", [P, TB, H])
        p_sz = psb("p_sz", [P, TB, H])
        p_st = psb("p_st", [P, TB, 6])
        p_mv = psb("p_mv", [P, TB, 2])
        p_ve = psb("p_ve", [P, TB])
        p_rs = psb("p_rs", [P, TB])
        p_nm = psb("p_nm", [P, TB])
        pre.close()

        bcs = sb("bcs", [P, 2, NS, L])
        Bs, Cs = bcs[:, 0], bcs[:, 1]
        dbu = sb("dbu", [P, NS, L])
        gs = sb("gs", [P, RING_G, L])
        xt = sb("xt", [P, TB, H])
        f_st = sb("f_st", [P, TB, 6])
        f_mv = sb("f_mv", [P, TB, 2])
        f_ve = sb("f_ve", [P, TB])
        f_rs = sb("f_rs", [P, TB])
        f_nm = sb("f_nm", [P, TB])
        f_xn = sb("f_xn", [P, 2, H])
        f_xnT = sb("f_xnT", [P, TB, H])
        f_sg = sb("f_sg", [P, 2, I])
        f_h = sb("f_h", [P, 2, I])
        f_hT = sb("f_hT", [P, 2, 3, P])

        slots = ExitStack()

        def msb(name, shape, dt=F32):
            return slots.enter_context(nc.sbuf_tensor(name, shape, dt))

        m_u = msb("m_u", [P, 2, L])
        m_dt = msb("m_dt", [P, 2, L])
        m_w = msb("m_w", [P, 2, L])
        m_x = msb("m_x", [P, 2, TB, P])
        m_sz = msb("m_sz", [P, 2, L])
        m_y = msb("m_y", [P, 2, L])
        slots.close()

        r_mx = sb("r_mx", [P, NT])
        r_e = sb("r_e", [P, NT, NE])
        r_sum = sb("r_sum", [P, NT])
        r_inv = sb("r_inv", [P, NT])
        r_s = sb("r_s", [P, NT, NE])
        r_top = sb("r_top", [P, NT, 8])
        r_ix = sb("r_ix", [P, NT, 8], U32)
        r_ixf = sb("r_ixf", [P, NT, K])
        r_m = sb("r_m", [P, K, NT, NE])
        r_ms = sb("r_ms", [P, NT, NE])
        r_tot = sb("r_tot", [P, NE, NT])
        r_res = sb("r_res", [P, NE, NT])
        r_inc = sb("r_inc", [P, NE, NT])
        r_cmp = sb("r_cmp", [P, NE, NT])
        r_nt = sb("r_nt", [P, NE])
        r_end = sb("r_end", [P, NE])
        r_base = sb("r_base", [P, NE])
        r_pos = sb("r_pos", [P, NT, NE])
        r_mp = sb("r_mp", [P, K, NT, NE])
        r_p = sb("r_p", [P, K, NT])
        r_pi = sb("r_pi", [P, K, NT], I32)
        r_qi = sb("r_qi", [P, K, NT], I32)
        r_ri = sb("r_ri", [P, K, NT], I32)
        r_q = sb("r_q", [P, K, NT])
        r_r = sb("r_r", [P, K, NT])
        r_tok = sb("r_tok", [P, K, NT])
        r_w = sb("r_w", [P, K, NT])
        t_exp = sb("t_exp", [P, UNITS + 1])
        t_expi = sb("t_expi", [P, UNITS + 1], I32)
        t_tok = sb("t_tok", [P, UNITS + 1], I32)
        t_w = sb("t_w", [P, UNITS + 1])
        flat = dbu[:, :, :].rearrange("p n l -> p (n l)")
        r_ohr = flat[:, 0:K * NT * P].rearrange("p (c j) -> p c j", j=P)
        o = K * NT * P
        r_rhs = flat[:, o:o + K * NT * 2 * UNITS].rearrange("p (c v u) -> p c v u", v=2, u=UNITS)
        r_ohq = gs[:, :, :].rearrange("p n l -> p (n l)")[:, 0:K * NT * UNITS].rearrange("p (c u) -> p c u", u=UNITS)
        o += K * NT * 2 * UNITS
        r_te = flat[:, o:o + UNITS * NE].rearrange("p (u e) -> p u e", e=NE)

        wide = bcs[:, :, :, :].rearrange("p a n l -> p (a n l)")
        e_gu = [wide[:, q * 2816:(q + 1) * 2816].rearrange("p (t n) -> p t n", t=KH) for q in range(2)]
        e_dn = [wide[:, 5632 + q * 1536:5632 + (q + 1) * 1536].rearrange("p (t n) -> p t n", t=3) for q in range(2)]
        e_gidx = sb("e_gidx", [P, 2], I32)
        e_sidx = sb("e_sidx", [P, 2], I32)
        e_w = sb("e_w", [P, 2])
        e_x = wide[:, 8704:9728].rearrange("p (a n) -> p a n", a=2)
        e_xT = wide[:, 9728:10752].rearrange("p (a n) -> p a n", a=2)
        e_sg = sb("e_sg", [P, I])
        e_h = sb("e_h", [P, I])
        e_hT = sb("e_hT", [P, 3, P])
        e_y = wide[:, 10752:11776].rearrange("p (a n) -> p a n", a=2)

        names = """const_loaded weights_loaded ctx_loaded z_loaded consts_made tables_made
            xin_ready acc_ready conv_done u_ready u_stored xd_ready xd_copied bc_stored
            dtp_ready dtp_free abs_done e_ready ln_ready ser_ready dt_ready dt_stored
            z_var z_rstd z_norm sz_ready sz_stored a_exp a_ready pool_step tap_done zstat_done soft_done dummy_ready
            u0_loaded u1_loaded d0_loaded d1_loaded x0_loaded x1_loaded s0_loaded s1_loaded
            b0_loaded b1_loaded b2_loaded b3_loaded c0_loaded c1_loaded c2_loaded c3_loaded
            w_ready dbu_ready exp_done scan_done g_ready ymm_done y_taken yT_ready x1_ready x1_stored
            xt0_loaded xt1_loaded xt2_loaded xt3_loaded var_ready rstd_ready norm_ready xn_ready xn0_stored xn1_stored xnT_ready xnT_copied lg_ready lg_copied
            gate_ready up_ready sg_ready h_ready hT_ready hT_copied down_ready down_added out_stored
            row_zeroed trash_stored rt_max rt_exp rt_mask rt_rank rt_oh rt_table tables_ready
            gu0_loaded gu1_loaded dn0_loaded dn1_loaded gidx_ready sidx_ready
            gx0_loaded gx1_loaded ex_ready exT_copied eg_ready eu_ready esg_ready eh_ready ehT_ready ehT_copied
            ey_ready ey_taken scattered gated_done tstat_done route_step idx_step waits_passed""".split()
        s = {n: sem(n) for n in names}
        (const_loaded, weights_loaded, ctx_loaded, z_loaded, consts_made, tables_made,
         xin_ready, acc_ready, conv_done, u_ready, u_stored, xd_ready, xd_copied, bc_stored,
         dtp_ready, dtp_free, abs_done, e_ready, ln_ready, ser_ready, dt_ready, dt_stored,
         z_var, z_rstd, z_norm, sz_ready, sz_stored, a_exp, a_ready, pool_step, tap_done, zstat_done, soft_done,
         dummy_ready) = [s[n] for n in names[:34]]
        u_loaded = [s["u0_loaded"], s["u1_loaded"]]
        d_loaded = [s["d0_loaded"], s["d1_loaded"]]
        x_loaded = [s["x0_loaded"], s["x1_loaded"]]
        s_loaded = [s["s0_loaded"], s["s1_loaded"]]
        b_loaded = [s[f"b{q}_loaded"] for q in range(NG)]
        c_loaded = [s[f"c{q}_loaded"] for q in range(NG)]
        at = names.index("w_ready")
        (w_ready, dbu_ready, exp_done, scan_done, g_ready, ymm_done, y_taken, yT_ready, x1_ready, x1_stored,
         xt0_loaded, xt1_loaded, xt2_loaded, xt3_loaded, var_ready, rstd_ready, norm_ready, xn_ready, xn0_stored, xn1_stored, xnT_ready, xnT_copied, lg_ready,
         lg_copied, gate_ready, up_ready, sg_ready, h_ready, hT_ready, hT_copied, down_ready, down_added,
         out_stored, row_zeroed, trash_stored, rt_max, rt_exp, rt_mask, rt_rank, rt_oh, rt_table,
         tables_ready) = [s[n] for n in names[at:at + 42]]
        xt_loaded = [xt0_loaded, xt1_loaded, xt2_loaded, xt3_loaded]
        xn_stored = [xn0_stored, xn1_stored]
        gu_loaded = [s["gu0_loaded"], s["gu1_loaded"]]
        dn_loaded = [s["dn0_loaded"], s["dn1_loaded"]]
        gx_loaded = [s["gx0_loaded"], s["gx1_loaded"]]
        (gidx_ready, sidx_ready) = s["gidx_ready"], s["sidx_ready"]
        at = names.index("ex_ready")
        (ex_ready, exT_copied, eg_ready, eu_ready, esg_ready, eh_ready, ehT_ready, ehT_copied,
         ey_ready, ey_taken, scattered, gated_done, tstat_done, route_step, idx_step, waits_passed) = [s[n] for n in names[at:at + 16]]
        block = stack.enter_context(nc.Block())

        def held(eng):
            eng.sem_inc(waits_passed)

        def from_one(eng, count):
            eng.sem_inc(count, 1)

        def pre_finished(eng):
            for stored in (u_stored, bc_stored, dt_stored, sz_stored):
                eng.wait_ge(stored, 1 + 16 * B)

        @block.sync
        def _(sp):
            for count in (u_stored, sz_stored, bc_stored, dt_stored, out_stored, xn0_stored, xn1_stored):
                from_one(sp, count)
            for dst, src in ((p_in[:], inT.rearrange("(t p) n -> p t n", p=P)), (c_conv[:], convw), (c_convb[:], convb),
                             (p_xp[:], xpT.rearrange("(t p) n -> p t n", p=P)), (p_dtw[:], dtT), (c_dtb[:], dtb),
                             (c_alog[:], alog), (c_d[:], dskip), (c_gate[:], gateT.rearrange("(t p) n -> p t n", p=P))):
                sp.dma_start(dst, src).then_inc(const_loaded, 16)
            with sp.Fori(0, B) as b:
                sp.wait_ge(xin_ready, 1 + b * DT)
                sp.dma_start(p_ctx[:], ctxT[bass.ds(b, 1)].rearrange("a (t p) l -> p (a t) l", p=P)).then_inc(ctx_loaded, 16)
                sp.wait_ge(sz_ready, 1 + b * TB)
                sp.dma_start(p_x[:], batch_rows(x, b)).then_inc(z_loaded, 16)
                sp.wait_ge(sz_ready, 1 + b * TB + TB)
                sp.dma_start(batch_rows(sz_d, b), p_sz[:]).then_inc(sz_stored, 16)
                sp.wait_ge(u_ready, b * DT + DT)
                sp.dma_start(u_d[bass.ds(b, 1)].rearrange("a p t l -> p (a t) l"), p_u[:]).then_inc(u_stored, 16)
                sp.wait_ge(xd_copied, 1 + b + 1)
                sp.dma_start(bc_d[bass.ds(b, 1)].rearrange("a n l -> (a n) l"), p_xd[RK:NX, :]).then_inc(bc_stored, 16)
                sp.wait_ge(dt_ready, 1 + b * DT + DT)
                sp.dma_start(dt_d[bass.ds(b, 1)].rearrange("a p t l -> p (a t) l"), p_dt[:]).then_inc(dt_stored, 16)

            sp.dma_start(ws_gu[:], sgu.rearrange("(t p) n -> p t n", p=P)).then_inc(weights_loaded, 16)
            for c in range(2):
                for t, (r, n) in enumerate(IT):
                    sp.dma_start(ws_dn[0:n, c, t, :], sdn[c * I + r:c * I + r + n, :]).then_inc(weights_loaded, 16)

            def load_slot(b, q):
                par = q % 2
                sp.dma_start(m_dt[:, par, :], dt_d[bass.ds(b, 1), :, q, :].rearrange("a p l -> p (a l)")).then_inc(d_loaded[par], 16)
                sp.dma_start(m_u[:, par, :], u_d[bass.ds(b, 1), :, q, :].rearrange("a p l -> p (a l)")).then_inc(u_loaded[par], 16)
                sp.dma_start(m_x[:, par], batch_rows(x, b)[:, :, q * P:(q + 1) * P]).then_inc(x_loaded[par], 16)
                sp.dma_start(m_sz[:, par], sz_d[bass.ds(b * L + q * P, P), :]).then_inc(s_loaded[par], 16)

            def load_bc(b, g, which):
                dst, row, done = ((Bs, 0, b_loaded), (Cs, NS, c_loaded))[which]
                src = bc_d[bass.ds(b, 1), row + g * GRP:row + (g + 1) * GRP, :].rearrange("a n l -> a (n l)")
                sp.dma_start(dst[:, g * GRP:(g + 1) * GRP, :].rearrange("p n l -> p (n l)"),
                             src.to_broadcast([P, GRP * L])).then_inc(done[g], 16)

            pre_finished(sp)
            load_slot(0, 0)
            for g in range(NG):
                load_bc(0, g, 0)
                load_bc(0, g, 1)
            load_slot(0, 1)

            def x1_store(b, q, i):
                sp.wait_ge(x1_ready, i + 1)
                held(sp)
                sp.dma_start(batch_rows(x1_d, b)[:, :, q * P:(q + 1) * P], m_x[:, q % 2]).then_inc(x1_stored, 16)

            def xt_load(j, jb):
                sp.wait_ge(x1_stored, jb * 16 * DT + 16 * DT)
                sp.dma_start(xt[:, j[1], :], x1_d[bass.ds(j[0] * P, P), :]).then_inc(xt_loaded[j[1]], 16)

            def xn_store(j):
                sp.wait_ge(xn_ready, j[0] + 1)
                sp.dma_start(xn_d[bass.ds(j[0] * P + P, P), :], f_xn[:, j[1] % 2, :]).then_inc(xn_stored[j[1] % 2], 16)

            def out_store(f):
                sp.wait_ge(down_added, 1 + 2 * f[0] + 2)
                sp.dma_start(out[bass.ds(f[0] * P, P), :], xt[:, (f[1] + 3) % 4, :]).then_inc(out_stored, 16)

            def slot(b, q, rows, last=False):
                i = b * DT + q
                if not (isinstance(b, int) and b == 0 and q == 0):
                    pb, pq = (b, q - 1) if q else (b - 1, DT - 1)
                    x1_store(pb, pq, i - 1)
                    if not (last and q == DT - 1):
                        nb, nq = (b, q + 1) if q < DT - 1 else (b + 1, 0)
                        sp.wait_ge(y_taken, i)
                        held(sp)
                        sp.wait_ge(x1_stored, i * 16)
                        held(sp)
                        load_slot(nb, nq)
                if rows:
                    j = ((b - 1) * DT + q, q)
                    sp.wait_ge(out_stored, 1 + j[0] * 16)
                    xt_load(j, b - 1)
                if q == DT - 1 and not last:
                    for g in range(NG):
                        sp.wait_ge(dbu_ready, i * NG + g + 1)
                        load_bc(b + 1, g, 0)
                        if rows and g == NG - 1:
                            xn_store(j)
                            out_store(j)
                        sp.wait_ge(g_ready, i * NS + g * GRP + GRP)
                        load_bc(b + 1, g, 1)
                elif rows:
                    xn_store(j)
                    out_store(j)

            for q in range(DT):
                slot(0, q, False)
            with sp.Fori(1, B - 1) as b:
                for q in range(DT):
                    slot(b, q, True)
            for q in range(DT):
                slot(B - 1, q, True, last=True)

            x1_store(B - 1, DT - 1, B * DT - 1)
            first = NT - TB
            for q in range(TB - 1):
                sp.wait_ge(out_stored, 1 + (first + q - 2) * 16)
                xt_load((first + q, q), B - 1)
            for q in range(TB - 1):
                xn_store((first + q, q))
            out_store((first, 0))
            sp.wait_ge(out_stored, 1 + (first + 1) * 16)
            xt_load((NT - 1, TB - 1), B - 1)
            xn_store((NT - 1, TB - 1))
            for f in range(first + 1, NT + 1):
                out_store((f, f % TB))

            def load_expert(k, par):
                sp.wait_ge(eu_ready, k - 1)
                e = sp.value_load(t_expi[0:1, bass.ds(k, 1)], min_val=0, max_val=NE - 1)
                sp.dma_start(e_gu[par], wgu[bass.ds(e, 1)].rearrange("a (t p) n -> p (a t) n", p=P)).then_inc(gu_loaded[par], 16)
                sp.wait_ge(ey_ready, k - 1)
                sp.dma_start(e_dn[par][:, 0:2, :], wdn[bass.ds(e, 1), 0:2 * P, :].rearrange("a (t p) n -> p (a t) n", p=P)).then_inc(dn_loaded[par], 16)
                sp.dma_start(e_dn[par][0:IT[2][1], 2, :], wdn[bass.ds(e, 1), 2 * P:I, :].rearrange("a p n -> (a p) n")).then_inc(dn_loaded[par], 16)

            sp.wait_ge(tables_ready, 1)
            for k in range(2):
                e = sp.value_load(t_expi[0:1, k:k + 1], min_val=0, max_val=NE - 1)
                sp.dma_start(e_gu[k], wgu[bass.ds(e, 1)].rearrange("a (t p) n -> p (a t) n", p=P)).then_inc(gu_loaded[k], 16)
                sp.dma_start(e_dn[k][:, 0:2, :], wdn[bass.ds(e, 1), 0:2 * P, :].rearrange("a (t p) n -> p (a t) n", p=P)).then_inc(dn_loaded[k], 16)
                sp.dma_start(e_dn[k][0:IT[2][1], 2, :], wdn[bass.ds(e, 1), 2 * P:I, :].rearrange("a p n -> (a p) n")).then_inc(dn_loaded[k], 16)
            with sp.Fori(1, UNITS // 2) as r:
                for par in range(2):
                    load_expert(r * 2 + par, par)
            load_expert(UNITS - 1, 0)
            sp.wait_ge(scattered, 16 * UNITS)
            sp.wait_ge(out_stored, 1 + 16 * (NT + 1))
            sp.wait_ge(trash_stored, 16)

        @block.tensor
        def _(pe):
            mm = nc.tensor.matmul
            for count in (xin_ready, xnT_ready, hT_ready, down_ready):
                from_one(pe, count)
            pe.wait_ge(const_loaded, 16 * 9)
            pe.wait_ge(consts_made, 5)
            with pe.Fori(0, B) as b:
                pe.wait_ge(ctx_loaded, b * 16 + 16)
                for q in range(DT):
                    pe.wait_ge(conv_done, b * DT + q + 1)
                    for t in range(2):
                        last = mm(XIN[q % 2][:], p_in[:, t, q * P:(q + 1) * P], p_ctx[:, t, :], start=t == 0, stop=t == 1)
                    last.then_inc(xin_ready, 1)
                pe.wait_ge(u_ready, b * DT + DT)
                pe.wait_ge(xd_copied, 1 + b)
                for q in range(DT):
                    last = mm(XDB[0:NX, :], p_xp[:, q, :], p_u[:, q, :], start=q == 0, stop=q == DT - 1)
                last.then_inc(xd_ready, 1)
                pe.wait_ge(xd_copied, 1 + b + 1)
                for q in range(DT):
                    pe.wait_ge(dtp_free, b * DT + q + 1)
                    mm(DTP[q % 2][:], p_dtw[:, q * P:(q + 1) * P], p_xd[0:RK, :], start=True, stop=True).then_inc(dtp_ready, 1)
            pre_finished(pe)
            pe.wait_ge(weights_loaded, 16 * 7)
            pe.wait_ge(dummy_ready, 1)

            def y_sum(b, q, n):
                i, k = b * DT + q, q * NS + n
                if n == 0:
                    pe.wait_ge(y_taken, i)
                pe.wait_ge(g_ready, i * NS + n + 1)
                mm(Y[:], ident[:], gs[:, k % RING_G, :], start=n == 0, stop=n == NS - 1).then_inc(ymm_done, 1)

            def y_turn(i, par, copied):
                pe.wait_ge(gated_done, i + 1)
                pe.wait_ge(x1_ready, i)
                pe.wait_ge(lg_copied, 1 + copied)
                for t in range(TB):
                    last = nc.tensor.transpose(TP[:, t * P:(t + 1) * P], m_y[:, par, t * P:(t + 1) * P], ident[:])
                last.then_inc(yT_ready, 1)

            def xn_turn(j, x1_count):
                pe.wait_ge(xn_ready, j[0] + 1)
                pe.wait_ge(x1_ready, x1_count)
                pe.wait_ge(lg_copied, 1 + j[0])
                for t in range(KH):
                    last = nc.tensor.transpose(TP[:, t * P:(t + 1) * P], f_xn[:, j[1] % 2, t * P:(t + 1) * P], ident[:])
                last.then_inc(xnT_ready, 1)

            def router(f, copied):
                pe.wait_ge(xnT_copied, 1 + copied)
                pe.wait_ge(lg_copied, 1 + f[0])
                for t in range(KH):
                    last = mm(TP[:, 0:NE], f_xnT[:, (f[1] + 3) % 4, t * P:(t + 1) * P], c_gate[:, t, :], start=t == 0, stop=t == KH - 1)
                last.then_inc(lg_ready, 1)

            def shared(f):
                at = (f[1] + 3) % 4
                lhs = [f_xnT[:, at, t * P:(t + 1) * P] for t in range(KH)]

                def up(c, half):
                    dst, off, done = ((G, 0, gate_ready), (U, 2 * I, up_ready))[half]
                    def piece(ts):
                        if ts[0] == 0:
                            if half == 0:
                                pe.wait_ge(sg_ready, 1 + 2 * f[0] + c)
                                pe.wait_ge(xnT_copied, 1 + f[0])
                            else:
                                pe.wait_ge(h_ready, 1 + 2 * f[0] + c)
                        for t in ts:
                            last = mm(dst[:, 0:I], lhs[t], ws_gu[:, t, off + c * I:off + (c + 1) * I], start=t == 0, stop=t == KH - 1)
                        if ts[-1] == KH - 1:
                            last.then_inc(done, 1)
                    return [lambda: piece([0, 1]), lambda: piece([2, 3])]

                def turn(c):
                    pe.wait_ge(h_ready, 1 + 2 * f[0] + c + 1)
                    pe.wait_ge(down_added, 1 + 2 * f[0] + c)
                    for t, (r, n) in enumerate(IT):
                        last = nc.tensor.transpose(YO[0:n, t * P:(t + 1) * P], f_h[:, c, r:r + n], ident[:])
                    last.then_inc(hT_ready, 1)

                def down(c, t):
                    if t == 0:
                        pe.wait_ge(hT_copied, 2 * f[0] + c + 1)
                    n = IT[t][1]
                    last = mm(YO[:], f_hT[0:n, c, t, :], ws_dn[0:n, c, t, :], start=t == 0, stop=t == 2)
                    if t == 2:
                        last.then_inc(down_ready, 1)

                (g0a, g0b), (u0a, u0b) = up(0, 0), up(0, 1)
                (g1a, g1b), (u1a, u1b) = up(1, 0), up(1, 1)
                return [[g0a], [g0b], [u0a], [u0b], [g1a], [g1b], [u1a], [u1b, lambda: turn(0)], [lambda: down(0, 0)],
                        [lambda: down(0, 1), lambda: down(0, 2)], [], [lambda: turn(1)],
                        [lambda: down(1, 0)], [lambda: down(1, 1), lambda: down(1, 2)], [], []]

            def slot(b, q, rows):
                i = b * DT + q
                if rows:
                    f = ((b - 1) * DT + q, q)
                    pieces = shared(f)
                for n in range(NS):
                    y_sum(b, q, n)
                    if rows and n == 0:
                        router(f, f[0])
                    if n == 4 and not (isinstance(b, int) and b == 0 and q == 0):
                        y_turn(i - 1, (q - 1) % 2, f[0] + 1 if rows else 0)
                    if rows:
                        for piece in pieces[n]:
                            piece()
                        if n == 14:
                            xn_turn(f, i)

            for q in range(DT):
                slot(0, q, False)
            with pe.Fori(1, B) as b:
                for q in range(DT):
                    slot(b, q, True)
            pe.wait_ge(xnT_copied, 1 + NT - TB)
            y_turn(B * DT - 1, (DT - 1) % 2, NT - TB)

            def whole(f):
                for piece in shared(f):
                    for run in piece:
                        run()

            first = NT - TB
            for q in range(TB - 1):
                xn_turn((first + q, q), B * DT)
                router((first + q, q), first + q + 1)
            whole((first, 0))
            xn_turn((NT - 1, TB - 1), B * DT)
            router((NT - 1, TB - 1), NT)
            router((NT, 0), NT)
            whole((first + 1, 1))
            pe.wait_ge(rt_mask, 1)
            ms = r_ms[:, :, :].rearrange("p t e -> p (t e)")
            mm(RANK[:, 0:NT * NE], upper[:], ms, start=True, stop=True).then_inc(rt_rank, 1)
            mm(TOT[:, 0:NT * NE], ones[:], ms, start=True, stop=True).then_inc(rt_rank, 1)
            whole((first + 2, 2))
            for c in range(K * NT):
                if c % 8 == 0:
                    pe.wait_ge(rt_oh, c // 8 + 1)
                last = mm(TABLE[:, 0:2 * UNITS], r_ohr[:, c, :], r_rhs[:, c, :, :].rearrange("p v u -> p (v u)"),
                          start=c == 0, stop=c == K * NT - 1)
            last.then_inc(rt_table, 1)
            whole((first + 3, 3))
            whole((NT, 0))

            def x_turn(k, par, loads):
                pe.wait_ge(gx_loaded[par], loads)
                pe.wait_ge(exT_copied, k)
                for t in range(KH):
                    last = nc.tensor.transpose(TX[:, t * P:(t + 1) * P], e_x[:, par, t * P:(t + 1) * P], ident[:])
                last.then_inc(ex_ready, 1)

            def up(k, par, loads):
                pe.wait_ge(exT_copied, k + 1)
                pe.wait_ge(gu_loaded[par], loads)
                for half, (dst, done, free) in enumerate(((G, eg_ready, esg_ready), (U, eu_ready, eh_ready))):
                    pe.wait_ge(free, k)
                    for t in range(KH):
                        last = mm(dst[:, 0:I], e_xT[:, par, t * P:(t + 1) * P], e_gu[par][:, t, half * I:(half + 1) * I],
                                  start=t == 0, stop=t == KH - 1)
                    last.then_inc(done, 1)

            def h_turn(k):
                pe.wait_ge(eh_ready, k + 1)
                for t, (r, n) in enumerate(IT):
                    last = nc.tensor.transpose(TH[0:n, t * P:(t + 1) * P], e_h[:, r:r + n], ident[:])
                last.then_inc(ehT_ready, 1)

            def down(k, par, loads):
                pe.wait_ge(ehT_copied, k + 1)
                pe.wait_ge(dn_loaded[par], loads * 2)
                pe.wait_ge(ey_taken, 1 + k)
                for t in range(3):
                    n = IT[t][1]
                    last = mm(YO[:], e_hT[0:n, t, :], e_dn[par][0:n, t, :], start=t == 0, stop=t == 2)
                last.then_inc(ey_ready, 1)

            pe.wait_ge(sg_ready, 1 + 2 * (NT + 1))
            pe.wait_ge(h_ready, 1 + 2 * (NT + 1))
            pe.wait_ge(down_added, 1 + 2 * (NT + 1))
            x_turn(0, 0, 16)
            up(0, 0, 16)
            h_turn(0)
            x_turn(1, 1, 16)
            with pe.Fori(0, UNITS // 2) as r:
                for half in range(2):
                    par = 1 - half
                    k = r * 2 + 1 + half
                    up(k, par, (r + half) * 16 + 16)
                    down(k - 1, 1 - par, (r * 16 + 16))
                    h_turn(k)
                    x_turn(k + 1, 1 - par, (r + 1) * 16 + 16)
            down(UNITS - 1, 0, (UNITS // 2) * 16 + 16)

        @block.scalar
        def _(act):
            f = nc.scalar.activation
            for count in (sz_ready, xd_copied, xnT_copied, sg_ready):
                from_one(act, count)
            act.wait_ge(const_loaded, 16 * 9)
            f(c_a[:], c_alog[:], ACT.Exp).then_inc(a_exp, 1)
            with act.Fori(0, B) as b:
                act.wait_ge(u_stored, 1 + b * 16)
                for q in range(DT):
                    act.wait_ge(xin_ready, 1 + b * DT + q + 1)
                    f(p_acc[:, q, :], XIN[q % 2][:], ACT.Identity, scale=c_conv[:, q, 3:4], bias=c_convb[:, q:q + 1]).then_inc(acc_ready, 1)
                act.wait_ge(z_norm, b + 1)
                act.wait_ge(sz_stored, 1 + b * 16)
                for t in range(TB):
                    f(p_sz[:, t, :], p_x[:, t, :], ACT.Silu, scale=p_rs[:, t:t + 1], bias=p_nm[:, t:t + 1]).then_inc(sz_ready, 1)
                for q in range(DT):
                    act.wait_ge(conv_done, b * DT + q + 3)
                    f(p_u[:, q, :], p_acc[:, q, :], ACT.Silu).then_inc(u_ready, 1)
                act.wait_ge(xd_ready, b + 1)
                act.wait_ge(bc_stored, 1 + b * 16)
                f(p_xd[:], XDB[0:NX, :], ACT.Copy).then_inc(xd_copied, 1)
                act.wait_ge(dt_ready, 1 + b * DT)
                for q in range(DT):
                    act.wait_ge(dtp_ready, b * DT + q + 1)
                    f(p_abs[:, q % 2, :], DTP[q % 2][:], ACT.Abs, bias=c_dtb[:, q:q + 1]).then_inc(abs_done, 1)
                    f(p_relu[:, q, :], DTP[q % 2][:], ACT.Relu, bias=c_dtb[:, q:q + 1]).then_inc(dtp_free, 1)
                    act.wait_ge(abs_done, b * DT + q + 1)
                    f(p_e[:, q, :], p_abs[:, q % 2, :], ACT.Exp, scale=-1.0).then_inc(e_ready, 1)
                for q in range(DT):
                    act.wait_ge(e_ready, b * DT + q + 1)
                    f(p_ln[:, q, :], p_e[:, q, :], ACT.Ln, bias=1.0).then_inc(ln_ready, 1)
            pre_finished(act)
            act.wait_ge(a_ready, 1)

            def decay(b, q, n):
                k = q * NS + n
                if k >= RING_H:
                    act.wait_ge(g_ready, b * STEPS + k - RING_H + 1)
                elif not (isinstance(b, int) and b == 0):
                    act.wait_ge(g_ready, b * STEPS - (0, 2, 1)[k])
                if n == 0:
                    act.wait_ge(d_loaded[q % 2], b * 32 + (q // 2) * 16 + 16)
                f(HS[k % RING_H][:], m_dt[:, q % 2, :], ACT.Exp, scale=c_a[:, q, n:n + 1]).then_inc(exp_done, 1)

            def gate(fx, c):
                act.wait_ge(gate_ready, 2 * fx[0] + c + 1)
                act.wait_ge(h_ready, 1 + 2 * fx[0])
                f(f_sg[:, c, :], G[:, 0:I], ACT.Silu).then_inc(sg_ready, 1)

            def hT_copy(fx, c):
                act.wait_ge(hT_ready, 1 + 2 * fx[0] + c + 1)
                act.wait_ge(down_ready, 1 + 2 * fx[0])
                f(f_hT[:, c, 0:2, :], YO[:, 0:2 * P].rearrange("p (t j) -> p t j", t=2), ACT.Copy)
                f(f_hT[0:96, c, 2, :], YO[0:96, 2 * P:3 * P], ACT.Copy).then_inc(hT_copied, 1)

            def xn(j, stored):
                act.wait_ge(norm_ready, j[0] + 1)
                act.wait_ge(xn_stored[j[1] % 2], 1 + stored)
                act.wait_ge(xnT_ready, 1 + j[0])
                f(f_xn[:, j[1] % 2, :], xt[:, j[1], :], ACT.Identity, scale=f_rs[:, j[1]:j[1] + 1], bias=f_nm[:, j[1]:j[1] + 1]).then_inc(xn_ready, 1)

            def xnT_copy(j, past):
                act.wait_ge(xnT_ready, 1 + j[0] + 1)
                act.wait_ge(down_ready, 1 + past)
                f(f_xnT[:, j[1], :], TP[:], ACT.Copy).then_inc(xnT_copied, 1)

            def slot(b, q, rows):
                for n in range(NS):
                    decay(b, q, n)
                    if rows:
                        j = ((b - 1) * DT + q, q)
                        if n == 4:
                            gate(j, 0)
                        if n == 8:
                            gate(j, 1)
                            hT_copy(j, 0)
                        if n == 13:
                            hT_copy(j, 1)
                        if n == 14:
                            xn(j, ((b - 1) * 2 + q // 2) * 16)
                if rows:
                    xnT_copy(j, 2 * j[0])

            for q in range(DT):
                slot(0, q, False)
            with act.Fori(1, B) as b:
                for q in range(DT):
                    slot(b, q, True)

            def whole(fx):
                gate(fx, 0)
                gate(fx, 1)
                hT_copy(fx, 0)
                hT_copy(fx, 1)

            first = NT - TB
            for q in range(TB):
                if q == TB - 1:
                    whole((first, 0))
                xn((first + q, q), ((first + q) // 2) * 16)
                xnT_copy((first + q, q), 2 * (first + q - 2))
            act.wait_ge(rt_max, 1)
            f(r_e[:], r_e[:], ACT.Exp).then_inc(rt_exp, 1)
            whole((first + 1, 1))
            whole((first + 2, 2))
            whole((first + 3, 3))
            whole((NT, 0))

            def x_copy(k, par, used):
                act.wait_ge(ex_ready, k + 1)
                act.wait_ge(eu_ready, used)
                f(e_xT[:, par, :], TX[:], ACT.Copy).then_inc(exT_copied, 1)

            def unit(k, par):
                act.wait_ge(eg_ready, k + 1)
                act.wait_ge(eh_ready, k)
                f(e_sg[:], G[:, 0:I], ACT.Silu).then_inc(esg_ready, 1)
                act.wait_ge(ehT_ready, k + 1)
                act.wait_ge(ey_ready, k)
                f(e_hT[:, 0:2, :], TH[:, 0:2 * P].rearrange("p (t j) -> p t j", t=2), ACT.Copy)
                f(e_hT[0:96, 2, :], TH[0:96, 2 * P:3 * P], ACT.Copy).then_inc(ehT_copied, 1)
                x_copy(k + 1, 1 - par, k)

            x_copy(0, 0, 0)
            unit(0, 0)
            with act.Fori(0, UNITS // 2) as r:
                for half in range(2):
                    unit(r * 2 + 1 + half, 1 - half)

        @block.gpsimd
        def _(pool):
            g = nc.gpsimd
            g.memset(ident[:], 0.0).then_inc(pool_step, 1)
            g.memset(ones[:], 1.0).then_inc(consts_made, 1)
            g.memset(halves[:], -0.5).then_inc(consts_made, 1)
            g.memset(upper[:], 1.0).then_inc(pool_step, 1)
            g.memset(zrow[:], 0.0).then_inc(row_zeroed, 1)
            pool.wait_ge(pool_step, 2)
            g.affine_select(out=ident[:], in_=ident[:], compare_op=ALU.not_equal, fill=1.0, base=0,
                            pattern=[[-1, P]], channel_multiplier=1).then_inc(consts_made, 1)
            g.affine_select(out=upper[:], in_=upper[:], compare_op=ALU.is_gt, fill=0.0, base=0,
                            pattern=[[1, P]], channel_multiplier=-1).then_inc(consts_made, 1)
            g.iota(iota_row[:], [[1, P]], base=0, channel_multiplier=0, allow_small_or_imprecise_dtypes=True).then_inc(consts_made, 1)
            g.iota(part[:], [[0, 1]], base=0, channel_multiplier=1, allow_small_or_imprecise_dtypes=True).then_inc(tables_made, 1)
            pool.wait_ge(row_zeroed, 1)
            pool.dma_start(xn_d[0:P, :], zrow[:]).then_inc(trash_stored, 16)
            pool.wait_ge(consts_made, 5)
            made = 2
            with pool.Fori(0, B) as b:
                pool.wait_ge(z_var, b + 1)
                g.tensor_tensor(p_rs[:], p_ve[:], halves[:], ALU.pow).then_inc(z_rstd, 1)
                for q in range(DT):
                    pool.wait_ge(e_ready, b * DT + q + 1)
                    held(pool)
                    g.tensor_scalar(p_ser[:, q, :], p_e[:, q, :], 1.0 / 3.0, -0.5, ALU.mult, ALU.add).then_inc(pool_step, 1)
                    pool.wait_ge(pool_step, b * DT + made + q + 1)
                    g.tensor_tensor(p_ser[:, q, :], p_ser[:, q, :], p_e[:, q, :], ALU.mult).then_inc(ser_ready, 1)
            pre_finished(pool)

            def slot(b, q, rows):
                i = b * DT + q
                pool.wait_ge(u_loaded[q % 2], b * 32 + (q // 2) * 16 + 16)
                pool.wait_ge(d_loaded[q % 2], b * 32 + (q // 2) * 16 + 16)
                g.tensor_tensor(m_w[:, q % 2, :], m_u[:, q % 2, :], m_dt[:, q % 2, :], ALU.mult).then_inc(w_ready, 1)
                pool.wait_ge(w_ready, i + 1)
                for gr in range(NG):
                    pool.wait_ge(b_loaded[gr], b * 16 + 16)
                    if not (isinstance(b, int) and i == 0):
                        pool.wait_ge(scan_done, (i - 1) * NS + gr * GRP + GRP)
                    part_ = dbu[:, gr * GRP:(gr + 1) * GRP, :]
                    w = m_w[:, q % 2:q % 2 + 1, :].to_broadcast([P, GRP, L])
                    g.tensor_tensor(part_, Bs[:, gr * GRP:(gr + 1) * GRP, :], w, ALU.mult).then_inc(dbu_ready, 1)
                if rows:
                    rstd(((b - 1) * DT + q, q))

            def rstd(j):
                pool.wait_ge(var_ready, j[0] + 1)
                g.tensor_tensor(f_rs[:, j[1]:j[1] + 1], f_ve[:, j[1]:j[1] + 1], halves[:, 0:1], ALU.pow).then_inc(rstd_ready, 1)

            for q in range(DT):
                slot(0, q, False)
            with pool.Fori(1, B) as b:
                for q in range(DT):
                    slot(b, q, True)
            for q in range(TB):
                rstd((NT - TB + q, q))

            pool.wait_ge(tables_ready, 1)
            for par in range(2):
                pool.wait_ge(xn_stored[par], 1 + 16 * (NT // 2))
            pool.wait_ge(trash_stored, 16)

            def gather(k, par):
                pool.wait_ge(gidx_ready, k + 1)
                held(pool)
                pool.indirect_dma_start(e_x[:, par, :], None, xn_d, bass.IndirectOffsetOnAxis(ap=e_gidx[:, par:par + 1], axis=0)).then_inc(gx_loaded[par], 16)

            def scatter(k, par):
                pool.wait_ge(ey_taken, 1 + k + 1)
                pool.wait_ge(sidx_ready, k + 1)
                if not (isinstance(k, int) and k == 0):
                    pool.wait_ge(scattered, k * 16)
                held(pool)
                pool.indirect_dma_start(out, bass.IndirectOffsetOnAxis(ap=e_sidx[:, par:par + 1], axis=0), e_y[:, par, :], None,
                                        compute_op=ALU.add).then_inc(scattered, 16)

            gather(0, 0)
            gather(1, 1)
            pool.wait_ge(out_stored, 1 + 16 * (NT + 1))

            def rows_of_two(r):
                for half in range(2):
                    k = r * 2 + half
                    pool.wait_ge(ex_ready, k + 1)
                    gather(k + 2, half)
                    scatter(k, half)

            rows_of_two(0)
            with pool.Fori(1, UNITS // 2) as r:
                rows_of_two(r)
            scatter(UNITS - 1, 0)
            pool.wait_ge(scattered, 16 * UNITS)

        @block.vector
        def _(dve):
            v = nc.vector
            for count in (dt_ready, h_ready, down_added, lg_copied, ey_taken):
                from_one(dve, count)
            dve.wait_ge(const_loaded, 16 * 9)
            dve.wait_ge(a_exp, 1)
            v.tensor_scalar(c_a[:], c_a[:], -1.0, None, ALU.mult).then_inc(a_ready, 1)
            dve.sem_inc(conv_done, 2)
            dve.sem_inc(dtp_free, 2)
            with dve.Fori(0, B) as b:
                dve.wait_ge(z_loaded, b * 16 + 16)
                for t in range(TB):
                    last = v.bn_stats(p_st[:, t, :], p_x[:, t, :])
                last.then_inc(zstat_done, 1)
                dve.wait_ge(zstat_done, b * 2 + 1)
                dve.wait_ge(sz_ready, 1 + b * TB)
                for t in range(TB):
                    held(dve) if t == 0 else None
                    last = v.bn_aggr(p_mv[:, t, :], p_st[:, t, :])
                last.then_inc(zstat_done, 1)
                dve.wait_ge(zstat_done, b * 2 + 2)
                v.tensor_scalar(p_ve[:], p_mv[:, :, 0:2][:, :, 1], EPS, None, ALU.add).then_inc(z_var, 1)
                for q in range(DT):
                    dve.wait_ge(acc_ready, b * DT + q + 1)
                    for back in range(1, 4):
                        if back > 1:
                            dve.wait_ge(tap_done, (b * DT + q) * 2 + back - 1)
                        a = p_acc[:, q, back:L]
                        ins = v.scalar_tensor_tensor(a, XIN[q % 2][:, 0:L - back], c_conv[:, q, 3 - back:4 - back], a, ALU.mult, ALU.add)
                        ins.then_inc(tap_done if back < 3 else conv_done, 1)
                    if q == 0:
                        dve.wait_ge(z_rstd, b + 1)
                        v.scalar_tensor_tensor(p_nm[:], p_mv[:, :, 0], -1.0, p_rs[:], ALU.mult, ALU.mult).then_inc(z_norm, 1)
                dve.wait_ge(dt_stored, 1 + b * 16)
                for q in range(DT):
                    dve.wait_ge(ser_ready, b * DT + q + 1)
                    v.tensor_scalar(p_mask[:, q % 2, :], p_e[:, q, :], THETA, None, ALU.is_ge)
                    v.scalar_tensor_tensor(p_ser[:, q, :], p_ser[:, q, :], 1.0, p_e[:, q, :], ALU.add, ALU.mult).then_inc(soft_done, 1)
                    dve.wait_ge(soft_done, (b * DT + q) * 2 + 1)
                    dve.wait_ge(ln_ready, b * DT + q + 1)
                    held(dve)
                    v.copy_predicated(p_ser[:, q, :], p_mask[:, q % 2, :], p_ln[:, q, :]).then_inc(soft_done, 1)
                    dve.wait_ge(soft_done, (b * DT + q) * 2 + 2)
                    v.tensor_tensor(p_dt[:, q, :], p_ser[:, q, :], p_relu[:, q, :], ALU.add).then_inc(dt_ready, 1)
            pre_finished(dve)
            v.memset(xt[:, TB - 1, :], 0.0)
            v.memset(f_xnT[:, TB - 1, :], 0.0).then_inc(dummy_ready, 1)

            def scan(b, q, n):
                k = q * NS + n
                if n % GRP == 0:
                    dve.wait_ge(dbu_ready, (b * DT + q) * NG + n // GRP + 1)
                dve.wait_ge(exp_done, b * STEPS + k + 1)
                h = HS[k % RING_H][:]
                v.tensor_tensor_scan(h, h, dbu[:, n, :], 0.0, ALU.mult, ALU.add).then_inc(scan_done, 1)

            def times_c(b, q, n):
                k = q * NS + n
                dve.wait_ge(scan_done, b * STEPS + k + 1)
                if n % GRP == 0:
                    dve.wait_ge(c_loaded[n // GRP], b * 16 + 16)
                if not (isinstance(b, int) and b == 0 and k < RING_G):
                    dve.wait_ge(ymm_done, b * STEPS + k - RING_G + 1)
                v.tensor_tensor(gs[:, k % RING_G, :], HS[k % RING_H][:], Cs[:, n, :], ALU.mult).then_inc(g_ready, 1)

            def take_y(b, i, q):
                dve.wait_ge(ymm_done, i * NS + NS)
                v.scalar_tensor_tensor(m_y[:, q % 2, :], m_u[:, q % 2, :], c_d[:, q:q + 1], Y[:], ALU.mult, ALU.add).then_inc(y_taken, 1)
                dve.wait_ge(y_taken, i + 1)
                dve.wait_ge(s_loaded[q % 2], b * 32 + (q // 2) * 16 + 16)
                v.tensor_tensor(m_y[:, q % 2, :], m_y[:, q % 2, :], m_sz[:, q % 2, :], ALU.mult).then_inc(gated_done, 1)

            def gated(b, i, q):
                par = q % 2
                dve.wait_ge(yT_ready, i + 1)
                dve.wait_ge(x_loaded[par], b * 32 + (q // 2) * 16 + 16)
                v.tensor_tensor(m_x[:, par], m_x[:, par], TP[:].rearrange("p (t j) -> p t j", t=TB), ALU.add).then_inc(x1_ready, 1)

            def stats(j, jb):
                at = j[1]
                dve.wait_ge(xt_loaded[at], jb * 16 + 16)
                v.bn_stats(f_st[:, at, :], xt[:, at, :]).then_inc(tstat_done, 1)
                dve.wait_ge(tstat_done, j[0] * 2 + 1)
                held(dve)
                v.bn_aggr(f_mv[:, at, :], f_st[:, at, :]).then_inc(tstat_done, 1)
                dve.wait_ge(tstat_done, j[0] * 2 + 2)
                v.tensor_scalar(f_ve[:, at:at + 1], f_mv[:, at, 1:2], EPS, None, ALU.add).then_inc(var_ready, 1)

            def norm(j):
                at = j[1]
                dve.wait_ge(rstd_ready, j[0] + 1)
                v.scalar_tensor_tensor(f_nm[:, at:at + 1], f_mv[:, at, 0:1], -1.0, f_rs[:, at:at + 1], ALU.mult, ALU.mult).then_inc(norm_ready, 1)

            def lg_copy(f):
                dve.wait_ge(lg_ready, f[0] + 1)
                v.tensor_copy(logits[:, bass.ds(f[0], 1), :].rearrange("p a e -> p (a e)"), TP[:, 0:NE]).then_inc(lg_copied, 1)

            def hidden(f, c):
                dve.wait_ge(sg_ready, 1 + 2 * f[0] + c + 1)
                dve.wait_ge(up_ready, 2 * f[0] + c + 1)
                dve.wait_ge(hT_ready, 1 + 2 * f[0])
                v.tensor_tensor(f_h[:, c, :], f_sg[:, c, :], U[:, 0:I], ALU.mult).then_inc(h_ready, 1)

            def add_shared(f, c):
                dve.wait_ge(down_ready, 1 + 2 * f[0] + c + 1)
                dve.wait_ge(down_added, 1 + 2 * f[0] + c)
                row = xt[:, (f[1] + 3) % 4, :]
                v.tensor_tensor(row, row, YO[:], ALU.add).then_inc(down_added, 1)

            def slot(b, q, rows):
                i = b * DT + q
                later = not (isinstance(b, int) and b == 0 and q == 0)
                j = ((b - 1) * DT + q, q)
                for n in range(NS):
                    scan(b, q, n)
                    if n:
                        times_c(b, q, n - 1)
                    if n == 2 and later:
                        take_y(*((b, i - 1, q - 1) if q else (b - 1, i - 1, DT - 1)))
                    if n == 7 and later:
                        gated(*((b, i - 1, q - 1) if q else (b - 1, i - 1, DT - 1)))
                    if rows:
                        if n == 3:
                            lg_copy(j)
                        if n == 6:
                            hidden(j, 0)
                        if n == 10:
                            hidden(j, 1)
                        if n == 11:
                            stats(j, b - 1)
                        if n == 12:
                            add_shared(j, 0)
                        if n == 14:
                            norm(j)
                times_c(b, q, NS - 1)
                if rows:
                    add_shared(j, 1)

            for q in range(DT):
                slot(0, q, False)
            with dve.Fori(1, B) as b:
                for q in range(DT):
                    slot(b, q, True)
            take_y(B - 1, B * DT - 1, DT - 1)
            gated(B - 1, B * DT - 1, DT - 1)

            def whole(f):
                for c in range(2):
                    hidden(f, c)
                    add_shared(f, c)

            first = NT - TB
            for q in range(TB - 1):
                stats((first + q, q), B - 1)
                norm((first + q, q))
            for q in range(TB - 1):
                lg_copy((first + q, q))
            whole((first, 0))
            stats((NT - 1, TB - 1), B - 1)
            norm((NT - 1, TB - 1))
            lg_copy((NT - 1, TB - 1))
            lg_copy((NT, 0))

            done = [0]

            def link(ins):
                done[0] += 1
                ins.then_inc(route_step, 1)
                dve.wait_ge(route_step, done[0])

            dve.wait_ge(lg_copied, 1 + NT + 1)
            lg = logits[:, 1:NT + 1, :]
            by_tile = [P, NT, NE]
            link(v.reduce_max(r_mx[:], lg, AX.X))
            v.tensor_tensor(r_e[:], lg, r_mx[:].unsqueeze(2).to_broadcast(by_tile), ALU.subtract).then_inc(rt_max, 1)
            dve.wait_ge(rt_exp, 1)
            link(v.reduce_sum(r_sum[:], r_e[:], AX.X))
            link(v.reciprocal(r_inv[:], r_sum[:]))
            link(v.tensor_tensor(r_s[:], r_e[:], r_inv[:].unsqueeze(2).to_broadcast(by_tile), ALU.mult))
            for t in range(NT):
                last = v.max(r_top[:, t, :], r_s[:, t, :])
            link(last)
            for t in range(NT):
                last = v.max_index(r_ix[:, t, :], r_top[:, t, :], r_s[:, t, :])
            link(last)
            link(v.tensor_copy(r_ixf[:], r_ix[:, :, 0:K]))
            for c in range(K):
                v.tensor_copy(r_w[:, c, :], r_top[:, :, c])
                last = v.tensor_tensor(r_m[:, c], iota_row[:, 0:NE].unsqueeze(1).to_broadcast(by_tile),
                                       r_ixf[:, :, c:c + 1].to_broadcast(by_tile), ALU.is_equal)
            link(last)
            v.tensor_tensor(r_ms[:], r_m[:, 0], r_m[:, 1], ALU.add).then_inc(rt_mask, 1)
            whole((first + 1, 1))
            dve.wait_ge(rt_rank, 2)
            v.memset(r_res[:], 1.0)
            link(v.tensor_copy(r_tot[:], TOT[:, 0:NT * NE].rearrange("p (t e) -> p e t", e=NE)))
            link(v.memset(r_res[:, :, 0:1], 0.0))
            flat_ = lambda a: a[:, :, :].rearrange("p e t -> p (e t)")
            link(v.tensor_tensor_scan(flat_(r_inc), flat_(r_res), flat_(r_tot), 0.0, ALU.mult, ALU.add))
            link(v.tensor_scalar(r_nt[:], iota_row[:, 0:NT], float(P), None, ALU.mult))
            link(v.tensor_tensor(r_cmp[:], r_inc[:, :, NT - 1:NT].to_broadcast([P, NE, NT]),
                                 r_nt[:].unsqueeze(1).to_broadcast([P, NE, NT]), ALU.is_gt))
            link(v.reduce_sum(r_nt[:], r_cmp[:], AX.X))
            link(v.tensor_tensor_scan(r_end[:], ones[:, 0:NE], r_nt[:], 0.0, ALU.mult, ALU.add))
            v.tensor_tensor(r_te, iota_row[:, 0:UNITS].unsqueeze(2).to_broadcast([P, UNITS, NE]),
                            r_end[:].unsqueeze(1).to_broadcast([P, UNITS, NE]), ALU.is_ge)
            link(v.tensor_tensor(r_base[:], r_end[:], r_nt[:], ALU.subtract))
            link(v.tensor_scalar(r_base[:], r_base[:], float(P), None, ALU.mult))
            v.reduce_sum(t_exp[:, 0:UNITS], r_te, AX.X)
            link(v.tensor_tensor(r_inc[:], r_inc[:], r_tot[:], ALU.subtract))
            link(v.tensor_tensor(r_inc[:], r_inc[:], r_base[:].unsqueeze(2).to_broadcast([P, NE, NT]), ALU.add))
            link(v.tensor_scalar(t_expi[:, 0:UNITS], t_exp[:, 0:UNITS], float(NE - 1), None, ALU.min))
            link(v.tensor_tensor(r_pos[:], RANK[:, 0:NT * NE].rearrange("p (t e) -> p t e", e=NE),
                                 r_inc[:, :, :].rearrange("p e t -> p t e"), ALU.add))
            for c in range(K):
                last = v.tensor_tensor(r_mp[:, c], r_m[:, c], r_pos[:], ALU.mult)
            link(last)
            link(v.reduce_sum(r_p[:], r_mp[:], AX.X))
            link(v.tensor_copy(r_pi[:], r_p[:]))
            v.tensor_single_scalar(r_qi[:], r_pi[:], 7, ALU.logical_shift_right)
            link(v.tensor_single_scalar(r_ri[:], r_pi[:], P - 1, ALU.bitwise_and))
            v.tensor_copy(r_q[:], r_qi[:])
            link(v.tensor_copy(r_r[:], r_ri[:]))
            link(v.tensor_scalar(r_tok[:, 0, :], iota_row[:, 0:NT], float(P), float(P), ALU.mult, ALU.add))
            link(v.tensor_scalar(r_tok[:, 1, :], r_tok[:, 0, :], part[:], None, ALU.add))
            link(v.tensor_copy(r_tok[:, 0, :], r_tok[:, 1, :]))
            link(v.tensor_tensor(r_tok[:], r_tok[:], r_r[:], ALU.subtract))
            cs = K * NT
            col = lambda a: a[:, :, :].rearrange("p c t -> p (c t)").unsqueeze(2)
            link(v.tensor_tensor(r_ohq, iota_row[:, 0:UNITS].unsqueeze(1).to_broadcast([P, cs, UNITS]),
                                 col(r_q).to_broadcast([P, cs, UNITS]), ALU.is_equal))
            v.tensor_tensor(r_rhs[:, :, 0, :], r_ohq, col(r_tok).to_broadcast([P, cs, UNITS]), ALU.mult)
            link(v.tensor_tensor(r_rhs[:, :, 1, :], r_ohq, col(r_w).to_broadcast([P, cs, UNITS]), ALU.mult))
            for c in range(0, cs, 8):
                v.tensor_tensor(r_ohr[:, c:c + 8, :], iota_row[:].unsqueeze(1).to_broadcast([P, 8, P]),
                                col(r_r)[:, c:c + 8, :].to_broadcast([P, 8, P]), ALU.is_equal).then_inc(rt_oh, 1)
            whole((first + 2, 2))
            dve.wait_ge(rt_table, 1)
            link(v.memset(t_tok[:, UNITS:UNITS + 1], 0))
            v.tensor_copy(t_w[:, 0:UNITS], TABLE[:, UNITS:2 * UNITS])
            link(v.tensor_scalar(t_tok[:, 0:UNITS], TABLE[:, 0:UNITS], part[:], None, ALU.add))
            for k in range(2):
                v.tensor_copy(e_gidx[:, k:k + 1], t_tok[:, k:k + 1]).then_inc(gidx_ready, 1)
            dve.wait_ge(gidx_ready, 2)
            link(v.tensor_copy(t_w[:, UNITS:UNITS + 1], part[:]))
            v.tensor_copy(e_w[:, 0:1], t_w[:, 0:1]).then_inc(tables_ready, 1)
            whole((first + 3, 3))
            whole((NT, 0))

            def hidden_of(k):
                dve.wait_ge(esg_ready, k + 1)
                dve.wait_ge(eu_ready, k + 1)
                dve.wait_ge(ehT_ready, k)
                v.tensor_tensor(e_h[:], e_sg[:], U[:, 0:I], ALU.mult).then_inc(eh_ready, 1)

            def weigh(k, par):
                if not (isinstance(k, int) and k == 0):
                    dve.wait_ge(scattered, k * 16)
                v.tensor_copy(e_sidx[:, par:par + 1], t_tok[:, bass.ds(k, 1)]).then_inc(sidx_ready, 1)
                v.tensor_copy(e_w[:, par:par + 1], t_w[:, bass.ds(k, 1)]).then_inc(idx_step, 1)
                dve.wait_ge(idx_step, k + 1)
                dve.wait_ge(ey_ready, k + 1)
                v.tensor_scalar(e_y[:, par, :], YO[:], e_w[:, par:par + 1], None, ALU.mult).then_inc(ey_taken, 1)

            hidden_of(0)

            def two_units(r):
                for half in range(2):
                    k = r * 2 + 1 + half
                    dve.wait_ge(gx_loaded[half], r * 16 + 16)
                    v.tensor_copy(e_gidx[:, half:half + 1], t_tok[:, bass.ds(k + 1, 1)]).then_inc(gidx_ready, 1)
                    hidden_of(k)
                    weigh(k - 1, half)

            two_units(0)
            with dve.Fori(1, UNITS // 2) as r:
                two_units(r)
            weigh(UNITS - 1, 0)


_INS = ["x", "ctxT", "inT", "convw", "convb", "xpT", "dtT", "dtb", "alog", "dskip", "gateT", "wgu", "wdn", "sgu", "sdn"]


def kernel(x, ctx_1024, L0_xattn_in_proj_w, L0_xattn_conv_w, L0_xattn_conv_b, L0_xattn_x_proj_w, L0_xattn_dt_proj_w,
           L0_xattn_dt_proj_b, L0_xattn_A_log, L0_xattn_D, L0_ffn_gate_w, L0_ffn_w_gate_up, L0_ffn_w_down,
           L0_ffn_shared_gate_up, L0_ffn_shared_down):
    import numpy as np
    import concourse.bacc as bacc
    from concourse.bass_utils import run_bass_kernel_spmd as run

    def by_channel(a):
        a = np.asarray(a)
        return a.reshape(DT, P, -1).transpose(1, 0, 2)

    data = {
        "x": np.asarray(x).reshape(T, H), "ctxT": np.asarray(ctx_1024).transpose(0, 2, 1),
        "inT": np.asarray(L0_xattn_in_proj_w).T, "convw": by_channel(L0_xattn_conv_w),
        "convb": by_channel(L0_xattn_conv_b)[:, :, 0], "xpT": np.asarray(L0_xattn_x_proj_w).T,
        "dtT": np.asarray(L0_xattn_dt_proj_w).T, "dtb": by_channel(L0_xattn_dt_proj_b)[:, :, 0],
        "alog": by_channel(L0_xattn_A_log), "dskip": by_channel(L0_xattn_D)[:, :, 0],
        "gateT": np.asarray(L0_ffn_gate_w).T, "wgu": np.asarray(L0_ffn_w_gate_up), "wdn": np.asarray(L0_ffn_w_down),
        "sgu": np.asarray(L0_ffn_shared_gate_up), "sdn": np.asarray(L0_ffn_shared_down),
    }
    nc = bacc.Bacc("TRN2", target_bir_lowering=False, num_devices=1)
    arrays, args = {}, []
    for name in _INS:
        arrays[f"in_{name}"] = np.ascontiguousarray(data[name])
        args.append(nc.dram_tensor(f"in_{name}", list(data[name].shape), F32, kind="ExternalInput").ap())
    out = nc.dram_tensor("out_rows", [T + P, H], F32, kind="ExternalOutput").ap()
    program(nc, *args, out)
    r = run(nc, [arrays], core_ids=[0])
    return r.results[0]["out_rows"][P:].reshape(B, L, H)
```

```python
import concourse.bass as bass
from concourse import mybir
from contextlib import ExitStack

F32 = mybir.dt.float32
I32 = mybir.dt.int32
U32 = mybir.dt.uint32
ALU = mybir.AluOpType
ACT = mybir.ActivationFunctionType
AX = mybir.AxisListType

P = 128
B, L = 4, 512
DM, H = 256, 512
DT, NE = H // P, 16
NS, RK = 16, 16
NX = RK + 2 * NS
I = 352
IT = [(0, 128), (128, 128), (256, 96)]
KH = H // P
T = B * L
NT = T // P
TB = L // P
K = 2
UNITS = T * K // P + NE - 1
EPS = 1e-5
THETA = 2.0 ** -6
GRP = 4
NG = NS // GRP
STEPS = DT * NS
RING_H, RING_G = 3, 8

PE_AT = (2, 3, 3, 3, 4, 4, 5, 6, 6, 7, 9, 10, 11, 13, 14, 15, 16)
Y_TURN_AT, XN_TURN_AT = 2, (15, 9)
GATE_AT, HT_AT, XN_AT, XNT_AT = 7, 13, (15, 12), (15, 14)
TAKE_AT, LOGITS_AT, GATED_AT, HIDDEN_AT, STATS_AT, NORM_AT = 2, 0, 6, (9, 12), (11, 5), (14, 7)


def program(nc, x, ctxT, inT, convw, convb, xpT, dtT, dtb, alog, dskip, gateT, wgu, wdn, sgu, sdn, out):
    bc_d = nc.dram_tensor("bc_scratch", [B, 2 * NS, L], F32, kind="Internal").ap()
    u_d = nc.dram_tensor("u_scratch", [B, P, DT, L], F32, kind="Internal").ap()
    dt_d = nc.dram_tensor("dt_scratch", [B, P, DT, L], F32, kind="Internal").ap()
    sz_d = nc.dram_tensor("silu_z_scratch", [T, H], F32, kind="Internal").ap()
    x1_d = nc.dram_tensor("x1_scratch", [T, H], F32, kind="Internal").ap()
    xn_d = nc.dram_tensor("xn_scratch", [T + P, H], F32, kind="Internal").ap()

    def batch_rows(t, b):
        return t[bass.ds(b * L, L), :].rearrange("(t p) h -> p t h", p=P)

    with ExitStack() as stack:
        def sb(name, shape, dt=F32):
            return stack.enter_context(nc.sbuf_tensor(name, shape, dt))

        def sem(name):
            return stack.enter_context(nc.semaphore(name))

        bank = [stack.enter_context(nc.psum_tensor(f"bank{i}", [P, 512], F32)) for i in range(8)]
        XIN, XDB, DTP = bank[0:2], bank[2], bank[4:8]
        HS, Y, G, U, YO, TP = bank[0:3], bank[3], bank[4], bank[5], bank[6], bank[7]
        RANK, TOT, TABLE = bank[0], bank[1], bank[2]
        TX, TH = bank[3], bank[7]
        GU = (G, U)

        ident = sb("ident", [P, P])
        ones = sb("ones", [P, P])
        upper = sb("upper", [P, P])
        iota_row = sb("iota_row", [P, P])
        part = sb("part", [P, 1])
        zrow = sb("zrow", [P, H])
        c_conv = sb("c_conv", [P, DT, 4])
        c_convb = sb("c_convb", [P, DT])
        c_dtb = sb("c_dtb", [P, DT])
        c_alog = sb("c_alog", [P, DT, NS])
        c_a = sb("c_a", [P, DT, NS])
        c_d = sb("c_d", [P, DT])
        c_gate = sb("c_gate", [P, KH, NE])
        ws_gu = sb("ws_gu", [P, KH, 4 * I])
        ws_dn = sb("ws_dn", [P, 2, 3, H])
        logits = sb("logits", [P, NT + 1, NE])

        halves = sb("halves", [P, TB])
        pre = ExitStack()

        def psb(name, shape, dt=F32):
            return pre.enter_context(nc.sbuf_tensor(name, shape, dt))

        p_ctx = psb("p_ctx", [P, 2, L])
        p_in = psb("p_in", [P, 2, H])
        p_xp = psb("p_xp", [P, DT, NX])
        p_dtw = psb("p_dtw", [RK, H])
        p_acc = psb("p_acc", [P, DT, L])
        p_u = psb("p_u", [P, DT, L])
        p_xd = psb("p_xd", [NX, L])
        p_abs = psb("p_abs", [P, 2, L])
        p_e = psb("p_e", [P, DT, L])
        p_relu = psb("p_relu", [P, DT, L])
        p_ln = psb("p_ln", [P, DT, L])
        p_ser = psb("p_ser", [P, DT, L])
        p_mask = psb("p_mask", [P, DT, L], I32)
        p_dt = psb("p_dt", [P, DT, L])
        p_x = psb("p_x", [P, TB, H])
        p_sz = psb("p_sz", [P, TB, H])
        p_st = psb("p_st", [P, TB, 6])
        p_mv = psb("p_mv", [P, TB, 2])
        p_ve = psb("p_ve", [P, TB])
        p_rs = psb("p_rs", [P, TB])
        p_nm = psb("p_nm", [P, TB])
        pre.close()

        bcs = sb("bcs", [P, 2, NS, L])
        Bs, Cs = bcs[:, 0], bcs[:, 1]
        dbu = sb("dbu", [P, NS, L])
        gs = sb("gs", [P, RING_G, L])
        xt = sb("xt", [P, TB, H])
        f_st = sb("f_st", [P, TB, 6])
        f_mv = sb("f_mv", [P, TB, 2])
        f_ve = sb("f_ve", [P, TB])
        f_rs = sb("f_rs", [P, TB])
        f_nm = sb("f_nm", [P, TB])
        f_xn = sb("f_xn", [P, 2, H])
        f_xnT = sb("f_xnT", [P, TB, H])
        f_sg = sb("f_sg", [P, 2, I])
        f_h = sb("f_h", [P, 2, I])
        f_hT = sb("f_hT", [P, 2, 3, P])

        slots = ExitStack()

        def msb(name, shape, dt=F32):
            return slots.enter_context(nc.sbuf_tensor(name, shape, dt))

        m_u = msb("m_u", [P, 2, L])
        m_dt = msb("m_dt", [P, 2, L])
        m_w = msb("m_w", [P, 2, L])
        m_x = msb("m_x", [P, 2, TB, P])
        m_sz = msb("m_sz", [P, 2, L])
        m_y = msb("m_y", [P, 2, L])
        slots.close()

        r_mx = sb("r_mx", [P, NT])
        r_e = sb("r_e", [P, NT, NE])
        r_sum = sb("r_sum", [P, NT])
        r_inv = sb("r_inv", [P, NT])
        r_s = sb("r_s", [P, NT, NE])
        r_top = sb("r_top", [P, NT, 8])
        r_ix = sb("r_ix", [P, NT, 8], U32)
        r_ixf = sb("r_ixf", [P, NT, K])
        r_m = sb("r_m", [P, K, NT, NE])
        r_ms = sb("r_ms", [P, NT, NE])
        r_tot = sb("r_tot", [P, NE, NT])
        r_res = sb("r_res", [P, NE, NT])
        r_inc = sb("r_inc", [P, NE, NT])
        r_cmp = sb("r_cmp", [P, NE, NT])
        r_nt = sb("r_nt", [P, NE])
        r_end = sb("r_end", [P, NE])
        r_base = sb("r_base", [P, NE])
        r_pos = sb("r_pos", [P, NT, NE])
        r_mp = sb("r_mp", [P, K, NT, NE])
        r_p = sb("r_p", [P, K, NT])
        r_pi = sb("r_pi", [P, K, NT], I32)
        r_qi = sb("r_qi", [P, K, NT], I32)
        r_ri = sb("r_ri", [P, K, NT], I32)
        r_q = sb("r_q", [P, K, NT])
        r_r = sb("r_r", [P, K, NT])
        r_tok = sb("r_tok", [P, K, NT])
        r_w = sb("r_w", [P, K, NT])
        t_exp = sb("t_exp", [P, UNITS + 1])
        t_expi = sb("t_expi", [P, UNITS + 1], I32)
        t_end = sb("t_end", [P, NE], I32)
        t_tok = sb("t_tok", [P, UNITS + 2], I32)
        t_w = sb("t_w", [P, UNITS + 1])
        flat = dbu[:, :, :].rearrange("p n l -> p (n l)")
        r_ohr = flat[:, 0:K * NT * P].rearrange("p (c j) -> p c j", j=P)
        o = K * NT * P
        r_rhs = flat[:, o:o + K * NT * 2 * UNITS].rearrange("p (c v u) -> p c v u", v=2, u=UNITS)
        r_ohq = gs[:, :, :].rearrange("p n l -> p (n l)")[:, 0:K * NT * UNITS].rearrange("p (c u) -> p c u", u=UNITS)
        o += K * NT * 2 * UNITS
        r_te = flat[:, o:o + UNITS * NE].rearrange("p (u e) -> p u e", e=NE)

        wide = bcs[:, :, :, :].rearrange("p a n l -> p (a n l)")
        e_gu = wide[:, 0:5632].rearrange("p (r t n) -> p r t n", r=2, t=KH)
        e_dn = wide[:, 5632:8704].rearrange("p (r t n) -> p r t n", r=2, t=3)
        e_gidx = sb("e_gidx", [P, 2], I32)
        e_sidx = sb("e_sidx", [P, 2], I32)
        e_w = sb("e_w", [P, 2])
        e_x = wide[:, 8704:9728].rearrange("p (a n) -> p a n", a=2)
        e_xT = wide[:, 9728:10752].rearrange("p (a n) -> p a n", a=2)
        e_sg = sb("e_sg", [P, I])
        e_h = sb("e_h", [P, I])
        e_hT = sb("e_hT", [P, 3, P])
        e_y = wide[:, 10752:11776].rearrange("p (a n) -> p a n", a=2)

        names = """const_loaded weights_loaded ctx_loaded z_loaded consts_made tables_made
            xin_ready acc_ready conv_done u_ready u_stored xd_ready xd_copied bc_stored
            dtp_ready dtp_free abs_done e_ready ln_ready ser_ready dt_ready dt_stored
            z_var z_rstd z_norm sz_ready sz_stored a_exp a_ready pool_step tap_done zstat_done soft_done dummy_ready
            u0_loaded u1_loaded d0_loaded d1_loaded x0_loaded x1_loaded s0_loaded s1_loaded
            b0_loaded b1_loaded b2_loaded b3_loaded c0_loaded c1_loaded c2_loaded c3_loaded
            w_ready dbu_ready exp_done scan_done g_ready ymm_done y_taken yT_ready x1_ready x1_stored
            xt0_loaded xt1_loaded xt2_loaded xt3_loaded var_ready rstd_ready norm_ready xn_ready xn0_stored xn1_stored xnT_ready xnT_copied lg_ready lg_copied
            gate_ready up_ready sg_ready h_ready hT_ready hT_copied down_ready down_added out_stored
            row_zeroed trash_stored rt_max rt_exp rt_mask rt_rank rt_oh rt_table tables_ready
            gu_loaded gu_here dn_loaded dn_here gidx_ready sidx_ready
            gx0_loaded gx1_loaded ex_ready exT_copied eg_ready eu_ready esg_ready eh_ready ehT_ready ehT_copied
            ey_ready ey_taken scattered gated_done tstat_done route_step idx_step waits_passed""".split()
        s = {n: sem(n) for n in names}
        (const_loaded, weights_loaded, ctx_loaded, z_loaded, consts_made, tables_made,
         xin_ready, acc_ready, conv_done, u_ready, u_stored, xd_ready, xd_copied, bc_stored,
         dtp_ready, dtp_free, abs_done, e_ready, ln_ready, ser_ready, dt_ready, dt_stored,
         z_var, z_rstd, z_norm, sz_ready, sz_stored, a_exp, a_ready, pool_step, tap_done, zstat_done, soft_done,
         dummy_ready) = [s[n] for n in names[:34]]
        u_loaded = [s["u0_loaded"], s["u1_loaded"]]
        d_loaded = [s["d0_loaded"], s["d1_loaded"]]
        x_loaded = [s["x0_loaded"], s["x1_loaded"]]
        s_loaded = [s["s0_loaded"], s["s1_loaded"]]
        b_loaded = [s[f"b{q}_loaded"] for q in range(NG)]
        c_loaded = [s[f"c{q}_loaded"] for q in range(NG)]
        at = names.index("w_ready")
        (w_ready, dbu_ready, exp_done, scan_done, g_ready, ymm_done, y_taken, yT_ready, x1_ready, x1_stored,
         xt0_loaded, xt1_loaded, xt2_loaded, xt3_loaded, var_ready, rstd_ready, norm_ready, xn_ready, xn0_stored, xn1_stored, xnT_ready, xnT_copied, lg_ready,
         lg_copied, gate_ready, up_ready, sg_ready, h_ready, hT_ready, hT_copied, down_ready, down_added,
         out_stored, row_zeroed, trash_stored, rt_max, rt_exp, rt_mask, rt_rank, rt_oh, rt_table,
         tables_ready) = [s[n] for n in names[at:at + 42]]
        xt_loaded = [xt0_loaded, xt1_loaded, xt2_loaded, xt3_loaded]
        xn_stored = [xn0_stored, xn1_stored]
        gu_loaded, gu_here, dn_loaded, dn_here = s["gu_loaded"], s["gu_here"], s["dn_loaded"], s["dn_here"]
        gx_loaded = [s["gx0_loaded"], s["gx1_loaded"]]
        (gidx_ready, sidx_ready) = s["gidx_ready"], s["sidx_ready"]
        at = names.index("ex_ready")
        (ex_ready, exT_copied, eg_ready, eu_ready, esg_ready, eh_ready, ehT_ready, ehT_copied,
         ey_ready, ey_taken, scattered, gated_done, tstat_done, route_step, idx_step, waits_passed) = [s[n] for n in names[at:at + 16]]
        block = stack.enter_context(nc.Block())

        def held(eng):
            eng.sem_inc(waits_passed)

        def from_one(eng, count):
            eng.sem_inc(count, 1)

        def pre_finished(eng):
            for stored in (u_stored, bc_stored, dt_stored, sz_stored):
                eng.wait_ge(stored, 1 + 16 * B)

        @block.sync
        def _(sp):
            for count in (u_stored, sz_stored, bc_stored, dt_stored, out_stored, xn0_stored, xn1_stored):
                from_one(sp, count)
            for dst, src in ((p_in[:], inT.rearrange("(t p) n -> p t n", p=P)), (c_conv[:], convw), (c_convb[:], convb),
                             (p_xp[:], xpT.rearrange("(t p) n -> p t n", p=P)), (p_dtw[:], dtT), (c_dtb[:], dtb),
                             (c_alog[:], alog), (c_d[:], dskip), (c_gate[:], gateT.rearrange("(t p) n -> p t n", p=P))):
                sp.dma_start(dst, src).then_inc(const_loaded, 16)
            def load_ctx(b):
                sp.dma_start(p_ctx[:], ctxT[bass.ds(b, 1)].rearrange("a (t p) l -> p (a t) l", p=P)).then_inc(ctx_loaded, 16)

            def load_x(b):
                sp.dma_start(p_x[:], batch_rows(x, b)).then_inc(z_loaded, 16)

            def dt_store(b):
                sp.wait_ge(dt_ready, 1 + b * DT + DT)
                sp.dma_start(dt_d[bass.ds(b, 1)].rearrange("a p t l -> p (a t) l"), p_dt[:]).then_inc(dt_stored, 16)

            def step(b, last=False):
                if not last:
                    sp.wait_ge(xin_ready, 1 + b * DT + DT)
                    load_ctx(b + 1)
                sp.wait_ge(u_ready, b * DT + DT)
                sp.dma_start(u_d[bass.ds(b, 1)].rearrange("a p t l -> p (a t) l"), p_u[:]).then_inc(u_stored, 16)
                sp.wait_ge(sz_ready, 1 + b * TB + TB)
                if not last:
                    load_x(b + 1)
                sp.dma_start(batch_rows(sz_d, b), p_sz[:]).then_inc(sz_stored, 16)
                sp.wait_ge(xd_copied, 1 + b + 1)
                sp.dma_start(bc_d[bass.ds(b, 1)].rearrange("a n l -> (a n) l"), p_xd[RK:NX, :]).then_inc(bc_stored, 16)

            load_ctx(0)
            load_x(0)
            step(0)
            with sp.Fori(1, B - 1) as b:
                step(b)
                dt_store(b - 1)
            step(B - 1, last=True)
            dt_store(B - 2)
            dt_store(B - 1)

            sp.dma_start(ws_gu[:], sgu.rearrange("(t p) n -> p t n", p=P)).then_inc(weights_loaded, 16)
            for c in range(2):
                for t, (r, n) in enumerate(IT):
                    sp.dma_start(ws_dn[0:n, c, t, :], sdn[c * I + r:c * I + r + n, :]).then_inc(weights_loaded, 16)

            def load_dtu(b, q):
                par = q % 2
                sp.dma_start(m_dt[:, par, :], dt_d[bass.ds(b, 1), :, q, :].rearrange("a p l -> p (a l)")).then_inc(d_loaded[par], 16)
                sp.dma_start(m_u[:, par, :], u_d[bass.ds(b, 1), :, q, :].rearrange("a p l -> p (a l)")).then_inc(u_loaded[par], 16)

            def load_xsz(b, q):
                par = q % 2
                sp.dma_start(m_x[:, par], batch_rows(x, b)[:, :, q * P:(q + 1) * P]).then_inc(x_loaded[par], 16)
                sp.dma_start(m_sz[:, par], sz_d[bass.ds(b * L + q * P, P), :]).then_inc(s_loaded[par], 16)

            def load_bc(b, g, which):
                dst, row, done = ((Bs, 0, b_loaded), (Cs, NS, c_loaded))[which]
                src = bc_d[bass.ds(b, 1), row + g * GRP:row + (g + 1) * GRP, :].rearrange("a n l -> a (n l)")
                sp.dma_start(dst[:, g * GRP:(g + 1) * GRP, :].rearrange("p n l -> p (n l)"),
                             src.to_broadcast([P, GRP * L])).then_inc(done[g], 16)

            pre_finished(sp)
            load_dtu(0, 0)
            load_xsz(0, 0)
            for g in range(NG):
                load_bc(0, g, 0)
                load_bc(0, g, 1)
            load_dtu(0, 1)
            load_xsz(0, 1)

            def x1_store(b, q, i):
                sp.wait_ge(x1_ready, i + 1)
                held(sp)
                sp.dma_start(batch_rows(x1_d, b)[:, :, q * P:(q + 1) * P], m_x[:, q % 2]).then_inc(x1_stored, 16)

            def xt_load(j, jb):
                sp.wait_ge(x1_stored, jb * 16 * DT + 16 * DT)
                sp.dma_start(xt[:, j[1], :], x1_d[bass.ds(j[0] * P, P), :]).then_inc(xt_loaded[j[1]], 16)

            def xn_store(j):
                sp.wait_ge(xn_ready, j[0] + 1)
                sp.dma_start(xn_d[bass.ds(j[0] * P + P, P), :], f_xn[:, j[1] % 2, :]).then_inc(xn_stored[j[1] % 2], 16)

            def out_store(f):
                sp.wait_ge(down_added, 1 + f[0] + 1)
                sp.dma_start(out[bass.ds(f[0] * P, P), :], xt[:, (f[1] + 3) % 4, :]).then_inc(out_stored, 16)

            def slot(b, q, rows, last=False):
                i = b * DT + q
                later = not (isinstance(b, int) and b == 0 and q == 0)
                more = later and not (last and q == DT - 1)
                nb, nq = (b, q + 1) if q < DT - 1 else (b + 1, 0)
                new_bc = q == DT - 1 and not last
                j = ((b - 1) * DT + q, q)
                if rows and q:
                    sp.wait_ge(out_stored, 1 + (j[0] - 1) * 16)
                    xt_load(j, b - 1)
                if more:
                    sp.wait_ge(y_taken, i)
                    held(sp)
                    load_dtu(nb, nq)
                if new_bc:
                    for g in range(NG):
                        sp.wait_ge(dbu_ready, i * NG + g + 1)
                        load_bc(b + 1, g, 0)
                if later:
                    x1_store(*((b, q - 1) if q else (b - 1, DT - 1)), i - 1)
                if more:
                    sp.wait_ge(x1_stored, i * 16)
                    held(sp)
                    load_xsz(nb, nq)
                if rows and q == 0:
                    sp.wait_ge(out_stored, 1 + j[0] * 16)
                    xt_load(j, b - 1)
                if new_bc:
                    for g in range(NG):
                        sp.wait_ge(g_ready, i * NS + g * GRP + GRP)
                        load_bc(b + 1, g, 1)
                        if rows and g == 2:
                            xn_store(j)
                elif rows:
                    xn_store(j)
                if rows:
                    out_store(j)

            for q in range(DT):
                slot(0, q, False)
            with sp.Fori(1, B - 1) as b:
                for q in range(DT):
                    slot(b, q, True)
            for q in range(DT):
                slot(B - 1, q, True, last=True)

            def load_gu(e, par):
                sp.dma_start(e_gu[:, par], wgu[bass.ds(e, 1)].rearrange("a (t p) n -> p (a t) n", p=P)).then_inc(gu_loaded, 16)

            def load_dn(e, par):
                sp.dma_start(e_dn[:, par, 0:2, :], wdn[bass.ds(e, 1), 0:2 * P, :].rearrange("a (t p) n -> p (a t) n", p=P)).then_inc(dn_loaded, 16)
                sp.dma_start(e_dn[0:IT[2][1], par, 2, :], wdn[bass.ds(e, 1), 2 * P:I, :].rearrange("a p n -> (a p) n")).then_inc(dn_loaded, 16)

            x1_store(B - 1, DT - 1, B * DT - 1)
            first = NT - TB
            for q in range(TB - 1):
                sp.wait_ge(out_stored, 1 + (first + q - 2) * 16)
                xt_load((first + q, q), B - 1)
            for q in range(TB - 1):
                xn_store((first + q, q))
            out_store((first, 0))
            sp.wait_ge(out_stored, 1 + (first + 1) * 16)
            xt_load((NT - 1, TB - 1), B - 1)
            xn_store((NT - 1, TB - 1))
            sp.wait_ge(g_ready, B * STEPS)
            load_gu(0, 0)
            load_dn(0, 0)
            for f in range(first + 1, NT + 1):
                out_store((f, f % TB))

            def landed(e):
                sp.wait_ge(gu_loaded, e * 16 + 16)
                sp.sem_inc(gu_here, 1)
                sp.wait_ge(dn_loaded, e * 32 + 32)
                sp.sem_inc(dn_here, 1)

            landed(0)
            load_gu(1, 1)
            load_dn(1, 1)
            sp.wait_ge(tables_ready, 1)
            with sp.Fori(1, NE // 2) as r:
                for par in range(2):
                    e = r * 2 + par
                    landed(e - 1)
                    end = sp.value_load(t_end[0:1, bass.ds(e - 2, 1)], min_val=0, max_val=UNITS)
                    sp.wait_ge(eu_ready, 1 + end)
                    load_gu(e, par)
                    sp.wait_ge(ey_ready, 1 + end)
                    load_dn(e, par)
            landed(NE - 1)
            sp.wait_ge(scattered, 16 * UNITS)
            sp.wait_ge(out_stored, 1 + 16 * (NT + 1))
            sp.wait_ge(trash_stored, 16)

        @block.tensor
        def _(pe):
            mm = nc.tensor.matmul
            for count in (xin_ready, xnT_ready, hT_ready, down_ready, eu_ready, ey_ready):
                from_one(pe, count)
            pe.wait_ge(const_loaded, 16 * 9)
            pe.wait_ge(consts_made, 5)

            def project(b):
                pe.wait_ge(ctx_loaded, b * 16 + 16)
                for q in range(DT):
                    pe.wait_ge(conv_done, b * DT + q + 1)
                    for t in range(2):
                        last = mm(XIN[q % 2][:], p_in[:, t, q * P:(q + 1) * P], p_ctx[:, t, :], start=t == 0, stop=t == 1)
                    last.then_inc(xin_ready, 1)
                pe.wait_ge(xd_copied, 1 + b)
                for q in range(DT):
                    pe.wait_ge(u_ready, b * DT + q + 1)
                    last = mm(XDB[0:NX, :], p_xp[:, q, :], p_u[:, q, :], start=q == 0, stop=q == DT - 1)
                last.then_inc(xd_ready, 1)
                pe.wait_ge(xd_copied, 1 + b + 1)
                for q in range(DT):
                    if not isinstance(b, int):
                        pe.wait_ge(dtp_free, (b - 1) * DT + q + 1)
                    mm(DTP[q][:], p_dtw[:, q * P:(q + 1) * P], p_xd[0:RK, :], start=True, stop=True).then_inc(dtp_ready, 1)

            project(0)
            with pe.Fori(1, B) as b:
                project(b)
            pre_finished(pe)
            pe.wait_ge(weights_loaded, 16 * 7)
            pe.wait_ge(dummy_ready, 1)

            def y_sum(b, q, n):
                i, k = b * DT + q, q * NS + n
                if n == 0:
                    pe.wait_ge(y_taken, i)
                pe.wait_ge(g_ready, i * NS + n + 1)
                mm(Y[:], ident[:], gs[:, k % RING_G, :], start=n == 0, stop=n == NS - 1).then_inc(ymm_done, 1)

            def y_turn(i, par, copied):
                pe.wait_ge(gated_done, i + 1)
                pe.wait_ge(x1_ready, i)
                pe.wait_ge(lg_copied, 1 + copied)
                for t in range(TB):
                    last = nc.tensor.transpose(TP[:, t * P:(t + 1) * P], m_y[:, par, t * P:(t + 1) * P], ident[:])
                last.then_inc(yT_ready, 1)

            def xn_turn(j, x1_count):
                pe.wait_ge(xn_ready, j[0] + 1)
                pe.wait_ge(x1_ready, x1_count)
                pe.wait_ge(lg_copied, 1 + j[0])
                for t in range(KH):
                    last = nc.tensor.transpose(TP[:, t * P:(t + 1) * P], f_xn[:, j[1] % 2, t * P:(t + 1) * P], ident[:])
                last.then_inc(xnT_ready, 1)

            def router(f, copied):
                pe.wait_ge(xnT_copied, 1 + copied)
                pe.wait_ge(lg_copied, 1 + f[0])
                for t in range(KH):
                    last = mm(TP[:, 0:NE], f_xnT[:, (f[1] + 3) % 4, t * P:(t + 1) * P], c_gate[:, t, :], start=t == 0, stop=t == KH - 1)
                last.then_inc(lg_ready, 1)

            def shared(f):
                at = (f[1] + 3) % 4
                lhs = [f_xnT[:, at, t * P:(t + 1) * P] for t in range(KH)]

                def rows_in(c, half):
                    dst, off, done = GU[c], half * 2 * I + c * I, (gate_ready, up_ready)[half]

                    def piece(ts):
                        if ts[0] == 0 and half == 0:
                            pe.wait_ge(hT_copied, 1 + 2 * f[0])
                            pe.wait_ge(xnT_copied, 1 + f[0])
                        elif ts[0] == 0:
                            pe.wait_ge(sg_ready, 2 * f[0] + c + 1)
                        for t in ts:
                            last = mm(dst[:, 0:I], lhs[t], ws_gu[:, t, off:off + I], start=t == 0, stop=t == KH - 1)
                        if ts[-1] == KH - 1:
                            last.then_inc(done, 1)
                    return [lambda: piece([0, 1]), lambda: piece([2, 3])]

                def turn(c):
                    pe.wait_ge(h_ready, 1 + 2 * f[0] + c + 1)
                    for t, (r, n) in enumerate(IT):
                        last = nc.tensor.transpose(GU[c][0:n, t * P:(t + 1) * P], f_h[:, c, r:r + n], ident[:])
                    last.then_inc(hT_ready, 1)

                def down(c, t):
                    if t == 0:
                        pe.wait_ge(hT_copied, 1 + 2 * f[0] + c + 1)
                    if t == 0 and c == 0:
                        pe.wait_ge(down_added, 1 + f[0])
                    n = IT[t][1]
                    last = mm(YO[:], f_hT[0:n, c, t, :], ws_dn[0:n, c, t, :], start=c == 0 and t == 0, stop=c == 1 and t == 2)
                    if c == 1 and t == 2:
                        last.then_inc(down_ready, 1)

                return (rows_in(0, 0) + rows_in(1, 0) + rows_in(0, 1) + rows_in(1, 1) + [lambda: turn(0), lambda: turn(1)]
                        + [lambda c=c, t=t: down(c, t) for c in range(2) for t in range(3)])

            def slot(b, q, rows):
                i = b * DT + q
                if rows:
                    f = ((b - 1) * DT + q, q)
                    pieces = shared(f)
                    router(f, f[0])
                    for piece in pieces[0:PE_AT[0]]:
                        piece()
                for n in range(NS):
                    y_sum(b, q, n)
                    if n == Y_TURN_AT and not (isinstance(b, int) and b == 0 and q == 0):
                        y_turn(i - 1, (q - 1) % 2, f[0] + 1 if rows else 0)
                    if rows:
                        for piece in pieces[PE_AT[n]:PE_AT[n + 1]]:
                            piece()
                        if n == XN_TURN_AT[q > 0]:
                            xn_turn(f, i)

            for q in range(DT):
                slot(0, q, False)
            with pe.Fori(1, B) as b:
                for q in range(DT):
                    slot(b, q, True)
            pe.wait_ge(xnT_copied, 1 + NT - TB)
            y_turn(B * DT - 1, (DT - 1) % 2, NT - TB)

            def whole(f):
                for piece in shared(f):
                    piece()

            first = NT - TB
            for q in range(TB - 1):
                xn_turn((first + q, q), B * DT)
                router((first + q, q), first + q + 1)
            whole((first, 0))
            xn_turn((NT - 1, TB - 1), B * DT)
            router((NT - 1, TB - 1), NT)
            router((NT, 0), NT)
            whole((first + 1, 1))
            pe.wait_ge(rt_mask, 1)
            ms = r_ms[:, :, :].rearrange("p t e -> p (t e)")
            mm(RANK[:, 0:NT * NE], upper[:], ms, start=True, stop=True).then_inc(rt_rank, 1)
            mm(TOT[:, 0:NT * NE], ones[:], ms, start=True, stop=True).then_inc(rt_rank, 1)
            whole((first + 2, 2))
            for c in range(K * NT):
                if c % 8 == 0:
                    pe.wait_ge(rt_oh, c // 8 + 1)
                last = mm(TABLE[:, 0:2 * UNITS], r_ohr[:, c, :], r_rhs[:, c, :, :].rearrange("p v u -> p (v u)"),
                          start=c == 0, stop=c == K * NT - 1)
            last.then_inc(rt_table, 1)
            whole((first + 3, 3))
            whole((NT, 0))

            def x_turn(k, par, loads):
                pe.wait_ge(gx_loaded[par], loads)
                pe.wait_ge(exT_copied, k)
                for t in range(KH):
                    last = nc.tensor.transpose(TX[:, t * P:(t + 1) * P], e_x[:, par, t * P:(t + 1) * P], ident[:])
                last.then_inc(ex_ready, 1)

            def expert_of(k):
                e = pe.value_load(t_expi[0:1, bass.ds(k, 1)], min_val=0, max_val=NE - 1)
                return e, e % 2

            def up(k, par, e, ring):
                pe.wait_ge(exT_copied, k + 1)
                pe.wait_ge(gu_here, e + 1)
                for half, (dst, done, free) in enumerate(((G, eg_ready, esg_ready), (U, eu_ready, eh_ready))):
                    pe.wait_ge(free, k)
                    for t in range(KH):
                        w = e_gu[:, bass.ds(ring, 1), t, half * I:(half + 1) * I].rearrange("p a n -> p (a n)")
                        last = mm(dst[:, 0:I], e_xT[:, par, t * P:(t + 1) * P], w, start=t == 0, stop=t == KH - 1)
                    last.then_inc(done, 1)

            def h_turn(k):
                pe.wait_ge(eh_ready, k + 1)
                for t, (r, n) in enumerate(IT):
                    last = nc.tensor.transpose(TH[0:n, t * P:(t + 1) * P], e_h[:, r:r + n], ident[:])
                last.then_inc(ehT_ready, 1)

            def down(k, e, ring):
                pe.wait_ge(ehT_copied, k + 1)
                pe.wait_ge(dn_here, e + 1)
                pe.wait_ge(ey_taken, 1 + k)
                for t in range(3):
                    n = IT[t][1]
                    w = e_dn[0:n, bass.ds(ring, 1), t, :].rearrange("p a n -> p (a n)")
                    last = mm(YO[:], e_hT[0:n, t, :], w, start=t == 0, stop=t == 2)
                last.then_inc(ey_ready, 1)

            pe.wait_ge(hT_copied, 1 + 2 * (NT + 1))
            pe.wait_ge(h_ready, 1 + 2 * (NT + 1))
            pe.wait_ge(down_added, 1 + NT + 1)
            pe.wait_ge(tables_ready, 1)
            x_turn(0, 0, 16)
            up(0, 0, *expert_of(0))
            x_turn(1, 1, 16)
            h_turn(0)
            with pe.Fori(0, UNITS // 2) as r:
                for half in range(2):
                    par = 1 - half
                    k = r * 2 + 1 + half
                    before, now = expert_of(k - 1), expert_of(k)
                    up(k, par, *now)
                    x_turn(k + 1, 1 - par, (r + 1) * 16 + 16)
                    down(k - 1, *before)
                    h_turn(k)
            down(UNITS - 1, *expert_of(UNITS - 1))

        @block.scalar
        def _(act):
            f = nc.scalar.activation
            for count in (sz_ready, xd_copied, xnT_copied, hT_copied):
                from_one(act, count)
            act.wait_ge(const_loaded, 16 * 9)
            f(c_a[:], c_alog[:], ACT.Exp).then_inc(a_exp, 1)

            def conv_first(b, q):
                act.wait_ge(xin_ready, 1 + b * DT + q + 1)
                f(p_acc[:, q, :], XIN[q % 2][:], ACT.Identity, scale=c_conv[:, q, 3:4], bias=c_convb[:, q:q + 1]).then_inc(acc_ready, 1)

            def silus(b):
                act.wait_ge(u_stored, 1 + b * 16)
                for q in range(DT):
                    act.wait_ge(conv_done, b * DT + q + 3)
                    f(p_u[:, q, :], p_acc[:, q, :], ACT.Silu).then_inc(u_ready, 1)
                act.wait_ge(z_norm, b + 1)
                act.wait_ge(sz_stored, 1 + b * 16)
                for t in range(TB):
                    f(p_sz[:, t, :], p_x[:, t, :], ACT.Silu, scale=p_rs[:, t:t + 1], bias=p_nm[:, t:t + 1]).then_inc(sz_ready, 1)
                act.wait_ge(xd_ready, b + 1)
                act.wait_ge(bc_stored, 1 + b * 16)
                f(p_xd[:], XDB[0:NX, :], ACT.Copy).then_inc(xd_copied, 1)

            def exps(b, qs):
                act.wait_ge(dt_ready, 1 + b * DT)
                for q in qs:
                    act.wait_ge(dtp_ready, b * DT + q + 1)
                    f(p_abs[:, q % 2, :], DTP[q][:], ACT.Abs, bias=c_dtb[:, q:q + 1]).then_inc(abs_done, 1)
                    f(p_relu[:, q, :], DTP[q][:], ACT.Relu, bias=c_dtb[:, q:q + 1]).then_inc(dtp_free, 1)
                    act.wait_ge(abs_done, b * DT + q + 1)
                    f(p_e[:, q, :], p_abs[:, q % 2, :], ACT.Exp, scale=-1.0).then_inc(e_ready, 1)

            def logs(b):
                for q in range(DT):
                    act.wait_ge(e_ready, b * DT + q + 1)
                    f(p_ln[:, q, :], p_e[:, q, :], ACT.Ln, bias=1.0).then_inc(ln_ready, 1)

            for q in range(DT):
                conv_first(0, q)
            silus(0)
            with act.Fori(1, B) as b:
                for q in range(DT):
                    conv_first(b, q)
                    exps(b - 1, (q,))
                silus(b)
                logs(b - 1)
            exps(B - 1, range(DT))
            logs(B - 1)
            pre_finished(act)
            act.wait_ge(a_ready, 1)

            def decay(b, q, n):
                k = q * NS + n
                if k >= RING_H:
                    act.wait_ge(g_ready, b * STEPS + k - RING_H + 1)
                elif not (isinstance(b, int) and b == 0):
                    act.wait_ge(g_ready, b * STEPS - (0, 2, 1)[k])
                if n == 0:
                    act.wait_ge(d_loaded[q % 2], b * 32 + (q // 2) * 16 + 16)
                f(HS[k % RING_H][:], m_dt[:, q % 2, :], ACT.Exp, scale=c_a[:, q, n:n + 1]).then_inc(exp_done, 1)

            def gate(fx, c):
                act.wait_ge(gate_ready, 2 * fx[0] + c + 1)
                act.wait_ge(h_ready, 1 + 2 * fx[0])
                f(f_sg[:, c, :], GU[c][:, 0:I], ACT.Silu).then_inc(sg_ready, 1)

            def hT_copy(fx, c):
                act.wait_ge(hT_ready, 1 + 2 * fx[0] + c + 1)
                act.wait_ge(down_ready, 1 + fx[0])
                f(f_hT[:, c, 0:2, :], GU[c][:, 0:2 * P].rearrange("p (t j) -> p t j", t=2), ACT.Copy)
                f(f_hT[0:96, c, 2, :], GU[c][0:96, 2 * P:3 * P], ACT.Copy).then_inc(hT_copied, 1)

            def xn(j, stored):
                act.wait_ge(norm_ready, j[0] + 1)
                act.wait_ge(xn_stored[j[1] % 2], 1 + stored)
                act.wait_ge(xnT_ready, 1 + j[0])
                f(f_xn[:, j[1] % 2, :], xt[:, j[1], :], ACT.Identity, scale=f_rs[:, j[1]:j[1] + 1], bias=f_nm[:, j[1]:j[1] + 1]).then_inc(xn_ready, 1)

            def xnT_copy(j, past):
                act.wait_ge(xnT_ready, 1 + j[0] + 1)
                act.wait_ge(down_ready, 1 + past)
                f(f_xnT[:, j[1], :], TP[:], ACT.Copy).then_inc(xnT_copied, 1)

            def slot(b, q, rows):
                for n in range(NS):
                    decay(b, q, n)
                    if rows:
                        j = ((b - 1) * DT + q, q)
                        if n == GATE_AT:
                            gate(j, 0)
                            gate(j, 1)
                        if n == HT_AT:
                            hT_copy(j, 0)
                            hT_copy(j, 1)
                        if n == XN_AT[q > 0]:
                            xn(j, ((b - 1) * 2 + q // 2) * 16)
                        if n == XNT_AT[q > 0]:
                            xnT_copy(j, j[0])

            for q in range(DT):
                slot(0, q, False)
            with act.Fori(1, B) as b:
                for q in range(DT):
                    slot(b, q, True)

            def whole(fx):
                gate(fx, 0)
                gate(fx, 1)
                hT_copy(fx, 0)
                hT_copy(fx, 1)

            first = NT - TB
            for q in range(TB):
                if q == TB - 1:
                    whole((first, 0))
                xn((first + q, q), ((first + q) // 2) * 16)
                xnT_copy((first + q, q), first + q - 2)
            act.wait_ge(rt_max, 1)
            f(r_e[:], r_e[:], ACT.Exp).then_inc(rt_exp, 1)
            whole((first + 1, 1))
            whole((first + 2, 2))
            whole((first + 3, 3))
            whole((NT, 0))

            def x_copy(k, par, used):
                act.wait_ge(ex_ready, k + 1)
                act.wait_ge(eu_ready, 1 + used)
                f(e_xT[:, par, :], TX[:], ACT.Copy).then_inc(exT_copied, 1)

            def unit(k, par):
                act.wait_ge(eg_ready, k + 1)
                act.wait_ge(eh_ready, k)
                f(e_sg[:], G[:, 0:I], ACT.Silu).then_inc(esg_ready, 1)
                x_copy(k + 1, 1 - par, k)
                act.wait_ge(ehT_ready, k + 1)
                act.wait_ge(ey_ready, 1 + k)
                f(e_hT[:, 0:2, :], TH[:, 0:2 * P].rearrange("p (t j) -> p t j", t=2), ACT.Copy)
                f(e_hT[0:96, 2, :], TH[0:96, 2 * P:3 * P], ACT.Copy).then_inc(ehT_copied, 1)

            x_copy(0, 0, 0)
            unit(0, 0)
            with act.Fori(0, UNITS // 2) as r:
                for half in range(2):
                    unit(r * 2 + 1 + half, 1 - half)

        @block.gpsimd
        def _(pool):
            g = nc.gpsimd
            g.memset(ident[:], 0.0).then_inc(pool_step, 1)
            g.memset(ones[:], 1.0).then_inc(consts_made, 1)
            g.memset(halves[:], -0.5).then_inc(consts_made, 1)
            g.memset(upper[:], 1.0).then_inc(pool_step, 1)
            g.memset(zrow[:], 0.0).then_inc(row_zeroed, 1)
            pool.wait_ge(pool_step, 2)
            g.affine_select(out=ident[:], in_=ident[:], compare_op=ALU.not_equal, fill=1.0, base=0,
                            pattern=[[-1, P]], channel_multiplier=1).then_inc(consts_made, 1)
            g.affine_select(out=upper[:], in_=upper[:], compare_op=ALU.is_gt, fill=0.0, base=0,
                            pattern=[[1, P]], channel_multiplier=-1).then_inc(consts_made, 1)
            g.iota(iota_row[:], [[1, P]], base=0, channel_multiplier=0, allow_small_or_imprecise_dtypes=True).then_inc(consts_made, 1)
            g.iota(part[:], [[0, 1]], base=0, channel_multiplier=1, allow_small_or_imprecise_dtypes=True).then_inc(tables_made, 1)
            pool.wait_ge(row_zeroed, 1)
            pool.dma_start(xn_d[0:P, :], zrow[:]).then_inc(trash_stored, 16)
            pool.wait_ge(consts_made, 5)
            made = 2

            def z_power(b):
                pool.wait_ge(z_var, b + 1)
                g.tensor_tensor(p_rs[:], p_ve[:], halves[:], ALU.pow).then_inc(z_rstd, 1)

            def series(b):
                for q in range(DT):
                    pool.wait_ge(e_ready, b * DT + q + 1)
                    held(pool)
                    g.tensor_scalar(p_ser[:, q, :], p_e[:, q, :], 1.0 / 3.0, -0.5, ALU.mult, ALU.add).then_inc(pool_step, 1)
                    pool.wait_ge(pool_step, b * DT + made + q + 1)
                    g.tensor_tensor(p_ser[:, q, :], p_ser[:, q, :], p_e[:, q, :], ALU.mult).then_inc(ser_ready, 1)

            z_power(0)
            with pool.Fori(1, B) as b:
                series(b - 1)
                z_power(b)
            series(B - 1)
            pre_finished(pool)

            def slot(b, q, rows):
                i = b * DT + q
                pool.wait_ge(u_loaded[q % 2], b * 32 + (q // 2) * 16 + 16)
                pool.wait_ge(d_loaded[q % 2], b * 32 + (q // 2) * 16 + 16)
                g.tensor_tensor(m_w[:, q % 2, :], m_u[:, q % 2, :], m_dt[:, q % 2, :], ALU.mult).then_inc(w_ready, 1)
                pool.wait_ge(w_ready, i + 1)
                for gr in range(NG):
                    pool.wait_ge(b_loaded[gr], b * 16 + 16)
                    if not (isinstance(b, int) and i == 0):
                        pool.wait_ge(scan_done, (i - 1) * NS + gr * GRP + GRP)
                    part_ = dbu[:, gr * GRP:(gr + 1) * GRP, :]
                    w = m_w[:, q % 2:q % 2 + 1, :].to_broadcast([P, GRP, L])
                    g.tensor_tensor(part_, Bs[:, gr * GRP:(gr + 1) * GRP, :], w, ALU.mult).then_inc(dbu_ready, 1)
                if rows:
                    rstd(((b - 1) * DT + q, q))

            def rstd(j):
                pool.wait_ge(var_ready, j[0] + 1)
                g.tensor_tensor(f_rs[:, j[1]:j[1] + 1], f_ve[:, j[1]:j[1] + 1], halves[:, 0:1], ALU.pow).then_inc(rstd_ready, 1)

            for q in range(DT):
                slot(0, q, False)
            with pool.Fori(1, B) as b:
                for q in range(DT):
                    slot(b, q, True)
            for q in range(TB):
                rstd((NT - TB + q, q))

            pool.wait_ge(tables_ready, 1)
            for par in range(2):
                pool.wait_ge(xn_stored[par], 1 + 16 * (NT // 2))
            pool.wait_ge(trash_stored, 16)

            def gather(k, par):
                pool.wait_ge(gidx_ready, k + 1)
                held(pool)
                pool.indirect_dma_start(e_x[:, par, :], None, xn_d, bass.IndirectOffsetOnAxis(ap=e_gidx[:, par:par + 1], axis=0)).then_inc(gx_loaded[par], 16)

            def scatter(k, par):
                pool.wait_ge(ey_taken, 1 + k + 1)
                pool.wait_ge(sidx_ready, k + 1)
                if not (isinstance(k, int) and k == 0):
                    pool.wait_ge(scattered, k * 16)
                held(pool)
                pool.indirect_dma_start(out, bass.IndirectOffsetOnAxis(ap=e_sidx[:, par:par + 1], axis=0), e_y[:, par, :], None,
                                        compute_op=ALU.add).then_inc(scattered, 16)

            gather(0, 0)
            gather(1, 1)
            pool.wait_ge(ex_ready, 1)
            gather(2, 0)
            pool.wait_ge(out_stored, 1 + 16 * (NT + 1))

            def rows_of_two(r):
                for half in range(2):
                    k = r * 2 + half
                    pool.wait_ge(ex_ready, k + 2)
                    gather(k + 3, 1 - half)
                    scatter(k, half)

            rows_of_two(0)
            with pool.Fori(1, UNITS // 2) as r:
                rows_of_two(r)
            scatter(UNITS - 1, 0)
            pool.wait_ge(scattered, 16 * UNITS)

        @block.vector
        def _(dve):
            v = nc.vector
            for count in (dt_ready, h_ready, down_added, lg_copied, ey_taken):
                from_one(dve, count)
            dve.wait_ge(const_loaded, 16 * 9)
            dve.wait_ge(a_exp, 1)
            v.tensor_scalar(c_a[:], c_a[:], -1.0, None, ALU.mult).then_inc(a_ready, 1)
            dve.sem_inc(conv_done, 2)

            def z_stats(b):
                dve.wait_ge(z_loaded, b * 16 + 16)
                for t in range(TB):
                    last = v.bn_stats(p_st[:, t, :], p_x[:, t, :])
                last.then_inc(zstat_done, 1)
                dve.wait_ge(zstat_done, b * 2 + 1)
                dve.wait_ge(sz_ready, 1 + b * TB)
                held(dve)
                for t in range(TB):
                    last = v.bn_aggr(p_mv[:, t, :], p_st[:, t, :])
                last.then_inc(zstat_done, 1)
                dve.wait_ge(zstat_done, b * 2 + 2)
                v.tensor_scalar(p_ve[:], p_mv[:, :, 0:2][:, :, 1], EPS, None, ALU.add).then_inc(z_var, 1)

            def z_shift(b):
                dve.wait_ge(z_rstd, b + 1)
                v.scalar_tensor_tensor(p_nm[:], p_mv[:, :, 0], -1.0, p_rs[:], ALU.mult, ALU.mult).then_inc(z_norm, 1)

            def taps(b, q):
                dve.wait_ge(acc_ready, b * DT + q + 1)
                for back in range(1, 4):
                    if back > 1:
                        dve.wait_ge(tap_done, (b * DT + q) * 2 + back - 1)
                    a = p_acc[:, q, back:L]
                    ins = v.scalar_tensor_tensor(a, XIN[q % 2][:, 0:L - back], c_conv[:, q, 3 - back:4 - back], a, ALU.mult, ALU.add)
                    ins.then_inc(tap_done if back < 3 else conv_done, 1)

            def small(b, q):
                dve.wait_ge(ser_ready, b * DT + q + 1)
                v.tensor_scalar(p_mask[:, q, :], p_e[:, q, :], THETA, None, ALU.is_ge)
                v.scalar_tensor_tensor(p_ser[:, q, :], p_ser[:, q, :], 1.0, p_e[:, q, :], ALU.add, ALU.mult).then_inc(soft_done, 1)

            def large(b):
                dve.wait_ge(dt_stored, 1 + b * 16)
                for q in range(DT):
                    dve.wait_ge(soft_done, b * 2 * DT + DT)
                    dve.wait_ge(ln_ready, b * DT + q + 1)
                    held(dve)
                    v.copy_predicated(p_ser[:, q, :], p_mask[:, q, :], p_ln[:, q, :]).then_inc(soft_done, 1)
                    if q:
                        total(b, q - 1)
                total(b, DT - 1)

            def total(b, q):
                dve.wait_ge(soft_done, b * 2 * DT + DT + q + 1)
                v.tensor_tensor(p_dt[:, q, :], p_ser[:, q, :], p_relu[:, q, :], ALU.add).then_inc(dt_ready, 1)

            for q in range(DT):
                taps(0, q)
            z_stats(0)
            z_shift(0)
            with dve.Fori(1, B) as b:
                for q in range(DT):
                    taps(b, q)
                    if q == 1:
                        small(b - 1, 0)
                z_stats(b)
                for q in range(1, DT):
                    small(b - 1, q)
                    if q == 1:
                        z_shift(b)
                large(b - 1)
            for q in range(DT):
                small(B - 1, q)
            large(B - 1)
            pre_finished(dve)
            v.memset(xt[:, TB - 1, :], 0.0)
            v.memset(f_xnT[:, TB - 1, :], 0.0).then_inc(dummy_ready, 1)

            def scan(b, q, n):
                k = q * NS + n
                if n % GRP == 0:
                    dve.wait_ge(dbu_ready, (b * DT + q) * NG + n // GRP + 1)
                dve.wait_ge(exp_done, b * STEPS + k + 1)
                h = HS[k % RING_H][:]
                v.tensor_tensor_scan(h, h, dbu[:, n, :], 0.0, ALU.mult, ALU.add).then_inc(scan_done, 1)

            def times_c(b, q, n):
                k = q * NS + n
                dve.wait_ge(scan_done, b * STEPS + k + 1)
                if n % GRP == 0:
                    dve.wait_ge(c_loaded[n // GRP], b * 16 + 16)
                if not (isinstance(b, int) and b == 0 and k < RING_G):
                    dve.wait_ge(ymm_done, b * STEPS + k - RING_G + 1)
                v.tensor_tensor(gs[:, k % RING_G, :], HS[k % RING_H][:], Cs[:, n, :], ALU.mult).then_inc(g_ready, 1)

            def take_y(b, i, q):
                dve.wait_ge(ymm_done, i * NS + NS)
                v.scalar_tensor_tensor(m_y[:, q % 2, :], m_u[:, q % 2, :], c_d[:, q:q + 1], Y[:], ALU.mult, ALU.add).then_inc(y_taken, 1)
                dve.wait_ge(y_taken, i + 1)
                dve.wait_ge(s_loaded[q % 2], b * 32 + (q // 2) * 16 + 16)
                v.tensor_tensor(m_y[:, q % 2, :], m_y[:, q % 2, :], m_sz[:, q % 2, :], ALU.mult).then_inc(gated_done, 1)

            def gated(b, i, q):
                par = q % 2
                dve.wait_ge(yT_ready, i + 1)
                dve.wait_ge(x_loaded[par], b * 32 + (q // 2) * 16 + 16)
                v.tensor_tensor(m_x[:, par], m_x[:, par], TP[:].rearrange("p (t j) -> p t j", t=TB), ALU.add).then_inc(x1_ready, 1)

            def stats(j, jb):
                at = j[1]
                dve.wait_ge(xt_loaded[at], jb * 16 + 16)
                v.bn_stats(f_st[:, at, :], xt[:, at, :]).then_inc(tstat_done, 1)
                dve.wait_ge(tstat_done, j[0] * 2 + 1)
                held(dve)
                v.bn_aggr(f_mv[:, at, :], f_st[:, at, :]).then_inc(tstat_done, 1)
                dve.wait_ge(tstat_done, j[0] * 2 + 2)
                v.tensor_scalar(f_ve[:, at:at + 1], f_mv[:, at, 1:2], EPS, None, ALU.add).then_inc(var_ready, 1)

            def norm(j):
                at = j[1]
                dve.wait_ge(rstd_ready, j[0] + 1)
                v.scalar_tensor_tensor(f_nm[:, at:at + 1], f_mv[:, at, 0:1], -1.0, f_rs[:, at:at + 1], ALU.mult, ALU.mult).then_inc(norm_ready, 1)

            def lg_copy(f):
                dve.wait_ge(lg_ready, f[0] + 1)
                v.tensor_copy(logits[:, bass.ds(f[0], 1), :].rearrange("p a e -> p (a e)"), TP[:, 0:NE]).then_inc(lg_copied, 1)

            def hidden(f, c):
                dve.wait_ge(sg_ready, 2 * f[0] + c + 1)
                dve.wait_ge(up_ready, 2 * f[0] + c + 1)
                dve.wait_ge(hT_ready, 1 + 2 * f[0])
                v.tensor_tensor(f_h[:, c, :], f_sg[:, c, :], GU[c][:, 0:I], ALU.mult).then_inc(h_ready, 1)

            def add_shared(f):
                dve.wait_ge(down_ready, 1 + f[0] + 1)
                row = xt[:, (f[1] + 3) % 4, :]
                v.tensor_tensor(row, row, YO[:], ALU.add).then_inc(down_added, 1)

            def slot(b, q, rows):
                i = b * DT + q
                later = not (isinstance(b, int) and b == 0 and q == 0)
                j = ((b - 1) * DT + q, q)
                for n in range(NS):
                    scan(b, q, n)
                    if n:
                        times_c(b, q, n - 1)
                    if n == TAKE_AT and later:
                        take_y(*((b, i - 1, q - 1) if q else (b - 1, i - 1, DT - 1)))
                    if n == GATED_AT and later:
                        gated(*((b, i - 1, q - 1) if q else (b - 1, i - 1, DT - 1)))
                    if rows:
                        if n == LOGITS_AT:
                            lg_copy(j)
                        for c in range(2):
                            if n == HIDDEN_AT[c]:
                                hidden(j, c)
                        if n == STATS_AT[q > 0]:
                            stats(j, b - 1)
                        if n == NORM_AT[q > 0]:
                            norm(j)
                times_c(b, q, NS - 1)
                if rows:
                    add_shared(j)

            for q in range(DT):
                slot(0, q, False)
            with dve.Fori(1, B) as b:
                for q in range(DT):
                    slot(b, q, True)
            take_y(B - 1, B * DT - 1, DT - 1)
            gated(B - 1, B * DT - 1, DT - 1)

            def whole(f):
                for c in range(2):
                    hidden(f, c)
                add_shared(f)

            first = NT - TB
            for q in range(TB - 1):
                stats((first + q, q), B - 1)
                norm((first + q, q))
            for q in range(TB - 1):
                lg_copy((first + q, q))
            whole((first, 0))
            stats((NT - 1, TB - 1), B - 1)
            norm((NT - 1, TB - 1))
            lg_copy((NT - 1, TB - 1))
            lg_copy((NT, 0))

            done = [0]

            def link(ins):
                done[0] += 1
                ins.then_inc(route_step, 1)
                dve.wait_ge(route_step, done[0])

            dve.wait_ge(lg_copied, 1 + NT + 1)
            lg = logits[:, 1:NT + 1, :]
            by_tile = [P, NT, NE]
            link(v.reduce_max(r_mx[:], lg, AX.X))
            v.tensor_tensor(r_e[:], lg, r_mx[:].unsqueeze(2).to_broadcast(by_tile), ALU.subtract).then_inc(rt_max, 1)
            dve.wait_ge(rt_exp, 1)
            link(v.reduce_sum(r_sum[:], r_e[:], AX.X))
            link(v.reciprocal(r_inv[:], r_sum[:]))
            link(v.tensor_tensor(r_s[:], r_e[:], r_inv[:].unsqueeze(2).to_broadcast(by_tile), ALU.mult))
            for t in range(NT):
                last = v.max(r_top[:, t, :], r_s[:, t, :])
            link(last)
            for t in range(NT):
                last = v.max_index(r_ix[:, t, :], r_top[:, t, :], r_s[:, t, :])
            link(last)
            link(v.tensor_copy(r_ixf[:], r_ix[:, :, 0:K]))
            for c in range(K):
                v.tensor_copy(r_w[:, c, :], r_top[:, :, c])
                last = v.tensor_tensor(r_m[:, c], iota_row[:, 0:NE].unsqueeze(1).to_broadcast(by_tile),
                                       r_ixf[:, :, c:c + 1].to_broadcast(by_tile), ALU.is_equal)
            link(last)
            v.tensor_tensor(r_ms[:], r_m[:, 0], r_m[:, 1], ALU.add).then_inc(rt_mask, 1)
            whole((first + 1, 1))
            dve.wait_ge(rt_rank, 2)
            v.memset(r_res[:], 1.0)
            link(v.tensor_copy(r_tot[:], TOT[:, 0:NT * NE].rearrange("p (t e) -> p e t", e=NE)))
            link(v.memset(r_res[:, :, 0:1], 0.0))
            flat_ = lambda a: a[:, :, :].rearrange("p e t -> p (e t)")
            link(v.tensor_tensor_scan(flat_(r_inc), flat_(r_res), flat_(r_tot), 0.0, ALU.mult, ALU.add))
            link(v.tensor_scalar(r_nt[:], iota_row[:, 0:NT], float(P), None, ALU.mult))
            link(v.tensor_tensor(r_cmp[:], r_inc[:, :, NT - 1:NT].to_broadcast([P, NE, NT]),
                                 r_nt[:].unsqueeze(1).to_broadcast([P, NE, NT]), ALU.is_gt))
            link(v.reduce_sum(r_nt[:], r_cmp[:], AX.X))
            link(v.tensor_tensor_scan(r_end[:], ones[:, 0:NE], r_nt[:], 0.0, ALU.mult, ALU.add))
            v.tensor_tensor(r_te, iota_row[:, 0:UNITS].unsqueeze(2).to_broadcast([P, UNITS, NE]),
                            r_end[:].unsqueeze(1).to_broadcast([P, UNITS, NE]), ALU.is_ge)
            link(v.tensor_tensor(r_base[:], r_end[:], r_nt[:], ALU.subtract))
            link(v.tensor_scalar(r_base[:], r_base[:], float(P), None, ALU.mult))
            v.reduce_sum(t_exp[:, 0:UNITS], r_te, AX.X)
            link(v.tensor_tensor(r_inc[:], r_inc[:], r_tot[:], ALU.subtract))
            link(v.tensor_tensor(r_inc[:], r_inc[:], r_base[:].unsqueeze(2).to_broadcast([P, NE, NT]), ALU.add))
            v.tensor_copy(t_end[:], r_end[:])
            link(v.tensor_scalar(t_expi[:, 0:UNITS], t_exp[:, 0:UNITS], float(NE - 1), None, ALU.min))
            link(v.tensor_tensor(r_pos[:], RANK[:, 0:NT * NE].rearrange("p (t e) -> p t e", e=NE),
                                 r_inc[:, :, :].rearrange("p e t -> p t e"), ALU.add))
            for c in range(K):
                last = v.tensor_tensor(r_mp[:, c], r_m[:, c], r_pos[:], ALU.mult)
            link(last)
            link(v.reduce_sum(r_p[:], r_mp[:], AX.X))
            link(v.tensor_copy(r_pi[:], r_p[:]))
            v.tensor_single_scalar(r_qi[:], r_pi[:], 7, ALU.logical_shift_right)
            link(v.tensor_single_scalar(r_ri[:], r_pi[:], P - 1, ALU.bitwise_and))
            v.tensor_copy(r_q[:], r_qi[:])
            link(v.tensor_copy(r_r[:], r_ri[:]))
            link(v.tensor_scalar(r_tok[:, 0, :], iota_row[:, 0:NT], float(P), float(P), ALU.mult, ALU.add))
            link(v.tensor_scalar(r_tok[:, 1, :], r_tok[:, 0, :], part[:], None, ALU.add))
            link(v.tensor_copy(r_tok[:, 0, :], r_tok[:, 1, :]))
            link(v.tensor_tensor(r_tok[:], r_tok[:], r_r[:], ALU.subtract))
            cs = K * NT
            col = lambda a: a[:, :, :].rearrange("p c t -> p (c t)").unsqueeze(2)
            link(v.tensor_tensor(r_ohq, iota_row[:, 0:UNITS].unsqueeze(1).to_broadcast([P, cs, UNITS]),
                                 col(r_q).to_broadcast([P, cs, UNITS]), ALU.is_equal))
            v.tensor_tensor(r_rhs[:, :, 0, :], r_ohq, col(r_tok).to_broadcast([P, cs, UNITS]), ALU.mult)
            link(v.tensor_tensor(r_rhs[:, :, 1, :], r_ohq, col(r_w).to_broadcast([P, cs, UNITS]), ALU.mult))
            for c in range(0, cs, 8):
                v.tensor_tensor(r_ohr[:, c:c + 8, :], iota_row[:].unsqueeze(1).to_broadcast([P, 8, P]),
                                col(r_r)[:, c:c + 8, :].to_broadcast([P, 8, P]), ALU.is_equal).then_inc(rt_oh, 1)
            whole((first + 2, 2))
            dve.wait_ge(rt_table, 1)
            link(v.memset(t_tok[:, UNITS:UNITS + 2], 0))
            v.tensor_copy(t_w[:, 0:UNITS], TABLE[:, UNITS:2 * UNITS])
            link(v.tensor_scalar(t_tok[:, 0:UNITS], TABLE[:, 0:UNITS], part[:], None, ALU.add))
            for k in range(2):
                v.tensor_copy(e_gidx[:, k:k + 1], t_tok[:, k:k + 1]).then_inc(gidx_ready, 1)
            dve.wait_ge(gidx_ready, 2)
            link(v.tensor_copy(t_w[:, UNITS:UNITS + 1], part[:]))
            v.tensor_copy(e_w[:, 0:1], t_w[:, 0:1]).then_inc(tables_ready, 1)
            whole((first + 3, 3))
            whole((NT, 0))

            def hidden_of(k):
                dve.wait_ge(esg_ready, k + 1)
                dve.wait_ge(eu_ready, 1 + k + 1)
                dve.wait_ge(ehT_ready, k)
                v.tensor_tensor(e_h[:], e_sg[:], U[:, 0:I], ALU.mult).then_inc(eh_ready, 1)

            def weigh(k, par):
                if not (isinstance(k, int) and k == 0):
                    dve.wait_ge(scattered, k * 16)
                v.tensor_copy(e_sidx[:, par:par + 1], t_tok[:, bass.ds(k, 1)]).then_inc(sidx_ready, 1)
                v.tensor_copy(e_w[:, par:par + 1], t_w[:, bass.ds(k, 1)]).then_inc(idx_step, 1)
                dve.wait_ge(idx_step, k + 1)
                dve.wait_ge(ey_ready, 1 + k + 1)
                v.tensor_scalar(e_y[:, par, :], YO[:], e_w[:, par:par + 1], None, ALU.mult).then_inc(ey_taken, 1)

            def rows_wanted(k, par, loads):
                dve.wait_ge(gx_loaded[par], loads)
                v.tensor_copy(e_gidx[:, par:par + 1], t_tok[:, bass.ds(k, 1)]).then_inc(gidx_ready, 1)

            hidden_of(0)
            rows_wanted(2, 0, 16)

            def two_units(r):
                for half in range(2):
                    k = r * 2 + 1 + half
                    hidden_of(k)
                    rows_wanted(k + 2, 1 - half, (r + half) * 16 + 16)
                    weigh(k - 1, half)

            two_units(0)
            with dve.Fori(1, UNITS // 2) as r:
                two_units(r)
            weigh(UNITS - 1, 0)


_INS = ["x", "ctxT", "inT", "convw", "convb", "xpT", "dtT", "dtb", "alog", "dskip", "gateT", "wgu", "wdn", "sgu", "sdn"]


def kernel(x, ctx_1024, L0_xattn_in_proj_w, L0_xattn_conv_w, L0_xattn_conv_b, L0_xattn_x_proj_w, L0_xattn_dt_proj_w,
           L0_xattn_dt_proj_b, L0_xattn_A_log, L0_xattn_D, L0_ffn_gate_w, L0_ffn_w_gate_up, L0_ffn_w_down,
           L0_ffn_shared_gate_up, L0_ffn_shared_down):
    import numpy as np
    import concourse.bacc as bacc
    from concourse.bass_utils import run_bass_kernel_spmd as run

    def by_channel(a):
        a = np.asarray(a)
        return a.reshape(DT, P, -1).transpose(1, 0, 2)

    data = {
        "x": np.asarray(x).reshape(T, H), "ctxT": np.asarray(ctx_1024).transpose(0, 2, 1),
        "inT": np.asarray(L0_xattn_in_proj_w).T, "convw": by_channel(L0_xattn_conv_w),
        "convb": by_channel(L0_xattn_conv_b)[:, :, 0], "xpT": np.asarray(L0_xattn_x_proj_w).T,
        "dtT": np.asarray(L0_xattn_dt_proj_w).T, "dtb": by_channel(L0_xattn_dt_proj_b)[:, :, 0],
        "alog": by_channel(L0_xattn_A_log), "dskip": by_channel(L0_xattn_D)[:, :, 0],
        "gateT": np.asarray(L0_ffn_gate_w).T, "wgu": np.asarray(L0_ffn_w_gate_up), "wdn": np.asarray(L0_ffn_w_down),
        "sgu": np.asarray(L0_ffn_shared_gate_up), "sdn": np.asarray(L0_ffn_shared_down),
    }
    nc = bacc.Bacc("TRN2", target_bir_lowering=False, num_devices=1)
    arrays, args = {}, []
    for name in _INS:
        arrays[f"in_{name}"] = np.ascontiguousarray(data[name])
        args.append(nc.dram_tensor(f"in_{name}", list(data[name].shape), F32, kind="ExternalInput").ap())
    out = nc.dram_tensor("out_rows", [T + P, H], F32, kind="ExternalOutput").ap()
    program(nc, *args, out)
    r = run(nc, [arrays], core_ids=[0])
    return r.results[0]["out_rows"][P:].reshape(B, L, H)
```

```python
import concourse.bass as bass
from concourse import mybir
from contextlib import ExitStack

F32 = mybir.dt.float32
I32 = mybir.dt.int32
U32 = mybir.dt.uint32
F32R = mybir.dt.float32r
ALU = mybir.AluOpType
ACT = mybir.ActivationFunctionType
AX = mybir.AxisListType

P = 128
B, L = 4, 512
DM, H = 256, 512
DT, NE = H // P, 16
NS, RK = 16, 16
NX = RK + 2 * NS
I = 352
IT = [(0, 128), (128, 128), (256, 96)]
KH = H // P
T = B * L
NT = T // P
TB = L // P
K = 2
UNITS = T * K // P + NE - 1
SPARE = 2 * P
EPS = 1e-5
THETA = 2.0 ** -6
GRP = 4
NG = NS // GRP
STEPS = DT * NS
RING_H, RING_G = 4, 8
PAIRED = (0, 1, 2, 3)
RSTD_AFTER = 2
BEYOND = 2624

SPLIT = 10
PE_AT = (0, 1, 2, 4, 4, 4, 4, 5, 5, 5, 6, 8, 8, 8, 8, 9, 10)
LATE_AT = (0, 0, 0, 0, 0, 2, 3, 4, 4, 4, 6, 6, 6, 6, 6, 6, 6)
Y_TURN_AT, XN_TURN_AT = 0, (14, 10)
GATE_AT, HT_AT, XN_AT, XNT_AT = 9, 4, (15, 11), (15, 15)
TAKE_AT, LOGITS_AT, GATED_AT, HIDDEN_AT, STATS_AT, NORM_AT, ADD_AT = 2, 2, 6, (12, 15), (14, 2), (14, 6), 13


def paired(i):
    return not isinstance(i, int) or i >= DT - 1


def first_of_pair(i, n):
    return paired(i) and n % GRP == GRP - 2 and n // GRP in PAIRED


def sums_before(i, n):
    full = DT - 1
    slots = i * NS if not paired(i) else full * NS + (i - full) * (NS - len(PAIRED))
    return slots + n - sum(first_of_pair(i, m) for m in range(n))


def program(nc, x, ctxT, inT, convw, convb, xpT, dtT, dtb, alog, dskip, gateT, wgu, wdn, sgu, sdn, out):
    bc_d = nc.dram_tensor("bc_scratch", [B, 2 * NS, L], F32, kind="Internal").ap()
    u_d = nc.dram_tensor("u_scratch", [B, P, DT, L], F32, kind="Internal").ap()
    dt_d = nc.dram_tensor("dt_scratch", [B, P, DT, L], F32, kind="Internal").ap()
    sz_d = nc.dram_tensor("silu_z_scratch", [T, H], F32, kind="Internal").ap()
    x1_d = nc.dram_tensor("x1_scratch", [T, H], F32, kind="Internal").ap()
    xn_d = nc.dram_tensor("xn_scratch", [T + SPARE, H], F32, kind="Internal").ap()

    def batch_rows(t, b):
        return t[bass.ds(b * L, L), :].rearrange("(t p) h -> p t h", p=P)

    with ExitStack() as stack:
        def sb(name, shape, dt=F32):
            return stack.enter_context(nc.sbuf_tensor(name, shape, dt))

        def sem(name):
            return stack.enter_context(nc.semaphore(name))

        bank = [stack.enter_context(nc.psum_tensor(f"bank{i}", [P, 512], F32)) for i in range(8)]
        XIN, XDB, DTP = bank[0:2], bank[2], bank[4:8]
        Y, GU, YO, TP = (bank[3], bank[0]), (bank[4:6], bank[1:3]), bank[6], bank[7]
        G, U = GU[0]
        RANK, TOT, TABLE = bank[0], bank[3], bank[7]
        TX, TH = bank[3], bank[7]

        ident = sb("ident", [P, P])
        ones = sb("ones", [P, P])
        upper = sb("upper", [P, P])
        iota_row = sb("iota_row", [P, P])
        part = sb("part", [P, 1])
        zero = sb("zero", [P, 1])
        c_conv = sb("c_conv", [P, DT, 4])
        c_convb = sb("c_convb", [P, DT])
        c_dtb = sb("c_dtb", [P, DT])
        c_alog = sb("c_alog", [P, DT, NS])
        c_a = sb("c_a", [P, DT, NS])
        c_d = sb("c_d", [P, DT])
        c_gate = sb("c_gate", [P, KH, NE])
        ws_gu = sb("ws_gu", [P, KH, 4 * I])
        ws_dn = sb("ws_dn", [P, 2, 3, H])
        logits = sb("logits", [P, NT + 1, NE])

        halves = sb("halves", [P, TB])
        pre = ExitStack()

        def psb(name, shape, dt=F32):
            return pre.enter_context(nc.sbuf_tensor(name, shape, dt))

        p_ctx = psb("p_ctx", [P, 2, L])
        p_in = psb("p_in", [P, 2, H])
        p_xp = psb("p_xp", [P, DT, NX])
        p_dtw = psb("p_dtw", [RK, H])
        p_acc = psb("p_acc", [P, DT, L])
        p_u = psb("p_u", [P, DT, L])
        p_xd = psb("p_xd", [NX, L])
        p_abs = psb("p_abs", [P, 2, L])
        p_e = psb("p_e", [P, DT, L])
        p_relu = psb("p_relu", [P, DT, L])
        p_ln = psb("p_ln", [P, DT, L])
        p_ser = psb("p_ser", [P, DT, L])
        p_mask = psb("p_mask", [P, DT, L], I32)
        p_dt = psb("p_dt", [P, DT, L])
        p_x = psb("p_x", [P, TB, H])
        p_sz = psb("p_sz", [P, TB, H])
        p_st = psb("p_st", [P, TB, 6])
        p_mv = psb("p_mv", [P, TB, 2])
        p_ve = psb("p_ve", [P, TB])
        p_rs = psb("p_rs", [P, TB])
        p_nm = psb("p_nm", [P, TB])
        pre.close()

        scan = ExitStack()
        dbu = scan.enter_context(nc.sbuf_tensor("dbu", [P, NS, L], F32))
        gs = scan.enter_context(nc.sbuf_tensor("gs", [P, RING_G, L], F32))
        scan.close()
        e_dn_hi = sb("e_dn_hi", [P, 2, 3, H], F32R)
        e_dn_lo = sb("e_dn_lo", [P, 2, 3, H], F32R)
        e_xT_hi = sb("e_xT_hi", [P, 2, H], F32R)
        e_xT_lo = sb("e_xT_lo", [P, 2, H], F32R)
        e_x = sb("e_x", [P, 2, H])
        e_y = sb("e_y", [P, 2, H])
        e_xT = sb("e_xT", [P, H])
        e_hT = sb("e_hT", [P, 3, P])
        e_u = sb("e_u", [P, I])
        sb("e_end", [P, (NS + RING_G) * L - 4 * 3 * H - 9 * H - 3 * P - I])
        xt = sb("xt", [P, TB, H])
        f_st = sb("f_st", [P, TB, 6])
        f_mv = sb("f_mv", [P, TB, 2])
        f_ve = sb("f_ve", [P, TB])
        f_rs = sb("f_rs", [P, TB])
        f_nm = sb("f_nm", [P, TB])
        f_xn = sb("f_xn", [P, 2, H])
        f_xnT = sb("f_xnT", [P, TB, H])
        f_sg = sb("f_sg", [P, 2, I])
        f_h = sb("f_h", [P, 2, I])
        f_hT = sb("f_hT", [P, 2, 3, P])

        slots = ExitStack()

        def msb(name, shape, dt=F32):
            return slots.enter_context(nc.sbuf_tensor(name, shape, dt))

        m_u = msb("m_u", [P, 2, L])
        m_dt = msb("m_dt", [P, 2, L])
        m_w = msb("m_w", [P, 1, L])
        m_x = msb("m_x", [P, 2, TB, P])
        m_sz = msb("m_sz", [P, 2, L])
        m_y = msb("m_y", [P, L])
        hs = msb("hs", [P, RING_H, L])
        slots.close()

        r_mx = sb("r_mx", [P, NT])
        r_e = sb("r_e", [P, NT, NE])
        r_sum = sb("r_sum", [P, NT])
        r_inv = sb("r_inv", [P, NT])
        r_s = sb("r_s", [P, NT, NE])
        r_top = sb("r_top", [P, NT, 8])
        r_ix = sb("r_ix", [P, NT, 8], U32)
        r_ixf = sb("r_ixf", [P, NT, K])
        r_m = sb("r_m", [P, K, NT, NE])
        r_ms = sb("r_ms", [P, NT, NE])
        r_tot = sb("r_tot", [P, NE, NT])
        r_res = sb("r_res", [P, NE, NT])
        r_inc = sb("r_inc", [P, NE, NT])
        r_cmp = sb("r_cmp", [P, NE, NT])
        r_nt = sb("r_nt", [P, NE])
        r_end = sb("r_end", [P, NE])
        r_base = sb("r_base", [P, NE])
        r_pos = sb("r_pos", [P, NT, NE])
        r_mp = sb("r_mp", [P, K, NT, NE])
        r_p = sb("r_p", [P, K, NT])
        r_pi = sb("r_pi", [P, K, NT], I32)
        r_qi = sb("r_qi", [P, K, NT], I32)
        r_ri = sb("r_ri", [P, K, NT], I32)
        r_q = sb("r_q", [P, K, NT])
        r_r = sb("r_r", [P, K, NT])
        r_tok = sb("r_tok", [P, K, NT])
        r_w = sb("r_w", [P, K, NT])
        t_exp = sb("t_exp", [P, UNITS + 1])
        t_expi = sb("t_expi", [P, UNITS + 1], I32)
        t_end = sb("t_end", [P, NE], I32)
        t_tok = sb("t_tok", [P, UNITS + 2], I32)
        t_w = sb("t_w", [P, UNITS + 1])
        e_gidx = sb("e_gidx", [P, 2], I32)
        e_sidx = sb("e_sidx", [P, 2], I32)
        e_w = sb("e_w", [P, 2])
        e_sg = sb("e_sg", [P, I])
        e_h = sb("e_h", [P, I])
        beyond = sb("beyond", [P, BEYOND])
        both = ExitStack()
        bcs = both.enter_context(nc.sbuf_tensor("bcs", [P, 2, NS, L], F32))
        Bs, Cs = bcs[:, 0], bcs[:, 1]
        both.close()
        flat = dbu[:, :, :].rearrange("p n l -> p (n l)")
        r_ohr = flat[:, 0:K * NT * P].rearrange("p (c j) -> p c j", j=P)
        o = K * NT * P
        r_rhs = flat[:, o:o + K * NT * 2 * UNITS].rearrange("p (c v u) -> p c v u", v=2, u=UNITS)
        r_ohq = gs[:, :, :].rearrange("p n l -> p (n l)")[:, 0:K * NT * UNITS].rearrange("p (c u) -> p c u", u=UNITS)
        o += K * NT * 2 * UNITS
        r_te = flat[:, o:o + UNITS * NE].rearrange("p (u e) -> p u e", e=NE)

        e_gu = sb("e_gu", [P, KH, 2 * I])
        e_dn = sb("e_dn", [P, 3, H])
        e_gu_hi = sb("e_gu_hi", [P, 2, KH, 2 * I], F32R)
        e_gu_lo = sb("e_gu_lo", [P, 2, KH, 2 * I], F32R)
        e_hT_hi = sb("e_hT_hi", [P, 3, P], F32R)
        e_hT_lo = sb("e_hT_lo", [P, 3, P], F32R)

        names = """const_loaded weights_loaded ctx_loaded z_loaded consts_made tables_made
            xin_ready acc_ready conv_done u_ready u_stored xd_ready xd_copied bc_stored
            dtp_ready dtp_free abs_done e_ready ln_ready ser_ready dt_ready dt_stored
            z_var z_rstd z_norm sz_ready sz_stored a_exp a_ready pool_step tap_done zstat_done soft_done dummy_ready
            u0_loaded u1_loaded d0_loaded d1_loaded x0_loaded x1_loaded s0_loaded s1_loaded
            b0_loaded b1_loaded b2_loaded b3_loaded c0_loaded c1_loaded c2_loaded c3_loaded
            w_ready dbu_ready exp_done scan_done g_ready pair_ready ymm_done y_taken yT_ready x1_ready x1_stored
            xt0_loaded xt1_loaded xt2_loaded xt3_loaded var_ready rstd_ready norm_ready xn_ready xn0_stored xn1_stored xnT_ready xnT_copied lg_ready lg_copied
            gate_ready up_ready sg_ready h_ready hT_ready hT_copied down_ready down_added out_stored
            trash_stored rt_max rt_exp rt_mask rt_rank rt_oh rt_table tables_ready
            gu_loaded gu_split dn_loaded dn_split split_step xT_split e_taken hT_split gidx_ready w_copied
            gx0_loaded gx1_loaded ex_ready exT_copied eg_ready eu_ready esg_ready eh_ready ehT_ready ehT_copied
            ey_ready ey_taken scattered gated_done tstat_done route_step idx_step waits_passed""".split()
        s = {n: sem(n) for n in names}
        (const_loaded, weights_loaded, ctx_loaded, z_loaded, consts_made, tables_made,
         xin_ready, acc_ready, conv_done, u_ready, u_stored, xd_ready, xd_copied, bc_stored,
         dtp_ready, dtp_free, abs_done, e_ready, ln_ready, ser_ready, dt_ready, dt_stored,
         z_var, z_rstd, z_norm, sz_ready, sz_stored, a_exp, a_ready, pool_step, tap_done, zstat_done, soft_done,
         dummy_ready) = [s[n] for n in names[:34]]
        u_loaded = [s["u0_loaded"], s["u1_loaded"]]
        d_loaded = [s["d0_loaded"], s["d1_loaded"]]
        x_loaded = [s["x0_loaded"], s["x1_loaded"]]
        s_loaded = [s["s0_loaded"], s["s1_loaded"]]
        b_loaded = [s[f"b{q}_loaded"] for q in range(NG)]
        c_loaded = [s[f"c{q}_loaded"] for q in range(NG)]
        at = names.index("w_ready")
        (w_ready, dbu_ready, exp_done, scan_done, g_ready, pair_ready, ymm_done, y_taken, yT_ready, x1_ready, x1_stored,
         xt0_loaded, xt1_loaded, xt2_loaded, xt3_loaded, var_ready, rstd_ready, norm_ready, xn_ready, xn0_stored, xn1_stored, xnT_ready, xnT_copied, lg_ready,
         lg_copied, gate_ready, up_ready, sg_ready, h_ready, hT_ready, hT_copied, down_ready, down_added,
         out_stored, trash_stored, rt_max, rt_exp, rt_mask, rt_rank, rt_oh, rt_table,
         tables_ready) = [s[n] for n in names[at:at + 42]]
        xt_loaded = [xt0_loaded, xt1_loaded, xt2_loaded, xt3_loaded]
        xn_stored = [xn0_stored, xn1_stored]
        gu_loaded, gu_split, dn_loaded, dn_split = s["gu_loaded"], s["gu_split"], s["dn_loaded"], s["dn_split"]
        split_step, xT_split, eu_taken, hT_split = s["split_step"], s["xT_split"], s["e_taken"], s["hT_split"]
        gx_loaded = [s["gx0_loaded"], s["gx1_loaded"]]
        (gidx_ready, w_copied) = s["gidx_ready"], s["w_copied"]
        at = names.index("ex_ready")
        (ex_ready, exT_copied, eg_ready, eu_ready, esg_ready, eh_ready, ehT_ready, ehT_copied,
         ey_ready, ey_taken, scattered, gated_done, tstat_done, route_step, idx_step, waits_passed) = [s[n] for n in names[at:at + 16]]
        block = stack.enter_context(nc.Block())

        def held(eng):
            eng.sem_inc(waits_passed)

        def from_one(eng, count):
            eng.sem_inc(count, 1)

        def pre_finished(eng):
            for stored in (u_stored, bc_stored, dt_stored, sz_stored):
                eng.wait_ge(stored, 1 + 16 * B)

        @block.sync
        def _(sp):
            for count in (u_stored, sz_stored, bc_stored, dt_stored, out_stored, xn0_stored, xn1_stored):
                from_one(sp, count)
            for dst, src in ((p_in[:], inT.rearrange("(t p) n -> p t n", p=P)), (c_conv[:], convw), (c_convb[:], convb),
                             (p_xp[:], xpT.rearrange("(t p) n -> p t n", p=P)), (p_dtw[:], dtT), (c_dtb[:], dtb),
                             (c_alog[:], alog), (c_d[:], dskip), (c_gate[:], gateT.rearrange("(t p) n -> p t n", p=P))):
                sp.dma_start(dst, src).then_inc(const_loaded, 16)
            def load_ctx(b):
                sp.dma_start(p_ctx[:], ctxT[bass.ds(b, 1)].rearrange("a (t p) l -> p (a t) l", p=P)).then_inc(ctx_loaded, 16)

            def load_x(b):
                sp.dma_start(p_x[:], batch_rows(x, b)).then_inc(z_loaded, 16)

            def dt_store(b):
                sp.wait_ge(dt_ready, 1 + b * DT + DT)
                sp.dma_start(dt_d[bass.ds(b, 1)].rearrange("a p t l -> p (a t) l"), p_dt[:]).then_inc(dt_stored, 16)

            def step(b, last=False):
                if not last:
                    sp.wait_ge(xin_ready, 1 + b * DT + DT)
                    load_ctx(b + 1)
                sp.wait_ge(u_ready, b * DT + DT)
                sp.dma_start(u_d[bass.ds(b, 1)].rearrange("a p t l -> p (a t) l"), p_u[:]).then_inc(u_stored, 16)
                sp.wait_ge(sz_ready, 1 + b * TB + TB)
                if not last:
                    load_x(b + 1)
                sp.dma_start(batch_rows(sz_d, b), p_sz[:]).then_inc(sz_stored, 16)
                sp.wait_ge(xd_copied, 1 + b + 1)
                sp.dma_start(bc_d[bass.ds(b, 1)].rearrange("a n l -> (a n) l"), p_xd[RK:NX, :]).then_inc(bc_stored, 16)

            def load_bc(b, g, which):
                dst, row, done = ((Bs, 0, b_loaded), (Cs, NS, c_loaded))[which]
                src = bc_d[bass.ds(b, 1), row + g * GRP:row + (g + 1) * GRP, :].rearrange("a n l -> a (n l)")
                sp.dma_start(dst[:, g * GRP:(g + 1) * GRP, :].rearrange("p n l -> p (n l)"),
                             src.to_broadcast([P, GRP * L])).then_inc(done[g], 16)

            load_ctx(0)
            load_x(0)
            sp.dma_start(ws_gu[:], sgu.rearrange("(t p) n -> p t n", p=P)).then_inc(weights_loaded, 16)
            for c in range(2):
                for t, (r, n) in enumerate(IT):
                    sp.dma_start(ws_dn[0:n, c, t, :], sdn[c * I + r:c * I + r + n, :]).then_inc(weights_loaded, 16)

            step(0)
            sp.wait_ge(bc_stored, 1 + 16)
            for g in range(NG):
                load_bc(0, g, 0)
            with sp.Fori(1, B - 1) as b:
                step(b)
                dt_store(b - 1)
            for g in range(NG):
                load_bc(0, g, 1)
            step(B - 1, last=True)
            dt_store(B - 2)
            dt_store(B - 1)

            def load_dtu(b, q):
                par = q % 2
                sp.dma_start(m_dt[:, par, :], dt_d[bass.ds(b, 1), :, q, :].rearrange("a p l -> p (a l)")).then_inc(d_loaded[par], 16)
                sp.dma_start(m_u[:, par, :], u_d[bass.ds(b, 1), :, q, :].rearrange("a p l -> p (a l)")).then_inc(u_loaded[par], 16)

            def load_xsz(b, q):
                par = q % 2
                sp.dma_start(m_x[:, par], batch_rows(x, b)[:, :, q * P:(q + 1) * P]).then_inc(x_loaded[par], 16)
                sp.dma_start(m_sz[:, par], sz_d[bass.ds(b * L + q * P, P), :]).then_inc(s_loaded[par], 16)

            pre_finished(sp)
            load_dtu(0, 0)
            load_xsz(0, 0)
            load_dtu(0, 1)
            load_xsz(0, 1)
            sp.wait_ge(dummy_ready, 1)
            for t in range(SPARE // P):
                sp.dma_start(xn_d[t * P:(t + 1) * P, :], f_xnT[:, 2, :]).then_inc(trash_stored, 16)

            def x1_store(b, q, i):
                sp.wait_ge(x1_ready, i + 1)
                held(sp)
                sp.dma_start(batch_rows(x1_d, b)[:, :, q * P:(q + 1) * P], m_x[:, q % 2]).then_inc(x1_stored, 16)

            def xt_load(j, jb):
                sp.wait_ge(x1_stored, jb * 16 * DT + 16 * DT)
                sp.dma_start(xt[:, j[1], :], x1_d[bass.ds(j[0] * P, P), :]).then_inc(xt_loaded[j[1]], 16)

            def xn_store(j):
                sp.wait_ge(xn_ready, j[0] + 1)
                sp.dma_start(xn_d[bass.ds(j[0] * P + SPARE, P), :], f_xn[:, j[1] % 2, :]).then_inc(xn_stored[j[1] % 2], 16)

            def out_store(f):
                sp.wait_ge(down_added, 1 + f[0] + 1)
                sp.dma_start(out[bass.ds(f[0] * P, P), :], xt[:, (f[1] + 2) % 4, :]).then_inc(out_stored, 16)

            def slot(b, q, rows, last=False):
                i = b * DT + q
                later = not (isinstance(b, int) and b == 0 and q == 0)
                more = later and not (last and q == DT - 1)
                nb, nq = (b, q + 1) if q < DT - 1 else (b + 1, 0)
                new_bc = q == DT - 1 and not last
                j = ((b - 1) * DT + q, q)
                if more:
                    sp.wait_ge(y_taken, i)
                    held(sp)
                    load_dtu(nb, nq)
                if new_bc:
                    for g in range(NG):
                        sp.wait_ge(dbu_ready, i * NG + g + 1)
                        load_bc(b + 1, g, 0)
                if later:
                    x1_store(*((b, q - 1) if q else (b - 1, DT - 1)), i - 1)
                if more:
                    sp.wait_ge(x1_stored, i * 16)
                    held(sp)
                    load_xsz(nb, nq)
                if rows:
                    sp.wait_ge(out_stored, 1 + j[0] * 16)
                    held(sp)
                    if q == 0:
                        xt_load(j, b - 1)
                    if q < TB - 1:
                        xt_load((j[0] + 1, q + 1), b - 1)
                if new_bc:
                    for g in range(NG):
                        sp.wait_ge(g_ready, i * NS + g * GRP + GRP)
                        load_bc(b + 1, g, 1)
                        if rows and g == 2:
                            out_store(j)
                            xn_store(j)
                elif rows:
                    out_store(j)
                    xn_store(j)

            for q in range(DT):
                slot(0, q, False)
            with sp.Fori(1, B - 1) as b:
                for q in range(DT):
                    slot(b, q, True)
            for q in range(DT):
                slot(B - 1, q, True, last=True)

            def load_gu(e):
                sp.dma_start(e_gu[:], wgu[bass.ds(e, 1)].rearrange("a (t p) n -> p (a t) n", p=P)).then_inc(gu_loaded, 16)

            def load_dn(e):
                sp.dma_start(e_dn[:, 0:2, :], wdn[bass.ds(e, 1), 0:2 * P, :].rearrange("a (t p) n -> p (a t) n", p=P)).then_inc(dn_loaded, 16)
                sp.dma_start(e_dn[0:IT[2][1], 2, :], wdn[bass.ds(e, 1), 2 * P:I, :].rearrange("a p n -> (a p) n")).then_inc(dn_loaded, 16)

            x1_store(B - 1, DT - 1, B * DT - 1)
            first = NT - TB
            sp.wait_ge(out_stored, 1 + first * 16)
            for q in range(2):
                xt_load((first + q, q), B - 1)
            out_store((first, 0))
            sp.wait_ge(out_stored, 1 + (first + 1) * 16)
            xt_load((first + 2, 2), B - 1)
            xn_store((first, 0))
            out_store((first + 1, 1))
            sp.wait_ge(out_stored, 1 + (first + 2) * 16)
            xt_load((NT - 1, TB - 1), B - 1)
            sp.wait_ge(g_ready, B * STEPS)
            load_gu(0)
            load_dn(0)
            for q in range(1, TB):
                xn_store((first + q, q))
            for f in range(first + 2, NT + 1):
                out_store((f, f % TB))

            def next_expert(e):
                sp.wait_ge(gu_split, e)
                held(sp)
                load_gu(e)
                sp.wait_ge(dn_split, e)
                held(sp)
                load_dn(e)

            next_expert(1)
            out_store((NT + 1, 1))
            with sp.Fori(2, NE) as e:
                next_expert(e)
            sp.wait_ge(scattered, 16 * UNITS)
            sp.wait_ge(out_stored, 1 + 16 * (NT + 2))
            sp.wait_ge(trash_stored, 16 * (SPARE // P))

        @block.tensor
        def _(pe):
            mm = nc.tensor.matmul
            for count in (xin_ready, xnT_ready, hT_ready, down_ready, eu_ready, ey_ready):
                from_one(pe, count)
            pe.wait_ge(const_loaded, 16 * 9)
            pe.wait_ge(consts_made, 6)

            def project(b):
                pe.wait_ge(ctx_loaded, b * 16 + 16)
                for q in range(DT):
                    pe.wait_ge(conv_done, b * DT + q + 1)
                    for t in range(2):
                        last = mm(XIN[q % 2][:], p_in[:, t, q * P:(q + 1) * P], p_ctx[:, t, :], start=t == 0, stop=t == 1)
                    last.then_inc(xin_ready, 1)
                pe.wait_ge(xd_copied, 1 + b)
                for q in range(DT):
                    pe.wait_ge(u_ready, b * DT + q + 1)
                    last = mm(XDB[0:NX, :], p_xp[:, q, :], p_u[:, q, :], start=q == 0, stop=q == DT - 1)
                last.then_inc(xd_ready, 1)
                pe.wait_ge(xd_copied, 1 + b + 1)
                for q in range(DT):
                    if not isinstance(b, int):
                        pe.wait_ge(dtp_free, (b - 1) * DT + q + 1)
                    mm(DTP[q][:], p_dtw[:, q * P:(q + 1) * P], p_xd[0:RK, :], start=True, stop=True).then_inc(dtp_ready, 1)

            project(0)
            with pe.Fori(1, B) as b:
                project(b)
            pre_finished(pe)
            pe.wait_ge(weights_loaded, 16 * 7)
            pe.wait_ge(dummy_ready, 1)

            def y_sum(b, q, n):
                i, k = b * DT + q, q * NS + n
                if first_of_pair(i, n):
                    return
                if n == 0 and not (isinstance(i, int) and i < 2):
                    pe.wait_ge(y_taken, i - 1)
                if n and first_of_pair(i, n - 1):
                    pe.wait_ge(pair_ready, (i - (DT - 1)) * len(PAIRED) + PAIRED.index(n // GRP) + 1)
                else:
                    pe.wait_ge(g_ready, i * NS + n + 1)
                mm(Y[q % 2][:], ident[:], gs[:, k % RING_G, :], start=n == 0, stop=n == NS - 1).then_inc(ymm_done, 1)

            def y_turn(i, copied):
                pe.wait_ge(gated_done, i + 1)
                pe.wait_ge(x1_ready, i)
                pe.wait_ge(lg_copied, 1 + copied)
                for t in range(TB):
                    last = nc.tensor.transpose(TP[:, t * P:(t + 1) * P], m_y[:, t * P:(t + 1) * P], ident[:])
                last.then_inc(yT_ready, 1)

            def xn_turn(j, x1_count):
                pe.wait_ge(xn_ready, j[0] + 1)
                pe.wait_ge(x1_ready, x1_count)
                pe.wait_ge(lg_copied, 1 + j[0])
                for t in range(KH):
                    last = nc.tensor.transpose(TP[:, t * P:(t + 1) * P], f_xn[:, j[1] % 2, t * P:(t + 1) * P], ident[:])
                last.then_inc(xnT_ready, 1)

            def router(f, copied):
                pe.wait_ge(xnT_copied, 1 + copied)
                pe.wait_ge(lg_copied, 1 + f[0])
                for t in range(KH):
                    last = mm(TP[:, 0:NE], f_xnT[:, (f[1] + 3) % 4, t * P:(t + 1) * P], c_gate[:, t, :], start=t == 0, stop=t == KH - 1)
                last.then_inc(lg_ready, 1)

            def shared(f):
                at = (f[1] + 2) % 4
                lhs = [f_xnT[:, at, t * P:(t + 1) * P] for t in range(KH)]

                def rows_in(c, half):
                    dst, off, done = GU[f[1] % 2][c], half * 2 * I + c * I, (gate_ready, up_ready)[half]

                    def piece(ts):
                        if ts[0] == 0 and half == 0:
                            if not (isinstance(f[0], int) and f[0] == 0):
                                pe.wait_ge(hT_copied, 1 + 2 * (f[0] - 1))
                            if not (isinstance(f[0], int) and f[0] == 0):
                                pe.wait_ge(xnT_copied, f[0])
                        elif ts[0] == 0:
                            pe.wait_ge(sg_ready, 2 * f[0] + c + 1)
                        for t in ts:
                            last = mm(dst[:, 0:I], lhs[t], ws_gu[:, t, off:off + I], start=t == 0, stop=t == KH - 1)
                        if ts[-1] == KH - 1:
                            last.then_inc(done, 1)
                    return [lambda: piece([0, 1]), lambda: piece([2, 3])]

                def turn(c):
                    pe.wait_ge(h_ready, 1 + 2 * f[0] + c + 1)
                    for t, (r, n) in enumerate(IT):
                        last = nc.tensor.transpose(GU[f[1] % 2][c][0:n, t * P:(t + 1) * P], f_h[:, c, r:r + n], ident[:])
                    last.then_inc(hT_ready, 1)

                def down(c, t):
                    if t == 0:
                        pe.wait_ge(hT_copied, 1 + 2 * f[0] + c + 1)
                    if t == 0 and c == 0:
                        pe.wait_ge(down_added, 1 + f[0])
                    n = IT[t][1]
                    last = mm(YO[:], f_hT[0:n, c, t, :], ws_dn[0:n, c, t, :], start=c == 0 and t == 0, stop=c == 1 and t == 2)
                    if c == 1 and t == 2:
                        last.then_inc(down_ready, 1)

                return (rows_in(0, 0) + rows_in(1, 0) + rows_in(0, 1) + rows_in(1, 1) + [lambda: turn(0), lambda: turn(1)]
                        + [lambda c=c, t=t: down(c, t) for c in range(2) for t in range(3)])

            def slot(b, q, rows):
                i = b * DT + q
                late, early = [], []
                if rows:
                    f = ((b - 1) * DT + q, q)
                    late = shared(f)[SPLIT:]
                    early = shared((f[0] + 1, (q + 1) % TB))[:SPLIT]
                    router(f, f[0])
                elif q == DT - 1:
                    early = shared((0, 0))[:SPLIT]
                for piece in early[0:PE_AT[0]] + late[0:LATE_AT[0]]:
                    piece()
                for n in range(NS):
                    y_sum(b, q, n)
                    if n == Y_TURN_AT and not (isinstance(b, int) and b == 0 and q == 0):
                        y_turn(i - 1, f[0] + 1 if rows else 0)
                    for piece in early[PE_AT[n]:PE_AT[n + 1]] + late[LATE_AT[n]:LATE_AT[n + 1]]:
                        piece()
                    if rows and n == XN_TURN_AT[q > 0]:
                        xn_turn(f, i)

            for q in range(DT):
                slot(0, q, False)
            with pe.Fori(1, B) as b:
                for q in range(DT):
                    slot(b, q, True)
            pe.wait_ge(xnT_copied, 1 + NT - TB)
            y_turn(B * DT - 1, NT - TB)

            def whole(f):
                for piece in shared(f):
                    piece()

            first = NT - TB
            for piece in shared((first, 0))[SPLIT:]:
                piece()
            whole((first + 1, 1))
            for q in range(TB - 1):
                xn_turn((first + q, q), B * DT)
                router((first + q, q), first + q + 1)
            whole((first + 2, 2))
            xn_turn((NT - 1, TB - 1), B * DT)
            router((NT - 1, TB - 1), NT)
            router((NT, 0), NT)
            whole((first + 3, 3))
            pe.wait_ge(rt_mask, 1)
            ms = r_ms[:, :, :].rearrange("p t e -> p (t e)")
            mm(RANK[:, 0:NT * NE], upper[:], ms, start=True, stop=True).then_inc(rt_rank, 1)
            mm(TOT[:, 0:NT * NE], ones[:], ms, start=True, stop=True).then_inc(rt_rank, 1)
            whole((NT, 0))
            for c in range(K * NT):
                if c % 8 == 0:
                    pe.wait_ge(rt_oh, c // 8 + 1)
                last = mm(TABLE[:, 0:2 * UNITS], r_ohr[:, c, :], r_rhs[:, c, :, :].rearrange("p v u -> p (v u)"),
                          start=c == 0, stop=c == K * NT - 1)
            last.then_inc(rt_table, 1)

            def x_turn(k, par, loads):
                pe.wait_ge(gx_loaded[par], loads)
                pe.wait_ge(exT_copied, k)
                for t in range(KH):
                    last = nc.tensor.transpose(TX[:, t * P:(t + 1) * P], e_x[:, par, t * P:(t + 1) * P], ident[:])
                last.then_inc(ex_ready, 1)

            def expert_of(k):
                e = pe.value_load(t_expi[0:1, bass.ds(k, 1)], min_val=0, max_val=NE - 1)
                return e, e % 2

            def in_parts(dst, lhs, rhs, first, final):
                (a_hi, a_lo), (w_hi, w_lo) = lhs, rhs
                mm(dst, a_hi, w_hi, start=first, stop=False)
                mm(dst, a_hi, w_lo, start=False, stop=False)
                return mm(dst, a_lo, w_hi, start=False, stop=final)

            def up(k, par, half, e, ring):
                if half == 0:
                    pe.wait_ge(xT_split, k + 1)
                    pe.wait_ge(gu_split, e + 1)
                dst, done, free = ((G, eg_ready, esg_ready), (U, eu_ready, eu_taken))[half]
                pe.wait_ge(free, k)
                for t in range(KH):
                    w = [a[:, bass.ds(ring, 1), t, half * I:(half + 1) * I].rearrange("p a n -> p (a n)") for a in (e_gu_hi, e_gu_lo)]
                    rows = [a[:, par, t * P:(t + 1) * P] for a in (e_xT_hi, e_xT_lo)]
                    last = in_parts(dst[:, 0:I], rows, w, t == 0, t == KH - 1)
                last.then_inc(done, 1)

            def h_turn(k):
                pe.wait_ge(eh_ready, k + 1)
                pe.wait_ge(ehT_copied, k)
                for t, (r, n) in enumerate(IT):
                    last = nc.tensor.transpose(TH[0:n, t * P:(t + 1) * P], e_h[:, r:r + n], ident[:])
                last.then_inc(ehT_ready, 1)

            def down(k, e, ring):
                pe.wait_ge(hT_split, k + 1)
                pe.wait_ge(dn_split, e + 1)
                pe.wait_ge(ey_taken, 1 + k)
                for t in range(3):
                    n = IT[t][1]
                    w = [a[0:n, bass.ds(ring, 1), t, :].rearrange("p a n -> p (a n)") for a in (e_dn_hi, e_dn_lo)]
                    last = in_parts(YO[:], [a[0:n, t, :] for a in (e_hT_hi, e_hT_lo)], w, t == 0, t == 2)
                last.then_inc(ey_ready, 1)

            rest = shared((NT + 1, 1))
            for piece in rest[:SPLIT - 2]:
                piece()
            x_turn(0, 0, 16)
            for piece in rest[SPLIT - 2:]:
                piece()
            pe.wait_ge(hT_copied, 1 + 2 * (NT + 2))
            pe.wait_ge(h_ready, 1 + 2 * (NT + 2))
            pe.wait_ge(down_added, 1 + NT + 2)
            pe.wait_ge(tables_ready, 1)

            def step(k, par, loads):
                static = isinstance(k, int)
                if not static or k > 1:
                    before = expert_of(k - 2)
                now = expert_of(k)
                if not static or k < UNITS - 1:
                    x_turn(k + 1, 1 - par, loads)
                up(k, par, 0, *now)
                if not static or k > 1:
                    down(k - 2, *before)
                if not static or k:
                    h_turn(k - 1)
                up(k, par, 1, *now)

            step(0, 0, 16)
            step(1, 1, 32)
            with pe.Fori(1, UNITS // 2) as r:
                for half in range(2):
                    step(r * 2 + half, half, (r + half) * 16 + 16)
            step(UNITS - 1, 0, 0)
            down(UNITS - 2, *expert_of(UNITS - 2))
            h_turn(UNITS - 1)
            down(UNITS - 1, *expert_of(UNITS - 1))

        @block.scalar
        def _(act):
            f = nc.scalar.activation
            for count in (sz_ready, xd_copied, xnT_copied, hT_copied):
                from_one(act, count)
            act.wait_ge(const_loaded, 16 * 9)
            f(c_a[:], c_alog[:], ACT.Exp).then_inc(a_exp, 1)

            def conv_first(b, q):
                act.wait_ge(xin_ready, 1 + b * DT + q + 1)
                f(p_acc[:, q, :], XIN[q % 2][:], ACT.Identity, scale=c_conv[:, q, 3:4], bias=c_convb[:, q:q + 1]).then_inc(acc_ready, 1)

            def silus(b):
                act.wait_ge(u_stored, 1 + b * 16)
                for q in range(DT):
                    act.wait_ge(conv_done, b * DT + q + 3)
                    f(p_u[:, q, :], p_acc[:, q, :], ACT.Silu).then_inc(u_ready, 1)
                act.wait_ge(z_norm, b + 1)
                act.wait_ge(sz_stored, 1 + b * 16)
                for t in range(TB):
                    f(p_sz[:, t, :], p_x[:, t, :], ACT.Silu, scale=p_rs[:, t:t + 1], bias=p_nm[:, t:t + 1]).then_inc(sz_ready, 1)
                act.wait_ge(xd_ready, b + 1)
                act.wait_ge(bc_stored, 1 + b * 16)
                f(p_xd[:], XDB[0:NX, :], ACT.Copy).then_inc(xd_copied, 1)

            def exps(b, qs):
                act.wait_ge(dt_ready, 1 + b * DT)
                for q in qs:
                    act.wait_ge(dtp_ready, b * DT + q + 1)
                    f(p_abs[:, q % 2, :], DTP[q][:], ACT.Abs, bias=c_dtb[:, q:q + 1]).then_inc(abs_done, 1)
                    f(p_relu[:, q, :], DTP[q][:], ACT.Relu, bias=c_dtb[:, q:q + 1]).then_inc(dtp_free, 1)
                    act.wait_ge(abs_done, b * DT + q + 1)
                    f(p_e[:, q, :], p_abs[:, q % 2, :], ACT.Exp, scale=-1.0).then_inc(e_ready, 1)

            def logs(b):
                for q in range(DT):
                    act.wait_ge(e_ready, b * DT + q + 1)
                    f(p_ln[:, q, :], p_e[:, q, :], ACT.Ln, bias=1.0).then_inc(ln_ready, 1)

            for q in range(DT):
                conv_first(0, q)
            silus(0)
            with act.Fori(1, B) as b:
                for q in range(DT):
                    conv_first(b, q)
                    exps(b - 1, (q,))
                silus(b)
                logs(b - 1)
            exps(B - 1, range(DT))
            logs(B - 1)
            pre_finished(act)
            act.wait_ge(a_ready, 1)

            def decay(b, q, n):
                k = q * NS + n
                if not (isinstance(b, int) and b == 0 and k < RING_H):
                    act.wait_ge(g_ready, b * STEPS + k - RING_H + 1)
                if n == 0:
                    act.wait_ge(d_loaded[q % 2], b * 32 + (q // 2) * 16 + 16)
                f(hs[:, k % RING_H, :], m_dt[:, q % 2, :], ACT.Exp, scale=c_a[:, q, n:n + 1]).then_inc(exp_done, 1)

            def gate(fx, c):
                act.wait_ge(gate_ready, 2 * fx[0] + c + 1)
                act.wait_ge(h_ready, 1 + 2 * fx[0])
                f(f_sg[:, c, :], GU[fx[1] % 2][c][:, 0:I], ACT.Silu).then_inc(sg_ready, 1)

            def hT_copy(fx, c):
                act.wait_ge(hT_ready, 1 + 2 * fx[0] + c + 1)
                act.wait_ge(down_ready, 1 + fx[0])
                f(f_hT[:, c, 0:2, :], GU[fx[1] % 2][c][:, 0:2 * P].rearrange("p (t j) -> p t j", t=2), ACT.Copy)
                f(f_hT[0:96, c, 2, :], GU[fx[1] % 2][c][0:96, 2 * P:3 * P], ACT.Copy).then_inc(hT_copied, 1)

            def xn(j, stored):
                act.wait_ge(norm_ready, j[0] + 1)
                act.wait_ge(xn_stored[j[1] % 2], 1 + stored)
                act.wait_ge(xnT_ready, 1 + j[0] - (isinstance(j[0], int) and j[0] > 0))
                f(f_xn[:, j[1] % 2, :], xt[:, j[1], :], ACT.Identity, scale=f_rs[:, j[1]:j[1] + 1], bias=f_nm[:, j[1]:j[1] + 1]).then_inc(xn_ready, 1)

            def xnT_copy(j, past):
                act.wait_ge(xnT_ready, 1 + j[0] + 1)
                act.wait_ge(down_ready, 1 + past)
                f(f_xnT[:, j[1], :], TP[:], ACT.Copy).then_inc(xnT_copied, 1)

            def slot(b, q, rows):
                j = ((b - 1) * DT + q, q)
                for n in range(NS):
                    decay(b, q, n)
                    if rows and n == HT_AT:
                        hT_copy(j, 0)
                        hT_copy(j, 1)
                    if n == GATE_AT:
                        for c in range(2):
                            if rows:
                                gate((j[0] + 1, (q + 1) % TB), c)
                            elif q == DT - 1:
                                gate((0, 0), c)
                    if rows and n == XN_AT[q > 0]:
                        xn(j, ((b - 1) * 2 + q // 2) * 16)
                    if rows and n == XNT_AT[q > 0]:
                        xnT_copy(j, j[0])

            for q in range(DT):
                slot(0, q, False)
            act.wait_ge(trash_stored, 16 * (SPARE // P))
            with act.Fori(1, B) as b:
                for q in range(DT):
                    slot(b, q, True)

            def whole(fx):
                gate(fx, 0)
                gate(fx, 1)
                hT_copy(fx, 0)
                hT_copy(fx, 1)

            first = NT - TB
            hT_copy((first, 0), 0)
            hT_copy((first, 0), 1)

            def xn_of(q):
                xn((first + q, q), ((first + q) // 2) * 16)

            def xnT_of(q):
                xnT_copy((first + q, q), first + q - 1)

            xn_of(0)
            whole((first + 1, 1))
            xnT_of(0)
            xn_of(1)
            xnT_of(1)
            xn_of(2)
            xnT_of(2)
            xn_of(3)
            whole((first + 2, 2))
            xnT_of(3)
            act.wait_ge(rt_max, 1)
            f(r_e[:], r_e[:], ACT.Exp).then_inc(rt_exp, 1)
            whole((first + 3, 3))
            whole((NT, 0))
            gate((NT + 1, 1), 0)
            gate((NT + 1, 1), 1)

            def x_copy(k, par):
                act.wait_ge(ex_ready, k + 1)
                if not isinstance(k, int) or k:
                    act.wait_ge(xT_split, k)
                if not isinstance(k, int) or k > 1:
                    act.wait_ge(eu_ready, 1 + k - 1)
                f(e_xT[:], TX[:], ACT.Copy)
                f(e_xT_hi[:, par, :], TX[:], ACT.Copy).then_inc(exT_copied, 1)

            def gate_of(k):
                act.wait_ge(eg_ready, k + 1)
                act.wait_ge(eh_ready, k)
                f(e_sg[:], G[:, 0:I], ACT.Silu).then_inc(esg_ready, 1)

            def up_of(k):
                act.wait_ge(eu_ready, 1 + k + 1)
                f(e_u[:], U[:, 0:I], ACT.Copy).then_inc(eu_taken, 1)

            def h_copy(k):
                act.wait_ge(ehT_ready, k + 1)
                act.wait_ge(hT_split, k)
                act.wait_ge(ey_ready, 1 + k)
                for n, ts in ((P, slice(0, 2)), (IT[2][1], slice(2, 3))):
                    src = TH[0:n, ts.start * P:ts.stop * P].rearrange("p (t j) -> p t j", j=P)
                    f(e_hT[0:n, ts, :], src, ACT.Copy)
                    last = f(e_hT_hi[0:n, ts, :], src, ACT.Copy)
                last.then_inc(ehT_copied, 1)

            def weigh(k, par):
                act.wait_ge(ey_ready, 1 + k + 1)
                act.wait_ge(w_copied, k + 1)
                if not isinstance(k, int) or k > 1:
                    act.wait_ge(scattered, (k - 1) * 16)
                f(e_y[:, par, :], YO[:], ACT.Identity, scale=e_w[:, par:par + 1], bias=zero[:]).then_inc(ey_taken, 1)

            def step(k, par):
                static = isinstance(k, int)
                if not static or k < UNITS - 1:
                    x_copy(k + 1, 1 - par)
                gate_of(k)
                if not static or k > 1:
                    weigh(k - 2, par)
                if not static or k:
                    h_copy(k - 1)
                up_of(k)

            act.wait_ge(tables_ready, 1)
            x_copy(0, 0)
            hT_copy((NT + 1, 1), 0)
            hT_copy((NT + 1, 1), 1)
            for k in range(4):
                step(k, k % 2)
            with act.Fori(2, UNITS // 2) as r:
                for half in range(2):
                    step(r * 2 + half, half)
            step(UNITS - 1, 0)
            weigh(UNITS - 2, 1)
            h_copy(UNITS - 1)
            weigh(UNITS - 1, 0)

        @block.gpsimd
        def _(pool):
            g = nc.gpsimd
            g.memset(ident[:], 0.0).then_inc(pool_step, 1)
            g.memset(ones[:], 1.0).then_inc(consts_made, 1)
            g.memset(halves[:], -0.5).then_inc(consts_made, 1)
            g.memset(upper[:], 1.0).then_inc(pool_step, 1)
            g.memset(zero[:], 0.0).then_inc(consts_made, 1)
            pool.wait_ge(pool_step, 2)
            g.affine_select(out=ident[:], in_=ident[:], compare_op=ALU.not_equal, fill=1.0, base=0,
                            pattern=[[-1, P]], channel_multiplier=1).then_inc(consts_made, 1)
            g.affine_select(out=upper[:], in_=upper[:], compare_op=ALU.is_gt, fill=0.0, base=0,
                            pattern=[[1, P]], channel_multiplier=-1).then_inc(consts_made, 1)
            g.iota(iota_row[:], [[1, P]], base=0, channel_multiplier=0, allow_small_or_imprecise_dtypes=True).then_inc(consts_made, 1)
            g.iota(part[:], [[0, 1]], base=0, channel_multiplier=1, allow_small_or_imprecise_dtypes=True).then_inc(tables_made, 1)
            pool.wait_ge(consts_made, 6)
            made = 2

            def z_power(b):
                pool.wait_ge(z_var, b + 1)
                g.tensor_tensor(p_rs[:], p_ve[:], halves[:], ALU.pow).then_inc(z_rstd, 1)

            def series(b):
                for q in range(DT):
                    pool.wait_ge(e_ready, b * DT + q + 1)
                    held(pool)
                    g.tensor_scalar(p_ser[:, q, :], p_e[:, q, :], 1.0 / 3.0, -0.5, ALU.mult, ALU.add).then_inc(pool_step, 1)
                    pool.wait_ge(pool_step, b * DT + made + q + 1)
                    g.tensor_tensor(p_ser[:, q, :], p_ser[:, q, :], p_e[:, q, :], ALU.mult).then_inc(ser_ready, 1)

            z_power(0)
            with pool.Fori(1, B) as b:
                series(b - 1)
                z_power(b)
            series(B - 1)
            pre_finished(pool)

            def slot(b, q, rows):
                i = b * DT + q
                pool.wait_ge(u_loaded[q % 2], b * 32 + (q // 2) * 16 + 16)
                pool.wait_ge(d_loaded[q % 2], b * 32 + (q // 2) * 16 + 16)
                if not (isinstance(i, int) and i == 0):
                    pool.wait_ge(dbu_ready, i * NG)
                g.tensor_tensor(m_w[:, 0, :], m_u[:, q % 2, :], m_dt[:, q % 2, :], ALU.mult).then_inc(w_ready, 1)
                pool.wait_ge(w_ready, i + 1)
                for gr in range(NG):
                    if gr in PAIRED and (not isinstance(b, int) or i - 1 >= DT - 1):
                        pair(i - 1, (q - 1) % DT, gr)
                    pool.wait_ge(b_loaded[gr], b * 16 + 16)
                    if not (isinstance(b, int) and i == 0):
                        pool.wait_ge(scan_done, (i - 1) * NS + gr * GRP + GRP)
                    part_ = dbu[:, gr * GRP:(gr + 1) * GRP, :]
                    w = m_w[:, 0:1, :].to_broadcast([P, GRP, L])
                    g.tensor_tensor(part_, Bs[:, gr * GRP:(gr + 1) * GRP, :], w, ALU.mult).then_inc(dbu_ready, 1)
                    if rows and q == 1 and gr == RSTD_AFTER:
                        rstd(((b - 1) * DT, 0))
                if rows and q:
                    rstd(((b - 1) * DT + q, q))

            def pair(i, q, gr):
                n = gr * GRP + GRP - 1
                k = q * NS + n
                pool.wait_ge(g_ready, i * NS + n + 1)
                first, second = gs[:, (k - 1) % RING_G, :], gs[:, k % RING_G, :]
                g.tensor_tensor(second, first, second, ALU.add).then_inc(pair_ready, 1)

            def rstd(j):
                pool.wait_ge(var_ready, j[0] + 1)
                g.tensor_tensor(f_rs[:, j[1]:j[1] + 1], f_ve[:, j[1]:j[1] + 1], halves[:, 0:1], ALU.pow).then_inc(rstd_ready, 1)

            for q in range(DT):
                slot(0, q, False)
            with pool.Fori(1, B) as b:
                for q in range(DT):
                    slot(b, q, True)
            for gr in PAIRED:
                pair(B * DT - 1, DT - 1, gr)
            for q in range(TB):
                rstd((NT - TB + q, q))

            pool.wait_ge(tables_ready, 1)
            for par in range(2):
                pool.wait_ge(xn_stored[par], 1 + 16 * (NT // 2))
            pool.wait_ge(trash_stored, 16 * (SPARE // P))

            def gather(k, par, loads):
                if loads is not None:
                    pool.wait_ge(ex_ready, k - 1)
                    pool.wait_ge(gx_loaded[par], loads)
                g.tensor_copy(e_gidx[:, par:par + 1], t_tok[:, bass.ds(k, 1)]).then_inc(gidx_ready, 1)
                pool.wait_ge(gidx_ready, k + 1)
                held(pool)
                pool.indirect_dma_start(e_x[:, par, :], None, xn_d, bass.IndirectOffsetOnAxis(ap=e_gidx[:, par:par + 1], axis=0)).then_inc(gx_loaded[par], 16)

            def split_rows(k, par):
                pool.wait_ge(exT_copied, k + 1)
                g.tensor_tensor(e_xT_lo[:, par, :], e_xT[:], e_xT_hi[:, par, :].bitcast(F32), ALU.subtract).then_inc(xT_split, 1)

            def hidden_of(k):
                pool.wait_ge(esg_ready, k + 1)
                pool.wait_ge(eu_taken, k + 1)
                if not isinstance(k, int) or k:
                    pool.wait_ge(ehT_ready, k)
                g.tensor_tensor(e_h[:], e_sg[:], e_u[:], ALU.mult).then_inc(eh_ready, 1)

            def split_hidden(k):
                pool.wait_ge(ehT_copied, k + 1)
                g.tensor_tensor(e_hT_lo[:, 0:2, :], e_hT[:, 0:2, :], e_hT_hi[:, 0:2, :].bitcast(F32), ALU.subtract)
                n = IT[2][1]
                g.tensor_tensor(e_hT_lo[0:n, 2, :], e_hT[0:n, 2, :], e_hT_hi[0:n, 2, :].bitcast(F32), ALU.subtract).then_inc(hT_split, 1)

            def weights_of(k, par):
                if not isinstance(k, int) or k > 1:
                    pool.wait_ge(ey_taken, 1 + k - 1)
                g.tensor_copy(e_w[:, par:par + 1], t_w[:, bass.ds(k, 1)]).then_inc(w_copied, 1)

            def scatter(k, par):
                if not isinstance(k, int) or k:
                    pool.wait_ge(scattered, k * 16)
                g.tensor_copy(e_sidx[:, par:par + 1], t_tok[:, bass.ds(k, 1)]).then_inc(idx_step, 1)
                pool.wait_ge(idx_step, k + 1)
                pool.wait_ge(ey_taken, 1 + k + 1)
                held(pool)
                pool.indirect_dma_start(out, bass.IndirectOffsetOnAxis(ap=e_sidx[:, par:par + 1], axis=0), e_y[:, par, :], None,
                                        compute_op=ALU.add).then_inc(scattered, 16)

            def step(k, par, loads):
                static = isinstance(k, int)
                if not static or k > 1:
                    weights_of(k - 2, par)
                if not static or k < UNITS - 1:
                    split_rows(k + 1, 1 - par)
                    gather(k + 3, 1 - par, loads)
                if not static or k:
                    split_hidden(k - 1)
                hidden_of(k)
                if not static or k > 1:
                    scatter(k - 2, par)

            gather(0, 0, None)
            gather(1, 1, None)
            split_rows(0, 0)
            gather(2, 0, 16)
            pool.wait_ge(out_stored, 1 + 16 * (NT + 2))
            for k in range(4):
                step(k, k % 2, (k // 2 + 1 + k % 2) * 16 if k % 2 else (k // 2 + 1) * 16)
            with pool.Fori(2, UNITS // 2) as r:
                for half in range(2):
                    step(r * 2 + half, half, (r + 1 + half) * 16)
            step(UNITS - 1, 0, 0)
            weights_of(UNITS - 2, 1)
            scatter(UNITS - 2, 1)
            split_hidden(UNITS - 1)
            weights_of(UNITS - 1, 0)
            scatter(UNITS - 1, 0)
            pool.wait_ge(scattered, 16 * UNITS)

        @block.vector
        def _(dve):
            v = nc.vector
            for count in (dt_ready, h_ready, down_added, lg_copied, ey_taken):
                from_one(dve, count)
            dve.wait_ge(const_loaded, 16 * 9)
            dve.wait_ge(a_exp, 1)
            v.tensor_scalar(c_a[:], c_a[:], -1.0, None, ALU.mult).then_inc(a_ready, 1)
            dve.sem_inc(conv_done, 2)

            def z_stats(b):
                dve.wait_ge(z_loaded, b * 16 + 16)
                for t in range(TB):
                    last = v.bn_stats(p_st[:, t, :], p_x[:, t, :])
                last.then_inc(zstat_done, 1)
                dve.wait_ge(zstat_done, b * 2 + 1)
                dve.wait_ge(sz_ready, 1 + b * TB)
                held(dve)
                for t in range(TB):
                    last = v.bn_aggr(p_mv[:, t, :], p_st[:, t, :])
                last.then_inc(zstat_done, 1)
                dve.wait_ge(zstat_done, b * 2 + 2)
                v.tensor_scalar(p_ve[:], p_mv[:, :, 0:2][:, :, 1], EPS, None, ALU.add).then_inc(z_var, 1)

            def z_shift(b):
                dve.wait_ge(z_rstd, b + 1)
                v.scalar_tensor_tensor(p_nm[:], p_mv[:, :, 0], -1.0, p_rs[:], ALU.mult, ALU.mult).then_inc(z_norm, 1)

            def taps(b, q):
                dve.wait_ge(acc_ready, b * DT + q + 1)
                for back in range(1, 4):
                    if back > 1:
                        dve.wait_ge(tap_done, (b * DT + q) * 2 + back - 1)
                    a = p_acc[:, q, back:L]
                    ins = v.scalar_tensor_tensor(a, XIN[q % 2][:, 0:L - back], c_conv[:, q, 3 - back:4 - back], a, ALU.mult, ALU.add)
                    ins.then_inc(tap_done if back < 3 else conv_done, 1)

            def small(b, q):
                dve.wait_ge(ser_ready, b * DT + q + 1)
                v.tensor_scalar(p_mask[:, q, :], p_e[:, q, :], THETA, None, ALU.is_ge)
                v.scalar_tensor_tensor(p_ser[:, q, :], p_ser[:, q, :], 1.0, p_e[:, q, :], ALU.add, ALU.mult).then_inc(soft_done, 1)

            def large(b):
                dve.wait_ge(dt_stored, 1 + b * 16)
                for q in range(DT):
                    dve.wait_ge(soft_done, b * 2 * DT + DT)
                    dve.wait_ge(ln_ready, b * DT + q + 1)
                    held(dve)
                    v.copy_predicated(p_ser[:, q, :], p_mask[:, q, :], p_ln[:, q, :]).then_inc(soft_done, 1)
                    if q:
                        total(b, q - 1)
                total(b, DT - 1)

            def total(b, q):
                dve.wait_ge(soft_done, b * 2 * DT + DT + q + 1)
                v.tensor_tensor(p_dt[:, q, :], p_ser[:, q, :], p_relu[:, q, :], ALU.add).then_inc(dt_ready, 1)

            for q in range(DT):
                taps(0, q)
            z_stats(0)
            z_shift(0)
            with dve.Fori(1, B) as b:
                for q in range(DT):
                    taps(b, q)
                    if q == 1:
                        small(b - 1, 0)
                z_stats(b)
                for q in range(1, DT):
                    small(b - 1, q)
                    if q == 1:
                        z_shift(b)
                large(b - 1)
            for q in range(DT):
                small(B - 1, q)
            large(B - 1)
            pre_finished(dve)
            v.memset(xt[:, 2:4, :], 0.0)
            v.memset(f_xnT[:, 2:4, :], 0.0).then_inc(dummy_ready, 1)

            def scan(b, q, n):
                k = q * NS + n
                if n % GRP == 0:
                    dve.wait_ge(dbu_ready, (b * DT + q) * NG + n // GRP + 1)
                dve.wait_ge(exp_done, b * STEPS + k + 1)
                h = hs[:, k % RING_H, :]
                v.tensor_tensor_scan(h, h, dbu[:, n, :], 0.0, ALU.mult, ALU.add).then_inc(scan_done, 1)

            def times_c(b, q, n):
                k = q * NS + n
                dve.wait_ge(scan_done, b * STEPS + k + 1)
                if n % GRP == 0:
                    dve.wait_ge(c_loaded[n // GRP], b * 16 + 16)
                if not (isinstance(b, int) and b == 0 and k < RING_G):
                    i, m = (b * DT + q, n - RING_G) if n >= RING_G else (b * DT + q - 1, n - RING_G + NS)
                    dve.wait_ge(ymm_done, sums_before(i, m + 1) + first_of_pair(i, m))
                v.tensor_tensor(gs[:, k % RING_G, :], hs[:, k % RING_H, :], Cs[:, n, :], ALU.mult).then_inc(g_ready, 1)

            def take_y(b, i, q):
                dve.wait_ge(ymm_done, sums_before(i, NS))
                v.scalar_tensor_tensor(m_y[:], m_u[:, q % 2, :], c_d[:, q:q + 1], Y[q % 2][:], ALU.mult, ALU.add).then_inc(y_taken, 1)
                dve.wait_ge(y_taken, i + 1)
                dve.wait_ge(s_loaded[q % 2], b * 32 + (q // 2) * 16 + 16)
                v.tensor_tensor(m_y[:], m_y[:], m_sz[:, q % 2, :], ALU.mult).then_inc(gated_done, 1)

            def gated(b, i, q):
                par = q % 2
                dve.wait_ge(yT_ready, i + 1)
                dve.wait_ge(x_loaded[par], b * 32 + (q // 2) * 16 + 16)
                v.tensor_tensor(m_x[:, par], m_x[:, par], TP[:].rearrange("p (t j) -> p t j", t=TB), ALU.add).then_inc(x1_ready, 1)

            def stats(j, jb):
                at = j[1]
                dve.wait_ge(xt_loaded[at], jb * 16 + 16)
                v.bn_stats(f_st[:, at, :], xt[:, at, :]).then_inc(tstat_done, 1)
                dve.wait_ge(tstat_done, j[0] * 2 + 1)
                held(dve)
                v.bn_aggr(f_mv[:, at, :], f_st[:, at, :]).then_inc(tstat_done, 1)
                dve.wait_ge(tstat_done, j[0] * 2 + 2)
                v.tensor_scalar(f_ve[:, at:at + 1], f_mv[:, at, 1:2], EPS, None, ALU.add).then_inc(var_ready, 1)

            def norm(j):
                at = j[1]
                dve.wait_ge(rstd_ready, j[0] + 1)
                v.scalar_tensor_tensor(f_nm[:, at:at + 1], f_mv[:, at, 0:1], -1.0, f_rs[:, at:at + 1], ALU.mult, ALU.mult).then_inc(norm_ready, 1)

            def lg_copy(f):
                dve.wait_ge(lg_ready, f[0] + 1)
                v.tensor_copy(logits[:, bass.ds(f[0], 1), :].rearrange("p a e -> p (a e)"), TP[:, 0:NE]).then_inc(lg_copied, 1)

            def hidden(f, c):
                dve.wait_ge(sg_ready, 2 * f[0] + c + 1)
                dve.wait_ge(up_ready, 2 * f[0] + c + 1)
                dve.wait_ge(hT_ready, 1 + 2 * f[0])
                v.tensor_tensor(f_h[:, c, :], f_sg[:, c, :], GU[f[1] % 2][c][:, 0:I], ALU.mult).then_inc(h_ready, 1)

            def add_shared(f):
                dve.wait_ge(down_ready, 1 + f[0] + 1)
                row = xt[:, (f[1] + 2) % 4, :]
                v.tensor_tensor(row, row, YO[:], ALU.add).then_inc(down_added, 1)

            def slot(b, q, rows):
                i = b * DT + q
                later = not (isinstance(b, int) and b == 0 and q == 0)
                j = ((b - 1) * DT + q, q)
                for n in range(NS):
                    scan(b, q, n)
                    if n:
                        times_c(b, q, n - 1)
                    if n == TAKE_AT and later:
                        take_y(*((b, i - 1, q - 1) if q else (b - 1, i - 1, DT - 1)))
                    if n == GATED_AT and later:
                        gated(*((b, i - 1, q - 1) if q else (b - 1, i - 1, DT - 1)))
                    for c in range(2):
                        if n == HIDDEN_AT[c]:
                            if rows:
                                hidden((j[0] + 1, (q + 1) % TB), c)
                            elif q == DT - 1:
                                hidden((0, 0), c)
                    if rows:
                        if n == LOGITS_AT:
                            lg_copy(j)
                        if n == ADD_AT:
                            add_shared(j)
                        if n == STATS_AT[q > 0]:
                            stats(j, b - 1)
                        if n == NORM_AT[q > 0]:
                            norm(j)
                times_c(b, q, NS - 1)

            for q in range(DT):
                slot(0, q, False)
            with dve.Fori(1, B) as b:
                for q in range(DT):
                    slot(b, q, True)
            take_y(B - 1, B * DT - 1, DT - 1)
            gated(B - 1, B * DT - 1, DT - 1)

            def whole(f):
                for c in range(2):
                    hidden(f, c)
                add_shared(f)

            first = NT - TB
            add_shared((first, 0))
            for q in range(TB - 1):
                stats((first + q, q), B - 1)
                norm((first + q, q))
            whole((first + 1, 1))
            for q in range(TB - 1):
                lg_copy((first + q, q))
            stats((NT - 1, TB - 1), B - 1)
            norm((NT - 1, TB - 1))
            whole((first + 2, 2))
            lg_copy((NT - 1, TB - 1))
            lg_copy((NT, 0))

            done = [0]

            def link(ins):
                done[0] += 1
                ins.then_inc(route_step, 1)
                dve.wait_ge(route_step, done[0])

            dve.wait_ge(lg_copied, 1 + NT + 1)
            lg = logits[:, 1:NT + 1, :]
            by_tile = [P, NT, NE]
            link(v.reduce_max(r_mx[:], lg, AX.X))
            v.tensor_tensor(r_e[:], lg, r_mx[:].unsqueeze(2).to_broadcast(by_tile), ALU.subtract).then_inc(rt_max, 1)
            dve.wait_ge(rt_exp, 1)
            link(v.reduce_sum(r_sum[:], r_e[:], AX.X))
            link(v.reciprocal(r_inv[:], r_sum[:]))
            link(v.tensor_tensor(r_s[:], r_e[:], r_inv[:].unsqueeze(2).to_broadcast(by_tile), ALU.mult))
            for t in range(NT):
                last = v.max(r_top[:, t, :], r_s[:, t, :])
            link(last)
            for t in range(NT):
                last = v.max_index(r_ix[:, t, :], r_top[:, t, :], r_s[:, t, :])
            link(last)
            link(v.tensor_copy(r_ixf[:], r_ix[:, :, 0:K]))
            for c in range(K):
                v.tensor_copy(r_w[:, c, :], r_top[:, :, c])
                last = v.tensor_tensor(r_m[:, c], iota_row[:, 0:NE].unsqueeze(1).to_broadcast(by_tile),
                                       r_ixf[:, :, c:c + 1].to_broadcast(by_tile), ALU.is_equal)
            link(last)
            v.tensor_tensor(r_ms[:], r_m[:, 0], r_m[:, 1], ALU.add).then_inc(rt_mask, 1)
            whole((first + 3, 3))
            dve.wait_ge(rt_rank, 2)
            v.memset(r_res[:], 1.0)
            link(v.tensor_copy(r_tot[:], TOT[:, 0:NT * NE].rearrange("p (t e) -> p e t", e=NE)))
            link(v.memset(r_res[:, :, 0:1], 0.0))
            flat_ = lambda a: a[:, :, :].rearrange("p e t -> p (e t)")
            link(v.tensor_tensor_scan(flat_(r_inc), flat_(r_res), flat_(r_tot), 0.0, ALU.mult, ALU.add))
            link(v.tensor_scalar(r_nt[:], iota_row[:, 0:NT], float(P), None, ALU.mult))
            link(v.tensor_tensor(r_cmp[:], r_inc[:, :, NT - 1:NT].to_broadcast([P, NE, NT]),
                                 r_nt[:].unsqueeze(1).to_broadcast([P, NE, NT]), ALU.is_gt))
            link(v.reduce_sum(r_nt[:], r_cmp[:], AX.X))
            link(v.tensor_scalar(r_nt[:], r_nt[:], 1.0, None, ALU.max))
            link(v.tensor_tensor_scan(r_end[:], ones[:, 0:NE], r_nt[:], 0.0, ALU.mult, ALU.add))
            v.tensor_tensor(r_te, iota_row[:, 0:UNITS].unsqueeze(2).to_broadcast([P, UNITS, NE]),
                            r_end[:].unsqueeze(1).to_broadcast([P, UNITS, NE]), ALU.is_ge)
            link(v.tensor_tensor(r_base[:], r_end[:], r_nt[:], ALU.subtract))
            link(v.tensor_scalar(r_base[:], r_base[:], float(P), None, ALU.mult))
            v.reduce_sum(t_exp[:, 0:UNITS], r_te, AX.X)
            link(v.tensor_tensor(r_inc[:], r_inc[:], r_tot[:], ALU.subtract))
            link(v.tensor_tensor(r_inc[:], r_inc[:], r_base[:].unsqueeze(2).to_broadcast([P, NE, NT]), ALU.add))
            v.tensor_copy(t_end[:], r_end[:])
            link(v.tensor_scalar(t_expi[:, 0:UNITS], t_exp[:, 0:UNITS], float(NE - 1), None, ALU.min))
            link(v.tensor_tensor(r_pos[:], RANK[:, 0:NT * NE].rearrange("p (t e) -> p t e", e=NE),
                                 r_inc[:, :, :].rearrange("p e t -> p t e"), ALU.add))
            for c in range(K):
                last = v.tensor_tensor(r_mp[:, c], r_m[:, c], r_pos[:], ALU.mult)
            link(last)
            link(v.reduce_sum(r_p[:], r_mp[:], AX.X))
            hidden((NT, 0), 0)
            link(v.tensor_copy(r_pi[:], r_p[:]))
            v.tensor_single_scalar(r_qi[:], r_pi[:], 7, ALU.logical_shift_right)
            link(v.tensor_single_scalar(r_ri[:], r_pi[:], P - 1, ALU.bitwise_and))
            v.tensor_copy(r_q[:], r_qi[:])
            link(v.tensor_copy(r_r[:], r_ri[:]))
            link(v.tensor_scalar(r_tok[:, 0, :], iota_row[:, 0:NT], float(P), float(SPARE), ALU.mult, ALU.add))
            link(v.tensor_scalar(r_tok[:, 1, :], r_tok[:, 0, :], part[:], None, ALU.add))
            link(v.tensor_copy(r_tok[:, 0, :], r_tok[:, 1, :]))
            link(v.tensor_tensor(r_tok[:], r_tok[:], r_r[:], ALU.subtract))
            hidden((NT, 0), 1)
            cs = K * NT
            col = lambda a: a[:, :, :].rearrange("p c t -> p (c t)").unsqueeze(2)
            link(v.tensor_tensor(r_ohq, iota_row[:, 0:UNITS].unsqueeze(1).to_broadcast([P, cs, UNITS]),
                                 col(r_q).to_broadcast([P, cs, UNITS]), ALU.is_equal))
            v.tensor_tensor(r_rhs[:, :, 0, :], r_ohq, col(r_tok).to_broadcast([P, cs, UNITS]), ALU.mult)
            link(v.tensor_tensor(r_rhs[:, :, 1, :], r_ohq, col(r_w).to_broadcast([P, cs, UNITS]), ALU.mult))
            for c in range(0, cs, 8):
                v.tensor_tensor(r_ohr[:, c:c + 8, :], iota_row[:].unsqueeze(1).to_broadcast([P, 8, P]),
                                col(r_r)[:, c:c + 8, :].to_broadcast([P, 8, P]), ALU.is_equal).then_inc(rt_oh, 1)
            add_shared((NT, 0))
            dve.wait_ge(rt_table, 1)
            link(v.memset(t_tok[:, UNITS:UNITS + 2], 0))
            v.tensor_copy(t_w[:, 0:UNITS], TABLE[:, UNITS:2 * UNITS])
            link(v.tensor_scalar(t_tok[:, 0:UNITS], TABLE[:, 0:UNITS], part[:], None, ALU.add))
            v.tensor_copy(t_w[:, UNITS:UNITS + 1], part[:]).then_inc(tables_ready, 1)

            def split(e, ring, end):
                for raw, hi, lo, loaded, used, done, pieces in (
                        (e_gu, e_gu_hi, e_gu_lo, (gu_loaded, 16), eu_ready, gu_split, ((P, slice(0, KH)),)),
                        (e_dn, e_dn_hi, e_dn_lo, (dn_loaded, 32), ey_ready, dn_split, ((P, slice(0, 2)), (IT[2][1], slice(2, 3))))):
                    dve.wait_ge(loaded[0], (e + 1) * loaded[1])
                    if end is not None:
                        dve.wait_ge(used, 1 + end)
                    for n, ts in pieces:
                        last = v.tensor_copy(hi[0:n, ring, ts, :], raw[0:n, ts, :])
                    last.then_inc(split_step, 1)
                    dve.wait_ge(split_step, 2 * e + (1 if raw is e_gu else 2))
                    for n, ts in pieces:
                        last = v.tensor_tensor(lo[0:n, ring, ts, :], raw[0:n, ts, :], hi[0:n, ring, ts, :].bitcast(F32), ALU.subtract)
                    last.then_inc(done, 1)

            split(0, 0, None)
            whole((NT + 1, 1))

            split(1, 1, None)
            with dve.Fori(1, NE // 2) as r:
                for ring in range(2):
                    e = r * 2 + ring
                    end = dve.value_load(t_end[0:1, bass.ds(e - 2, 1)], min_val=0, max_val=UNITS)
                    split(e, ring, end)


_INS = ["x", "ctxT", "inT", "convw", "convb", "xpT", "dtT", "dtb", "alog", "dskip", "gateT", "wgu", "wdn", "sgu", "sdn"]


def kernel(x, ctx_1024, L0_xattn_in_proj_w, L0_xattn_conv_w, L0_xattn_conv_b, L0_xattn_x_proj_w, L0_xattn_dt_proj_w,
           L0_xattn_dt_proj_b, L0_xattn_A_log, L0_xattn_D, L0_ffn_gate_w, L0_ffn_w_gate_up, L0_ffn_w_down,
           L0_ffn_shared_gate_up, L0_ffn_shared_down):
    import numpy as np
    import concourse.bacc as bacc
    from concourse.bass_utils import run_bass_kernel_spmd as run

    def by_channel(a):
        a = np.asarray(a)
        return a.reshape(DT, P, -1).transpose(1, 0, 2)

    data = {
        "x": np.asarray(x).reshape(T, H), "ctxT": np.asarray(ctx_1024).transpose(0, 2, 1),
        "inT": np.asarray(L0_xattn_in_proj_w).T, "convw": by_channel(L0_xattn_conv_w),
        "convb": by_channel(L0_xattn_conv_b)[:, :, 0], "xpT": np.asarray(L0_xattn_x_proj_w).T,
        "dtT": np.asarray(L0_xattn_dt_proj_w).T, "dtb": by_channel(L0_xattn_dt_proj_b)[:, :, 0],
        "alog": by_channel(L0_xattn_A_log), "dskip": by_channel(L0_xattn_D)[:, :, 0],
        "gateT": np.asarray(L0_ffn_gate_w).T, "wgu": np.asarray(L0_ffn_w_gate_up), "wdn": np.asarray(L0_ffn_w_down),
        "sgu": np.asarray(L0_ffn_shared_gate_up), "sdn": np.asarray(L0_ffn_shared_down),
    }
    nc = bacc.Bacc("TRN2", target_bir_lowering=False, num_devices=1)
    arrays, args = {}, []
    for name in _INS:
        arrays[f"in_{name}"] = np.ascontiguousarray(data[name])
        args.append(nc.dram_tensor(f"in_{name}", list(data[name].shape), F32, kind="ExternalInput").ap())
    out = nc.dram_tensor("out_rows", [T + SPARE, H], F32, kind="ExternalOutput").ap()
    program(nc, *args, out)
    r = run(nc, [arrays], core_ids=[0])
    return r.results[0]["out_rows"][SPARE:].reshape(B, L, H)
```
